# Optimizing a Trainium2 kernel written in Bass

```python
import numpy as np
import jax
import jax.numpy as jnp

def _softmax(x, axis=-1):
    return jax.nn.softmax(x, axis=axis)

def _gelu(x):
    return jax.nn.gelu(x, approximate=True)

def _silu(x):
    return jax.nn.silu(x)

def _sigmoid(x):
    return jax.nn.sigmoid(x)

def _layernorm(x, axis=-1, eps=1e-05):
    m = jnp.mean(x, axis=axis, keepdims=True)
    v = jnp.var(x, axis=axis, keepdims=True)
    return (x - m) / jnp.sqrt(v + eps)

def _scatter_add(tgt, idx, src, axis=0):
    return tgt.at[idx].add(src)

def _segment_sum(src, seg, n):
    return jax.ops.segment_sum(src, seg, n)
kernel_name = 'mk_flamingo_gated_d2_seqx_r8_f80d03'

def setup_inputs(seed: int=0):
    np.random.seed(seed)
    _w = jnp.asarray

    def _rec_inputs():
        import jax
        import jax.numpy as jnp
        _rk = jax.random.key(seed)
        x = -0.0003929 + 0.9999 * jax.random.normal(jax.random.fold_in(_rk, 1), (4, 256, 128), jnp.float32)
        _lenS = 256 - jax.random.randint(jax.random.fold_in(_rk, 7), (4,), 0, max(1, 256 // 4) + 1, jnp.int32)
        _lenS2 = 256 - jax.random.randint(jax.random.fold_in(_rk, 8), (4,), 0, max(1, 256 // 4) + 1, jnp.int32)
        _ctx_1024P = jax.random.normal(jax.random.fold_in(_rk, 11), (4, 16, 128), jnp.float32)
        _ctx_1024c = jax.random.dirichlet(jax.random.fold_in(_rk, 511), 0.3 * jnp.ones((16,), jnp.float32), (4, 256))
        _ctx_1024t = jnp.einsum('bsk,bkd->bsd', _ctx_1024c, _ctx_1024P)
        _ctx_1024t = _ctx_1024t * jax.lax.rsqrt(jnp.mean(jnp.square(_ctx_1024t)) + 1e-12) * 0.953939
        ctx_1024 = 2.81802e-05 + 1.00001 * (_ctx_1024t + 0.3 * jax.random.normal(jax.random.fold_in(_rk, 611), (4, 256, 128), jnp.float32))
        itok_BxS_0_4095 = jax.random.randint(jax.random.fold_in(_rk, 12), (4, 256), 0, 512, jnp.int32)
        itok_BxS2_1_4095 = jax.random.randint(jax.random.fold_in(_rk, 13), (4, 256), 1, 512, jnp.int32)
        _g = jax.random.normal(jax.random.fold_in(_rk, 9001), (2, 2), jnp.float32)
        _g = jnp.sign(_g) * jnp.maximum(jnp.abs(_g), 1.0) + (_g == 0) * 1.0
        g_xattn = _g[0]
        g_ffn = _g[1]
        return (x, ctx_1024, itok_BxS_0_4095, itok_BxS2_1_4095, g_xattn, g_ffn)
    x, ctx_1024, itok_BxS_0_4095, itok_BxS2_1_4095, g_xattn, g_ffn = _rec_inputs()

    def _L0_xattn_setup():
        import math
        import jax, jax.numpy as jnp
        import numpy as np
        D_MODEL = 128
        N_HEADS = 16
        D_K = D_MODEL // N_HEADS

        def _autocorr_forward(queries, keys, values, Wq, bq, Wk, bk, Wv, bv, Wo, bo):
            B, L, D = queries.shape
            H, dk = (N_HEADS, D_K)
            q = (queries @ Wq.T + bq).reshape(B, L, H, dk)
            k = (keys @ Wk.T + bk).reshape(B, L, H, dk)
            v = (values @ Wv.T + bv).reshape(B, L, H, dk)
            qf = jnp.fft.rfft(q, axis=1)
            kf = jnp.fft.rfft(k, axis=1)
            corr = jnp.fft.irfft(qf * jnp.conj(kf), n=L, axis=1).mean(axis=-1)
            corr = corr.transpose(0, 2, 1)
            topk = min(max(1, int(math.log(L))), L)
            weights, delays = jax.lax.top_k(corr, topk)
            w = jax.nn.softmax(weights, axis=-1)
            idx = (jnp.arange(L)[None, None, None, :] - delays[..., None]) % L
            v_h = v.transpose(0, 2, 1, 3)
            gathered = jnp.take_along_axis(v_h[:, :, None], idx[..., None], axis=3)
            out = (w[..., None, None] * gathered).sum(axis=2)
            out = out.transpose(0, 2, 1, 3).reshape(B, L, D)
            return out @ Wo.T + bo
        key = jax.random.key(seed)
        ks = jax.random.split(key, 12)
        B, L, D = (8, 256, D_MODEL)
        scale = 1.0 / math.sqrt(D)
        inp = {'queries': jax.random.normal(ks[0], (B, L, D), jnp.float32), 'keys': jax.random.normal(ks[1], (B, L, D), jnp.float32), 'values': jax.random.normal(ks[2], (B, L, D), jnp.float32), 'Wq': jax.random.normal(ks[3], (D, D), jnp.float32) * scale, 'bq': jnp.zeros((D,), jnp.float32), 'Wk': jax.random.normal(ks[4], (D, D), jnp.float32) * scale, 'bk': jnp.zeros((D,), jnp.float32), 'Wv': jax.random.normal(ks[5], (D, D), jnp.float32) * scale, 'bv': jnp.zeros((D,), jnp.float32), 'Wo': jax.random.normal(ks[6], (D, D), jnp.float32) * scale, 'bo': jnp.zeros((D,), jnp.float32)}
        return inp
    _L0_xattn_all = _L0_xattn_setup()
    _L0_xattn_in = {k: v for k, v in _L0_xattn_all.items() if k in ('Wq', 'bq', 'Wk', 'bk', 'Wv', 'bv', 'Wo', 'bo')}
    del _L0_xattn_all

    def _L0_ffn_setup():
        import jax, jax.numpy as jnp
        import numpy as np
        H = 8
        KD = 128
        TOPK = 8
        NUM_KEYS = 32
        N_EXPERTS = NUM_KEYS * NUM_KEYS
        N_DIM = 128
        BN_EPS = 1e-05

        def gelu_new(x):
            c = jnp.sqrt(jnp.asarray(2.0 / jnp.pi, x.dtype))
            return 0.5 * x * (1.0 + jnp.tanh(c * (x + 0.044715 * x * x * x)))
        key = jax.random.key(seed)
        ks = jax.random.split(key, 5)
        b, s = (2, 128)
        x = jax.random.normal(ks[0], (b, s, N_DIM), dtype=jnp.float32)
        w_q = jax.random.normal(ks[1], (N_DIM, 2 * H * KD), dtype=jnp.float32) * 0.02
        bn_gamma = jnp.ones((2 * H * KD,), dtype=jnp.float32)
        bn_beta = jnp.zeros((2 * H * KD,), dtype=jnp.float32)
        keys = jax.random.normal(ks[2], (H, NUM_KEYS, 2, KD), dtype=jnp.float32) * 0.02
        down_embed = jax.random.normal(ks[3], (N_EXPERTS, N_DIM), dtype=jnp.float32) * 0.02
        up_embed = jax.random.normal(ks[4], (N_EXPERTS, N_DIM), dtype=jnp.float32) * 0.02
        return {'x': x, 'w_q': w_q, 'bn_gamma': bn_gamma, 'bn_beta': bn_beta, 'keys': keys, 'down_embed': down_embed, 'up_embed': up_embed}
    _L0_ffn_all = _L0_ffn_setup()
    _L0_ffn_in = {k: v for k, v in _L0_ffn_all.items() if k in ('w_q', 'bn_gamma', 'bn_beta', 'keys', 'down_embed', 'up_embed')}
    del _L0_ffn_all

    def _L1_xattn_setup():
        import jax, jax.numpy as jnp
        import numpy as np
        N_EMBED = 128
        N_HEAD = 16
        HEAD_DIM = N_EMBED // N_HEAD
        ROPE_BASE = 10000.0

        def rotate_half(x):
            x1, x2 = jnp.split(x, 2, axis=-1)
            return jnp.concatenate((-x2, x1), axis=-1)

        def rope_cos_sin(position_ids):
            inv_freq = 1.0 / ROPE_BASE ** (jnp.arange(0, HEAD_DIM, 2, dtype=jnp.float32) / HEAD_DIM)
            freqs = position_ids.astype(jnp.float32)[:, :, None] * inv_freq[None, None, :]
            emb = jnp.concatenate((freqs, freqs), axis=-1)
            return (jnp.cos(emb), jnp.sin(emb))

        def apply_rope(x, cos, sin):
            cos = cos[:, None, :, :]
            sin = sin[:, None, :, :]
            return x * cos + rotate_half(x) * sin
        key = jax.random.key(seed)
        ks = jax.random.split(key, 10)
        B, Tx, Ty = (4, 128, 256)
        x = jax.random.normal(ks[0], (B, Tx, N_EMBED), dtype=jnp.float32)
        y = jax.random.normal(ks[1], (B, Ty, N_EMBED), dtype=jnp.float32)
        x_pos = jnp.sort(jax.random.randint(ks[2], (B, Tx), 0, 512), axis=-1)
        y_pos = jnp.sort(jax.random.randint(ks[3], (B, Ty), 0, 512), axis=-1)
        s = 1.0 / np.sqrt(N_EMBED)
        W_q = jax.random.normal(ks[4], (N_EMBED, N_EMBED), dtype=jnp.float32) * s
        b_q = jnp.zeros((N_EMBED,), dtype=jnp.float32)
        W_kv = jax.random.normal(ks[5], (N_EMBED, 2 * N_EMBED), dtype=jnp.float32) * s
        b_kv = jnp.zeros((2 * N_EMBED,), dtype=jnp.float32)
        W_o = jax.random.normal(ks[6], (N_EMBED, N_EMBED), dtype=jnp.float32) * s
        b_o = jnp.zeros((N_EMBED,), dtype=jnp.float32)
        return {'x': x, 'y': y, 'W_q': W_q, 'b_q': b_q, 'W_kv': W_kv, 'b_kv': b_kv, 'W_o': W_o, 'b_o': b_o, 'x_pos': x_pos, 'y_pos': y_pos}
    _L1_xattn_all = _L1_xattn_setup()
    _L1_xattn_in = {k: v for k, v in _L1_xattn_all.items() if k in ('W_q', 'b_q', 'W_kv', 'b_kv', 'W_o', 'b_o')}
    del _L1_xattn_all

    def _L1_ffn_setup():
        import jax, jax.numpy as jnp
        import numpy as np
        B, S, H, E, I, MAX_K, A_HID = (2, 256, 128, 8, 336, 6, 50)
        key = jax.random.key(seed)
        ks = jax.random.split(key, 10)
        sc = 0.02
        return {'hidden_states': jax.random.normal(ks[0], (B, S, H), dtype=jnp.float32), 'router_w': jax.random.normal(ks[1], (E, H), dtype=jnp.float32) * sc, 'actor_w1': jax.random.normal(ks[2], (A_HID, H), dtype=jnp.float32) * sc, 'actor_b1': jnp.zeros((A_HID,), dtype=jnp.float32), 'actor_w2': jax.random.normal(ks[3], (MAX_K, A_HID), dtype=jnp.float32) * sc, 'actor_b2': jnp.zeros((MAX_K,), dtype=jnp.float32), 'gate_w': jax.random.normal(ks[4], (E, I, H), dtype=jnp.float32) * sc, 'up_w': jax.random.normal(ks[5], (E, I, H), dtype=jnp.float32) * sc, 'down_w': jax.random.normal(ks[6], (E, H, I), dtype=jnp.float32) * sc}
    _L1_ffn_all = _L1_ffn_setup()
    _L1_ffn_in = {k: v for k, v in _L1_ffn_all.items() if k in ('router_w', 'actor_w1', 'actor_b1', 'actor_w2', 'actor_b2', 'gate_w', 'up_w', 'down_w')}
    del _L1_ffn_all
    return {'x': x, 'ctx_1024': ctx_1024, 'itok_BxS_0_4095': itok_BxS_0_4095, 'itok_BxS2_1_4095': itok_BxS2_1_4095, 'g_xattn': g_xattn, 'g_ffn': g_ffn, 'L0_xattn_Wq': _L0_xattn_in['Wq'], 'L0_xattn_bq': _L0_xattn_in['bq'], 'L0_xattn_Wk': _L0_xattn_in['Wk'], 'L0_xattn_bk': _L0_xattn_in['bk'], 'L0_xattn_Wv': _L0_xattn_in['Wv'], 'L0_xattn_bv': _L0_xattn_in['bv'], 'L0_xattn_Wo': _L0_xattn_in['Wo'], 'L0_xattn_bo': _L0_xattn_in['bo'], 'L0_ffn_w_q': _L0_ffn_in['w_q'], 'L0_ffn_bn_gamma': _L0_ffn_in['bn_gamma'], 'L0_ffn_bn_beta': _L0_ffn_in['bn_beta'], 'L0_ffn_keys': _L0_ffn_in['keys'], 'L0_ffn_down_embed': _L0_ffn_in['down_embed'], 'L0_ffn_up_embed': _L0_ffn_in['up_embed'], 'L1_xattn_W_q': _L1_xattn_in['W_q'], 'L1_xattn_b_q': _L1_xattn_in['b_q'], 'L1_xattn_W_kv': _L1_xattn_in['W_kv'], 'L1_xattn_b_kv': _L1_xattn_in['b_kv'], 'L1_xattn_W_o': _L1_xattn_in['W_o'], 'L1_xattn_b_o': _L1_xattn_in['b_o'], 'L1_ffn_router_w': _L1_ffn_in['router_w'], 'L1_ffn_actor_w1': _L1_ffn_in['actor_w1'], 'L1_ffn_actor_b1': _L1_ffn_in['actor_b1'], 'L1_ffn_actor_w2': _L1_ffn_in['actor_w2'], 'L1_ffn_actor_b2': _L1_ffn_in['actor_b2'], 'L1_ffn_gate_w': _L1_ffn_in['gate_w'], 'L1_ffn_up_w': _L1_ffn_in['up_w'], 'L1_ffn_down_w': _L1_ffn_in['down_w']}

def reference(x, ctx_1024, itok_BxS_0_4095, itok_BxS2_1_4095, g_xattn, g_ffn, L0_xattn_Wq, L0_xattn_bq, L0_xattn_Wk, L0_xattn_bk, L0_xattn_Wv, L0_xattn_bv, L0_xattn_Wo, L0_xattn_bo, L0_ffn_w_q, L0_ffn_bn_gamma, L0_ffn_bn_beta, L0_ffn_keys, L0_ffn_down_embed, L0_ffn_up_embed, L1_xattn_W_q, L1_xattn_b_q, L1_xattn_W_kv, L1_xattn_b_kv, L1_xattn_W_o, L1_xattn_b_o, L1_ffn_router_w, L1_ffn_actor_w1, L1_ffn_actor_b1, L1_ffn_actor_w2, L1_ffn_actor_b2, L1_ffn_gate_w, L1_ffn_up_w, L1_ffn_down_w):
    import jax
    import jax.numpy as jnp

    def _L0_xattn_ref(queries, keys, values, Wq, bq, Wk, bk, Wv, bv, Wo, bo):
        import math
        import jax, jax.numpy as jnp
        import numpy as np
        D_MODEL = 128
        N_HEADS = 16
        D_K = D_MODEL // N_HEADS

        def _autocorr_forward(queries, keys, values, Wq, bq, Wk, bk, Wv, bv, Wo, bo):
            B, L, D = queries.shape
            H, dk = (N_HEADS, D_K)
            q = (queries @ Wq.T + bq).reshape(B, L, H, dk)
            k = (keys @ Wk.T + bk).reshape(B, L, H, dk)
            v = (values @ Wv.T + bv).reshape(B, L, H, dk)
            qf = jnp.fft.rfft(q, axis=1)
            kf = jnp.fft.rfft(k, axis=1)
            corr = jnp.fft.irfft(qf * jnp.conj(kf), n=L, axis=1).mean(axis=-1)
            corr = corr.transpose(0, 2, 1)
            topk = min(max(1, int(math.log(L))), L)
            weights, delays = jax.lax.top_k(corr, topk)
            w = jax.nn.softmax(weights, axis=-1)
            idx = (jnp.arange(L)[None, None, None, :] - delays[..., None]) % L
            v_h = v.transpose(0, 2, 1, 3)
            gathered = jnp.take_along_axis(v_h[:, :, None], idx[..., None], axis=3)
            out = (w[..., None, None] * gathered).sum(axis=2)
            out = out.transpose(0, 2, 1, 3).reshape(B, L, D)
            return out @ Wo.T + bo
        return _autocorr_forward(queries, keys, values, Wq, bq, Wk, bk, Wv, bv, Wo, bo)

    def _L0_ffn_ref(x, w_q, bn_gamma, bn_beta, keys, down_embed, up_embed):
        import jax, jax.numpy as jnp
        import numpy as np
        H = 8
        KD = 128
        TOPK = 8
        NUM_KEYS = 32
        N_EXPERTS = NUM_KEYS * NUM_KEYS
        N_DIM = 128
        BN_EPS = 1e-05

        def gelu_new(x):
            c = jnp.sqrt(jnp.asarray(2.0 / jnp.pi, x.dtype))
            return 0.5 * x * (1.0 + jnp.tanh(c * (x + 0.044715 * x * x * x)))
        b, n, d = x.shape
        q = jnp.einsum('bnd,de->bne', x, w_q)
        mean = jnp.mean(q, axis=(0, 1))
        var = jnp.var(q, axis=(0, 1))
        q = (q - mean) * jax.lax.rsqrt(var + BN_EPS) * bn_gamma + bn_beta
        q = q.reshape(b, n, 2, H, KD).transpose(2, 0, 1, 3, 4)
        sim = jnp.einsum('pbnhd,hkpd->pbnhk', q, keys)
        sx, ix = jax.lax.top_k(sim[0], TOPK)
        sy, iy = jax.lax.top_k(sim[1], TOPK)
        all_scores = (sx[..., :, None] + sy[..., None, :]).reshape(b, n, H, TOPK * TOPK)
        all_indices = (ix[..., :, None] * NUM_KEYS + iy[..., None, :]).reshape(b, n, H, TOPK * TOPK)
        scores, pk = jax.lax.top_k(all_scores, TOPK)
        indices = jnp.take_along_axis(all_indices, pk, axis=-1)
        wd = down_embed[indices]
        wu = up_embed[indices]
        h = jnp.einsum('bnd,bnhkd->bnhk', x, wd)
        h = gelu_new(h)
        h = jax.nn.softmax(scores, axis=-1) * h
        out = jnp.einsum('bnhk,bnhkd->bnd', h, wu)
        return out

    def _L1_xattn_ref(x, y, W_q, b_q, W_kv, b_kv, W_o, b_o, x_pos, y_pos):
        import jax, jax.numpy as jnp
        import numpy as np
        N_EMBED = 128
        N_HEAD = 16
        HEAD_DIM = N_EMBED // N_HEAD
        ROPE_BASE = 10000.0

        def rotate_half(x):
            x1, x2 = jnp.split(x, 2, axis=-1)
            return jnp.concatenate((-x2, x1), axis=-1)

        def rope_cos_sin(position_ids):
            inv_freq = 1.0 / ROPE_BASE ** (jnp.arange(0, HEAD_DIM, 2, dtype=jnp.float32) / HEAD_DIM)
            freqs = position_ids.astype(jnp.float32)[:, :, None] * inv_freq[None, None, :]
            emb = jnp.concatenate((freqs, freqs), axis=-1)
            return (jnp.cos(emb), jnp.sin(emb))

        def apply_rope(x, cos, sin):
            cos = cos[:, None, :, :]
            sin = sin[:, None, :, :]
            return x * cos + rotate_half(x) * sin
        B, Tx, C = x.shape
        Ty = y.shape[1]
        q = x @ W_q + b_q
        kv = y @ W_kv + b_kv
        k, v = jnp.split(kv, 2, axis=-1)
        q = q.reshape(B, Tx, N_HEAD, HEAD_DIM).transpose(0, 2, 1, 3)
        k = k.reshape(B, Ty, N_HEAD, HEAD_DIM).transpose(0, 2, 1, 3)
        v = v.reshape(B, Ty, N_HEAD, HEAD_DIM).transpose(0, 2, 1, 3)
        cos_q, sin_q = rope_cos_sin(x_pos)
        cos_k, sin_k = rope_cos_sin(y_pos)
        q = apply_rope(q, cos_q, sin_q)
        k = apply_rope(k, cos_k, sin_k)
        scale = 1.0 / np.sqrt(HEAD_DIM)
        scores = jnp.einsum('bhqd,bhkd->bhqk', q, k) * scale
        attn = jax.nn.softmax(scores, axis=-1)
        out = jnp.einsum('bhqk,bhkd->bhqd', attn, v)
        out = out.transpose(0, 2, 1, 3).reshape(B, Tx, C)
        return out @ W_o + b_o

    def _L1_ffn_ref(hidden_states, router_w, actor_w1, actor_b1, actor_w2, actor_b2, gate_w, up_w, down_w):
        import jax, jax.numpy as jnp
        import numpy as np
        B, S, H, E, I, MAX_K, A_HID = (2, 256, 128, 8, 336, 6, 50)
        probs = jax.nn.softmax(jnp.einsum('bsh,eh->bse', hidden_states, router_w).astype(jnp.float32), axis=-1)
        a_h = jax.nn.gelu(jnp.einsum('bsh,ah->bsa', hidden_states, actor_w1) + actor_b1)
        actor_logits = jnp.clip(jnp.einsum('bsa,ka->bsk', a_h, actor_w2) + actor_b2, -30.0, 30.0)
        sampled_k = jnp.argmax(actor_logits, axis=-1) + 1
        order = jnp.argsort(-probs, axis=-1)
        rank = jnp.argsort(order, axis=-1)
        mask = rank < sampled_k[..., None]
        scores = jnp.where(mask, probs, 0.0).astype(hidden_states.dtype)
        out = jnp.zeros_like(hidden_states)
        for e in range(E):
            g = jnp.einsum('bsh,ih->bsi', hidden_states, gate_w[e])
            u = jnp.einsum('bsh,ih->bsi', hidden_states, up_w[e])
            y = jnp.einsum('bsi,hi->bsh', jax.nn.silu(g) * u, down_w[e])
            out = out + scores[..., e:e + 1] * y
        return out
    x = x + jnp.tanh(g_xattn[0]) * _L0_xattn_ref(_layernorm(x, axis=-1), ctx_1024, ctx_1024, L0_xattn_Wq, L0_xattn_bq, L0_xattn_Wk, L0_xattn_bk, L0_xattn_Wv, L0_xattn_bv, L0_xattn_Wo, L0_xattn_bo)
    x = x + jnp.tanh(g_ffn[0]) * _L0_ffn_ref(_layernorm(x, axis=-1), L0_ffn_w_q, L0_ffn_bn_gamma, L0_ffn_bn_beta, L0_ffn_keys, L0_ffn_down_embed, L0_ffn_up_embed)
    x = x + jnp.tanh(g_xattn[1]) * _L1_xattn_ref(_layernorm(x, axis=-1), ctx_1024, L1_xattn_W_q, L1_xattn_b_q, L1_xattn_W_kv, L1_xattn_b_kv, L1_xattn_W_o, L1_xattn_b_o, itok_BxS_0_4095, itok_BxS2_1_4095)
    x = x + jnp.tanh(g_ffn[1]) * _L1_ffn_ref(_layernorm(x, axis=-1), L1_ffn_router_w, L1_ffn_actor_w1, L1_ffn_actor_b1, L1_ffn_actor_w2, L1_ffn_actor_b2, L1_ffn_gate_w, L1_ffn_up_w, L1_ffn_down_w)
    return x

_drawn_inputs = setup_inputs


def setup_inputs(seed=0):
    import zlib

    import numpy as np

    out = dict(_drawn_inputs(seed))
    spreads = {'g_ffn': (-1.0, 0.6),
     'L0_xattn_bq': (0.0, 0.8),
     'L0_xattn_bk': (0.0, 0.8),
     'L0_xattn_bv': (0.0, 0.1),
     'L0_xattn_bo': (0.0, 0.1),
     'L0_ffn_bn_gamma': (1.0, 0.6),
     'L0_ffn_bn_beta': (0.0, 0.8),
     'L1_xattn_b_q': (0.0, 0.702),
     'L1_xattn_b_kv': (0.0, 0.1),
     'L1_xattn_b_o': (0.0, 0.1),
     'L1_ffn_actor_b1': (0.0, 0.1),
     'L1_ffn_actor_b2': (0.0, 0.8)}
    factors = {'L0_ffn_w_q': 8.0,
     'L0_ffn_keys': 8.0,
     'L0_ffn_down_embed': 8.0,
     'L0_ffn_up_embed': 8.0,
     'L1_ffn_router_w': 8.0,
     'L1_ffn_gate_w': 8.0,
     'L1_ffn_up_w': 8.0,
     'L1_ffn_down_w': 8.0}
    for name, (base, spread) in spreads.items():
        noise = np.random.default_rng([zlib.crc32(name.encode()), seed]).standard_normal(out[name].shape)
        drawn = base * np.exp(spread * noise) if base else spread * noise
        out[name] = jnp.asarray(drawn.astype(out[name].dtype))
    for name, factor in factors.items():
        out[name] = (out[name] * factor).astype(out[name].dtype)
    return out
```

```python
from contextlib import ExitStack

import numpy as np

import concourse.bass as bass
from concourse import mybir

F32 = mybir.dt.float32
BF16 = mybir.dt.bfloat16
F16 = mybir.dt.float16
I32 = mybir.dt.int32
U32 = mybir.dt.uint32
ALU = mybir.AluOpType
ACT = mybir.ActivationFunctionType
AX = mybir.AxisListType.X

P = 128
B, L, D = 4, 256, 128
NT = B * L // P
H, DK = 16, 8
TOP = 5
PH, NK = 8, 32
KT8 = 8
NE = NK * NK
EH = NE // P
CAND = 20
E8, I, IT, IP = 8, 336, 3, 112
AH, MK = 50, 6
EPS = 1e-5
WSCALE = 1024.0
SL = 8
TWO_PI = 6.283185307179586
C1 = 6.28125
C2 = float(np.float32(TWO_PI - C1))
C3 = float(TWO_PI - C1 - float(np.float32(TWO_PI - C1)))
ROUND = 12582912.0
VC, VSN, VS, VCN = range(4)


def program(nc, a, out):
    with ExitStack() as ctx:
        def sb(name, shape, dt=F32):
            return ctx.enter_context(nc.sbuf_tensor(name, shape, dt))

        sems = {}

        def sem(name):
            if name not in sems:
                sems[name] = ctx.enter_context(nc.semaphore(name))
            return sems[name]

        ps = ctx.enter_context(nc.psum_tensor("ps", [P, 8, 512], F32))

        def bank16(n, k=1):
            return ps[:, n:n + k, :].rearrange("p a c -> p (a c)").bitcast(BF16)

        Gb, Xb, HDb = sb("Gb", [P, EH * NT * P]), sb("Xb", [P, P * P // 2]), sb("HDb", [P, EH * 2 * P])
        KTb, xnb, ctxTb = sb("KTb", [P, H // 4 * NT * P]), sb("xnb", [P, NT * D]), sb("ctxTb", [P, NT * P])
        taken = {}

        def over(base, shape):
            n, at = int(np.prod(shape[1:])), taken.get(id(base), 0)
            taken[id(base)] = at + n
            w = base[:, at:at + n]
            if len(shape) == 3:
                return w.rearrange("p (a c) -> p a c", a=shape[1])
            if len(shape) == 4:
                return w.rearrange("p (a c d) -> p a c d", a=shape[1], c=shape[2])
            return w

        ld = {}
        for name, ap in a.items():
            shape = list(ap.shape)
            if name == "gates":
                shape = [P, 4]
            if name == "rows":
                shape = [33, shape[1]]
            if name == "dn":
                dnb = sb("dnb", [P, E8 * IT * D])
                ld[name] = dnb[0:IP, :].rearrange("p (a c) -> p a c", a=E8 * IT)
            elif name in ("w_q", "w_qT"):
                ld[name] = over(KTb, shape)
            elif name in ("dft", "idft", "keysT", "ctx", "wkv0T", "wq0T", "wo0T"):
                ld[name] = over(Gb, shape)
            else:
                ld[name] = sb("sb_" + name, shape, ap.dtype)
        ident, ones, cur = ld["ident"], ld["ones"], ld["x"]
        identb = sb("identb", [P, P], BF16)
        tg = sb("tg", [P, 4])

        cf = over(Xb, [P, B, 4 * P])
        ctxT = ctxTb
        kv = over(Xb, [P, 5, B * P])
        KC, KS, KCN, VVC, VVS = range(5)
        qf = over(Xb, [P, 2, B * P])
        tmp = over(Gb, [P, 2048])
        spec = over(Xb, [P, 2, B * P])
        cps = over(Gb, [P, 2, B * H])
        corr = over(Gb, [P, L])
        ew = over(Gb, [P, L])
        sm = sb("sm", [P, 64])
        wcT = over(Gb, [P, 2, B * H])
        wf = over(Gb, [P, 3, B * H])
        aoT = over(Xb, [P, NT * P])

        xn = xnb[:, :].rearrange("p (t d) -> p t d", t=NT)
        xnT = over(dnb, [P, NT * P])
        st = sb("st", [P, NT, 6])
        mv = sb("mv", [P, NT, 2])
        rs = sb("rs", [P, 4, NT])

        xc = over(HDb, [P, NT, D])
        xcT = over(HDb, [P, NT * P])
        cov = over(Gb, [P, D])
        var = sb("var", [P, 4, 16])
        keyS = over(Gb, [P, 16, NK])
        M = over(dnb, [P, 512])
        crow = ld["rows"][32:33, 0:512]
        sim = sb("sim", [P, NT, 512])
        top = sb("top", [P, 2, 16, 8])
        tix = sb("tix", [P, 2, 16, 8], U32)
        tixf = sb("tixf", [P, 2, 16, 8])
        cand = sb("cand", [P, 2, PH, CAND])
        candi = sb("candi", [P, 2, PH, CAND])
        sc = sb("sc", [P, 2, PH, 8])
        pk = sb("pk", [P, 2, PH, 8], U32)
        pkf = sb("pkf", [P, PH * 8])
        hot = sb("hot", [P, PH * 8, CAND])
        dd = sb("dd", [P, 2, PH, 8])
        zz = sb("zz", [P, 2, PH])
        ex_ = sb("ex_", [P, 2, PH, 8])
        wts = sb("wts", [P, 2, 2, 64])
        eid = sb("eid", [P, 2, 2, 64])
        eidi = sb("eidi", [P, 3, P], I32)
        elh = sb("elh", [P, 2, P])
        elT = sb("elT", [P, 2, P], F16)
        whl = sb("whl", [P, 2, P], F16)
        iox = sb("iox", [P, 16, P], F16)
        elS = sb("elS", [P, EH, P], F16)
        X = Xb[:, :].bitcast(F16).rearrange("p (e t) -> p e t", e=P)
        Yq = sb("Yq", [P, EH, P], F16)
        Y = sb("Y", [P, 2, EH, P], F16)
        G = Gb[:, :].rearrange("p (e t) -> p e t", e=EH)
        HD = HDb[:, :].rearrange("p (e t) -> p e t", e=EH)

        cs = sb("cs", [P, 2, 2 * NT, 4])
        ang = sb("ang", [P, 3, 2 * NT * 4])
        posf = sb("posf", [P, 2 * NT])
        qs = Xb[:, 3072:4096].bitcast(BF16).rearrange("p (h s d) -> p h s d", s=SL, d=DK)
        KT = KTb[:, :].bitcast(BF16).rearrange("p (j t) -> p j t", j=H // 2)
        QT = Xb[:, 4096:5120].bitcast(BF16).rearrange("p (j t) -> p j t", j=H // 2)
        V = sb("V", [P, NT, H, DK + 1])
        ra = Xb[:, 5120:5376].rearrange("p (t d) -> p t d", t=2)
        rb = Xb[:, 5376:5632].rearrange("p (t d) -> p t d", t=2)
        rq = Xb[:, 5632:5888].rearrange("p (t d) -> p t d", t=2)
        mx = sb("mx", [P, 2, H])
        mrep = sb("mrep", [P, 2, P], BF16)
        mT = sb("mT", [P, 2 * P], BF16)
        PE_ = Xb[:, 0:1024].rearrange("p (a k c) -> p a k c", a=2, k=2)
        rcp = sb("rcp", [P, 2 * H])
        att = xnb[:, 256:512].rearrange("p (t d) -> p t d", t=2)
        attT = ctxTb[:, 0:256]
        xn2 = xnb[:, 0:256].rearrange("p (t d) -> p t d", t=2)
        xn2T = ctxTb[:, 256:512]

        xn3 = xnb[:, 512:768].rearrange("p (t d) -> p t d", t=2)
        xn3T = ctxTb[:, 512:768]
        ah = sb("ah", [64, 2 * P])
        rt = sb("rt", [P, 8, 16])
        cmp = sb("cmp", [P, 2, 2, 8, 8])
        sg = Xb[0:IP, 1024:1536].rearrange("p (a c) -> p a c", a=2)
        av = Xb[0:IP, 1536:3072].rearrange("p (a c) -> p a c", a=6)
        macc = xnb[:, 768:1024].rearrange("p (t d) -> p t d", t=2)

        assert all(v <= n for v, n in ((taken[id(Gb)], EH * NT * P), (taken[id(Xb)], P * P // 2)))

        block = ctx.enter_context(nc.Block())

        groups = [
            ["ctx", "dft"], ["x", "wkv0T", "wq0T", "rows", "ident", "ones", "lrow"],
            ["idft", "wo0T", "gates", "gamma", "beta", "pos", "io20", "tri", "io9", "io16"],
            ["w_q", "w_qT", "keysT", "downT"],
            ["upl", "Wq1", "Wkv1", "Wo1"],
            ["rw", "w1T", "b1", "w2T", "guT", "dn"],
        ]

        def loaded(eng, g):
            eng.wait_ge(sem(f"load{g}"), 16 * len(groups[g]))

        @block.sync
        def _(sp):
            for g, names in enumerate(groups):
                for n in names:
                    if n == "dn":
                        sp.wait_ge(sem("G_psum"), 2 * EH)
                    src = a[n]
                    if n == "gates":
                        src = src.broadcast_to([P, 4])
                    idx = (slice(None),) * len(ld[n].shape)
                    dst = ld[n][0:1, :] if n == "rows" else ld[n][idx]
                    sp.dma_start(dst, src[idx]).then_inc(sem(f"load{g}"), 16)
            for t in range(NT):
                if t % 2 == 0:
                    sp.wait_ge(sem("x4_ready"), t // 2 + 1)
                sp.dma_start(out.rearrange("b (j p) d -> (b j) p d", p=P)[t], cur[:, t, :]).then_inc(sem("stored"), 16)
            sp.wait_ge(sem("stored"), 16 * NT)

        @block.gpsimd
        def _(g):
            g.iota(iox[:, :, :], pattern=[[1, 16], [0, P]], base=0, channel_multiplier=0,
                   allow_small_or_imprecise_dtypes=True).then_inc(sem("iox_ready"), 1)

            n = [0]

            def link(ins):
                ins.then_inc(sem("pool_chain"), 1)
                n[0] += 1
                g.wait_ge(sem("pool_chain"), n[0])

            loaded(g, 2)
            for t in range(NT):
                q, b = t % 2, t // 2
                g.wait_ge(sem("tix_ready"), t + 1)
                g.tensor_scalar(tixf[:, q, 0:8, :], tix[:, q, 0:8, :], float(NK), None, ALU.mult)
                link(g.tensor_copy(tixf[:, q, 8:16, :], tix[:, q, 8:16, :]))
                xi, yi = tixf[:, q, 0:8, :], tixf[:, q, 8:16, :]
                link(g.tensor_tensor(candi[:, q, :, 0:8], yi, xi[:, :, 0:1].broadcast_to([P, PH, 8]), ALU.add))
                link(g.tensor_tensor(candi[:, q, :, 8:12], yi[:, :, 0:4], xi[:, :, 1:2].broadcast_to([P, PH, 4]), ALU.add))
                link(g.tensor_tensor(candi[:, q, :, 12:16].rearrange("p h (a b) -> p h a b", a=2),
                                     yi[:, :, 0:2].unsqueeze(2).broadcast_to([P, PH, 2, 2]),
                                     xi[:, :, 2:4].unsqueeze(3).broadcast_to([P, PH, 2, 2]), ALU.add))
                link(g.tensor_tensor(candi[:, q, :, 16:20], xi[:, :, 4:8], yi[:, :, 0:1].broadcast_to([P, PH, 4]), ALU.add))
                g.wait_ge(sem("pk_ready"), t + 1)
                link(g.tensor_copy(pkf[:, :], pk[:, q, :, :].rearrange("p h k -> p (h k)")))
                if t >= 1:
                    g.wait_ge(sem("hot_used"), t)
                link(g.tensor_tensor(hot[:, :, :], pkf[:, :].unsqueeze(2).broadcast_to([P, 64, CAND]),
                                     ld["io20"][:, :].unsqueeze(1).broadcast_to([P, 64, CAND]), ALU.subtract))
                link(g.tensor_scalar(hot[:, :, :], hot[:, :, :], 0.0, None, ALU.is_equal))
                h4 = hot[:, :, :].rearrange("p (h k) c -> p h k c", h=PH)
                g.tensor_tensor(h4, h4, candi[:, q, :, :].unsqueeze(2).broadcast_to([P, PH, 8, CAND]),
                                ALU.mult).then_inc(sem("hot_ready"), 1)

        @block.scalar
        def _(act):
            def copy(dst, src, s, scale=1.0):
                act.activation(dst, src, ACT.Copy, scale=scale).then_inc(sem(s), 1)

            loaded(act, 1)
            act.activation(identb[:, :], ident[:, :], ACT.Copy).then_inc(sem("identb_ready"), 1)
            loaded(act, 2)
            act.activation(tg[:, :], ld["gates"][:, :], ACT.Tanh).then_inc(sem("tg_ready"), 1)
            for b in range(B):
                act.wait_ge(sem("cf_psum"), b + 1)
                copy(cf[:, b, :], ps[:, b, :], "cf_ready")
            for k in range(2):
                act.wait_ge(sem("ctxT_psum"), k + 1)
                copy(ctxT[:, 512 * k:512 * k + 512], ps[:, 4 + k, :], "ctxT_ready")
            act.wait_ge(sem("kv_psum"), 1)
            copy(kv[:, 0:4, :], ps[:, 0:4, :], "kv_ready")
            copy(kv[:, 4, :], ps[:, 6, :], "kv_ready")
            act.wait_ge(sem("ang_ready"), 1)
            act.activation(cs[:, :, :, :].rearrange("p a t f -> p (a t f)"),
                           ang[:, 0:2, :].rearrange("p a t -> p (a t)"), ACT.Sin).then_inc(sem("cs_ready"), 1)
            act.wait_ge(sem("xnf_psum"), 1)
            copy(cf[:, 0:2, :], ps[:, 4:6, :], "xnf_ready")
            act.wait_ge(sem("corr_psum"), 1)
            copy(corr[0:64, :], ps[0:64, 0, 0:L], "corr_ready", 1.0 / DK)
            act.wait_ge(sem("corr_max"), 1)
            act.activation(ew[0:64, :], corr[0:64, :], ACT.Exp, bias=sm[0:64, 8:9]).then_inc(sem("ew_ready"), 1)
            act.wait_ge(sem("wcT_psum"), 1)
            copy(wcT[:, :, :].rearrange("p a c -> p (a c)"), ps[:, 1, 0:128], "wcT_ready")
            act.wait_ge(sem("wf_psum"), 1)
            copy(wf[:, :, :].rearrange("p a c -> p (a c)"), ps[:, 2, 0:192], "wf_ready")
            act.wait_ge(sem("ao_psum"), 1)
            copy(aoT[:, :], ps[:, 4:6, :].rearrange("p a c -> p (a c)"), "ao_ready")
            act.wait_ge(sem("xn1T_psum"), 1)
            copy(xnT[:, :], ps[:, 0:2, :].rearrange("p a c -> p (a c)"), "xn1T_ready")
            act.wait_ge(sem("xcT_psum"), 1)
            copy(xcT[:, :], ps[:, 2:4, :].rearrange("p a c -> p (a c)"), "xcT_ready")
            act.wait_ge(sem("cov_psum"), 1)
            copy(cov[:, :], ps[:, 7, 128:256], "cov_ready", 1.0 / (NT * P))
            act.wait_ge(sem("M_psum"), 1)
            copy(M[:, :], ps[:, 4, :], "M_ready")
            copy(crow, ps[32:33, 5, :], "M_ready")
            for t in range(NT):
                act.wait_ge(sem("sim_psum"), t + 1)
                copy(sim[:, t, :], ps[:, t % 4, :], "sim_ready")
            for n in range(2 * EH):
                act.wait_ge(sem("G_psum"), n + 1)
                act.activation(G[:, n // 2, 512 * (n % 2):512 * (n % 2) + 512], ps[:, 4 + n % 4, :],
                               ACT.Gelu_apprx_tanh).then_inc(sem("G_ready"), 1)
            for t in range(NT):
                act.wait_ge(sem("v_psum"), t + 1)
                act.wait_ge(sem("ks_ready"), t + 1)
                act.activation(V[:, t, :, 0:DK], ps[:, 6 + t % 2, 128:256].rearrange("p (h d) -> p h d", h=H),
                               ACT.Copy).then_inc(sem("v_ready"), 1)
                act.wait_ge(sem("kt_psum"), t + 1)
                act.activation(KT[:, :, t * P:t * P + P], bank16(4 + t % 2).rearrange("p (j c) -> p j c", j=8),
                               ACT.Copy).then_inc(sem("kt_ready"), 1)

            def experts_softmax(b):
                for t in (2 * b, 2 * b + 1):
                    act.wait_ge(sem("dd_ready"), t + 1)
                    act.activation(ex_[:, t % 2, :, :], dd[:, t % 2, :, :], ACT.Exp).then_inc(sem("ex_ready"), 1)

            def onehots(b):
                act.wait_ge(sem("eT_psum"), b + 1)
                copy(elT[:, :, :].rearrange("p a c -> p (a c)"), ps[:, 0, 0:256], "elT_ready")
                copy(whl[:, 0, :], ps[:, 0, 256:384], "whi_ready", WSCALE)

            def attention(b):
                act.wait_ge(sem("xn2T_psum"), b + 1)
                copy(xn2T[:, :], ps[:, 7, 0:256], "xn2T_ready")
                act.wait_ge(sem("qT_psum"), b + 1)
                act.activation(QT[:, :, :].rearrange("p j c -> p (j c)"), bank16(4, 2), ACT.Copy).then_inc(sem("QT_ready"), 1)
                act.wait_ge(sem("mT_psum"), b + 1)
                act.activation(mT[:, :], bank16(6)[:, 0:256], ACT.Copy).then_inc(sem("mT_ready"), 1)
                for h in range(H):
                    n = b * H + h
                    act.wait_ge(sem("s2_psum"), n + 1)
                    if n >= 2:
                        act.wait_ge(sem("av_done"), n - 1)
                    act.activation(PE_[:, h % 2, :, :].rearrange("p a c -> p (a c)"), ps[:, 4 + h % 3, :], ACT.Exp,
                                   scale=float(1.0 / np.sqrt(DK))).then_inc(sem("p_ready"), 1)
                act.wait_ge(sem("attT_psum"), b + 1)
                copy(attT[:, :], ps[:, 4, 0:256], "attT_ready")

            def moe(b):
                act.wait_ge(sem("xn3T_psum"), b + 1)
                copy(xn3T[:, :], ps[:, 0, 0:256], "xn3T_ready")
                act.wait_ge(sem("ah_psum"), b + 1)
                act.activation(ah[0:AH, :], ps[0:AH, 1, 256:512], ACT.Gelu_apprx_tanh,
                               bias=ld["b1"][:, 0:1]).then_inc(sem("ah_ready"), 1)
                act.wait_ge(sem("rl_ready"), b + 1)
                act.activation(rt[:, 1, :], rt[:, 0, :], ACT.Exp).then_inc(sem("rexp_ready"), 1)
                for n in range(E8 * IT):
                    m = b * E8 * IT + n
                    act.wait_ge(sem("gu_psum"), m + 1)
                    if m >= 2:
                        act.wait_ge(sem("av_ready"), m - 1)
                    act.activation(sg[:, n % 2, :], ps[0:IP, n % 3, 0:256], ACT.Silu).then_inc(sem("sg_ready"), 1)

            experts_softmax(0)
            for b in range(B):
                if b + 1 < B:
                    experts_softmax(b + 1)
                onehots(b)
                attention(b)
                moe(b)

        @block.vector
        def _(v):
            n = [0]

            def link(ins):
                ins.then_inc(sem("dve_chain"), 1)
                n[0] += 1
                v.wait_ge(sem("dve_chain"), n[0])

            def layer_norm(dst, src, k, signal):
                for t in range(k):
                    i = v.bn_stats(st[:, t, :], src[:, t, :])
                link(i)
                for t in range(k):
                    i = v.bn_aggr(mv[:, t, :], st[:, t, :])
                link(i)
                rsqrt(rs, mv[:, 0:k, 1], k)
                for t in range(k):
                    i = v.tensor_scalar(dst[:, t, :], src[:, t, :], mv[:, t, 0:1], rs[:, 1, t:t + 1],
                                        ALU.subtract, ALU.mult)
                i.then_inc(sem(signal), 1)

            def rsqrt(w, src, k):
                x, y, u = w[:, 0, 0:k], w[:, 1, 0:k], w[:, 2, 0:k]
                link(v.tensor_scalar(x, src, EPS, None, ALU.add))
                link(v.tensor_scalar(u.bitcast(I32), x.bitcast(I32), 1, None, ALU.logical_shift_right))
                link(v.tensor_scalar(y.bitcast(I32), u.bitcast(I32), -1.0, float(0x5f3759df), ALU.mult, ALU.add))
                for _ in range(3):
                    link(v.scalar_tensor_tensor(u, y, -0.5, y, ALU.mult, ALU.mult))
                    link(v.tensor_tensor(u, u, x, ALU.mult))
                    link(v.scalar_tensor_tensor(y, u, 1.5, y, ALU.add, ALU.mult))

            v.memset(V[:, :, :, DK:DK + 1], 1.0)
            v.memset(ah[:, :], 1.0)
            v.memset(mrep[:, :, :], 0.0).then_inc(sem("consts"), 1)
            v.wait_ge(sem("consts"), 1)
            loaded(v, 1)
            loaded(v, 2)
            link(v.tensor_copy(posf[:, :], ld["pos"][:, :]))
            A0, A1, A2 = ang[:, 0, :], ang[:, 1, :], ang[:, 2, :]
            inv = [float(x) for x in (np.float32(1.0) / np.float32(10000.0) ** (np.arange(0, DK, 2, dtype=np.float32) / np.float32(DK)))]
            for f in range(4):
                i = v.tensor_scalar(A2.rearrange("p (t f) -> p t f", f=4)[:, :, f], posf[:, :], inv[f], None, ALU.mult)
            link(i)
            for dst, turn, shift in ((A0, 0.25, TWO_PI / 4), (A1, 0.0, 0.0)):
                k = sm[:, :]
                link(v.tensor_scalar(k, A2, 1.0 / TWO_PI, turn, ALU.mult, ALU.add))
                link(v.tensor_scalar(k, k, ROUND, None, ALU.add))
                link(v.tensor_scalar(k, k, ROUND, None, ALU.subtract))
                link(v.scalar_tensor_tensor(dst, k, -C1, A2, ALU.mult, ALU.add))
                link(v.scalar_tensor_tensor(dst, k, -C2, dst, ALU.mult, ALU.add))
                link(v.scalar_tensor_tensor(dst, k, -C3, dst, ALU.mult, ALU.add))
                link(v.tensor_scalar(dst, dst, shift, None, ALU.add))
                i = v.tensor_scalar(dst, dst, 3.1415925, -3.1415925, ALU.min, ALU.max)
                if turn:
                    link(i)
            i.then_inc(sem("ang_ready"), 1)

            layer_norm(xn, cur, NT, "xn0_ready")
            v.wait_ge(sem("q_psum"), 1)
            link(v.tensor_copy(qf[:, :, :], ps[:, 2:4, :]))
            v.wait_ge(sem("kv_ready"), 2)
            t0, t1 = tmp[:, 0:512], tmp[:, 512:1024]

            def cross(dst, x0, y0, x1, y1, op, last=None):
                v.tensor_tensor(t0, x0, y0, ALU.mult)
                link(v.tensor_tensor(t1, x1, y1, ALU.mult))
                i = v.tensor_tensor(dst, t0, t1, op)
                if last:
                    i.then_inc(sem(last), 1)
                else:
                    link(i)

            cross(spec[:, 0, :], qf[:, 0, :], kv[:, KC, :], qf[:, 1, :], kv[:, KS, :], ALU.add)
            cross(spec[:, 1, :], qf[:, 1, :], kv[:, KCN, :], qf[:, 0, :], kv[:, KS, :], ALU.subtract)
            v.tensor_reduce(cps[:, :, :].rearrange("p a c -> p (a c)"),
                            spec[:, :, :].rearrange("p a (c d) -> p (a c) d", d=DK), AX, ALU.add).then_inc(sem("cps_ready"), 1)
            v.wait_ge(sem("corr_ready"), 1)
            link(v.max(sm[0:64, 0:8], corr[0:64, :]))
            v.tensor_scalar(sm[0:64, 8:9], sm[0:64, 0:1], -1.0, None, ALU.mult).then_inc(sem("corr_max"), 1)
            v.wait_ge(sem("ew_ready"), 1)
            link(v.scalar_tensor_tensor(ew[0:64, :], corr[0:64, :], sm[0:64, TOP - 1:TOP], ew[0:64, :], ALU.is_ge, ALU.mult))
            link(v.tensor_reduce(sm[0:64, 9:10], ew[0:64, :], AX, ALU.add))
            link(v.reciprocal(sm[0:64, 10:11], sm[0:64, 9:10]))
            v.tensor_scalar(ew[0:64, :], ew[0:64, :], sm[0:64, 10:11], None, ALU.mult).then_inc(sem("wc_ready"), 1)
            v.wait_ge(sem("wf_ready"), 1)

            def spread(k):
                return wf[:, k, :].unsqueeze(2).broadcast_to([P, B * H, DK])

            def wide(x):
                return x.rearrange("p (c d) -> p c d", d=DK)

            t0, t1 = wide(tmp[:, 0:512]), wide(tmp[:, 512:1024])
            vc, vs = wide(kv[:, VVC, :]), wide(kv[:, VVS, :])
            cross(wide(spec[:, 0, :]), vc, spread(0), vs, spread(1), ALU.subtract)
            cross(wide(spec[:, 1, :]), vc, spread(1), vs, spread(2), ALU.add, "of_ready")
            v.wait_ge(sem("tg_ready"), 1)
            v.wait_ge(sem("y0_psum"), 1)
            link(v.scalar_tensor_tensor(cur[:, :, :], ps[:, 6:8, :].rearrange("p a (t d) -> p (a t) d", t=4), tg[:, 0:1],
                                        cur[:, :, :], ALU.mult, ALU.add))

            layer_norm(xn, cur, NT, "xn1_ready")
            v.wait_ge(sem("xn1_ready"), 1)
            v.wait_ge(sem("mean_psum"), 1)
            v.tensor_tensor(xc[:, :, :], xn[:, :, :], ps[:, 7, 0:128].unsqueeze(1).broadcast_to([P, NT, D]),
                            ALU.subtract).then_inc(sem("xc_ready"), 1)
            v.wait_ge(sem("cw_psum"), 1)
            loaded(v, 3)
            link(v.tensor_tensor(tmp[:, :], ps[:, 0:4, :].rearrange("p a c -> p (a c)"),
                                 ld["w_qT"][:, :, :].rearrange("p a c -> p (a c)"), ALU.mult))
            link(v.tensor_reduce(var[:, 3, :], tmp[:, :].rearrange("p (c d) -> p c d", d=D), AX, ALU.add))
            rsqrt(var, var[:, 3, :], 16)
            link(v.tensor_tensor(var[:, 1, :], var[:, 1, :], ld["gamma"][:, :], ALU.mult))
            v.tensor_tensor(keyS[:, :, :], ld["keysT"][:, :, :], var[:, 1, :].unsqueeze(2).broadcast_to([P, 16, NK]),
                            ALU.mult).then_inc(sem("keyS_ready"), 1)

            def top_keys(t):
                q = t % 2
                v.wait_ge(sem("sim_ready"), t + 1)
                if t >= 2:
                    v.wait_ge(sem("hot_ready"), t - 1)
                s3 = sim[:, t, :].rearrange("p (g k) -> p g k", k=NK)
                for g in range(16):
                    i = v.max(top[:, q, g, :], s3[:, g, :])
                link(i)
                for g in range(16):
                    i = v.max_index(tix[:, q, g, :], top[:, q, g, :], s3[:, g, :])
                i.then_inc(sem("tix_ready"), 1)
                xs, ys = top[:, q, 0:8, :], top[:, q, 8:16, :]
                v.tensor_tensor(cand[:, q, :, 0:8], ys, xs[:, :, 0:1].broadcast_to([P, PH, 8]), ALU.add)
                v.tensor_tensor(cand[:, q, :, 8:12], ys[:, :, 0:4], xs[:, :, 1:2].broadcast_to([P, PH, 4]), ALU.add)
                v.tensor_tensor(cand[:, q, :, 12:16].rearrange("p h (a b) -> p h a b", a=2),
                                ys[:, :, 0:2].unsqueeze(2).broadcast_to([P, PH, 2, 2]),
                                xs[:, :, 2:4].unsqueeze(3).broadcast_to([P, PH, 2, 2]), ALU.add)
                link(v.tensor_tensor(cand[:, q, :, 16:20], xs[:, :, 4:8], ys[:, :, 0:1].broadcast_to([P, PH, 4]), ALU.add))
                for h in range(PH):
                    i = v.max(sc[:, q, h, :], cand[:, q, h, :])
                link(i)
                for h in range(PH):
                    i = v.max_index(pk[:, q, h, :], sc[:, q, h, :], cand[:, q, h, :])
                i.then_inc(sem("pk_ready"), 1)
                v.tensor_tensor(dd[:, q, :, :], sc[:, q, :, :], sc[:, q, :, 0:1].broadcast_to([P, PH, 8]),
                                ALU.subtract).then_inc(sem("dd_ready"), 1)

            def top_weights(t):
                q, b = t % 2, t // 2
                v.wait_ge(sem("ex_ready"), t + 1)
                if b >= 2:
                    v.wait_ge(sem("eT_psum"), b - 1)
                link(v.tensor_reduce(zz[:, q, :], ex_[:, q, :, :], AX, ALU.add))
                link(v.reciprocal(zz[:, q, :], zz[:, q, :]))
                v.tensor_tensor(wts[:, b % 2, q, :].rearrange("p (h k) -> p h k", h=PH), ex_[:, q, :, :],
                                zz[:, q, :].unsqueeze(2).broadcast_to([P, PH, 8]), ALU.mult)
                v.wait_ge(sem("hot_ready"), t + 1)
                v.tensor_reduce(eid[:, b % 2, q, :], hot[:, :, :], AX, ALU.add).then_inc(sem("hot_used"), 1)

            def onehots(b):
                v.wait_ge(sem("hot_used"), 2 * b + 2)
                e = eid[:, b % 2, :, :].rearrange("p a c -> p (a c)")
                link(v.tensor_copy(eidi[:, 0, :], e))
                v.tensor_scalar(eidi[:, 1, :], eidi[:, 0, :], P - 1, None, ALU.bitwise_and)
                link(v.tensor_scalar(eidi[:, 2, :], eidi[:, 0, :], 7, None, ALU.logical_shift_right))
                if b >= 1:
                    v.wait_ge(sem("eT_psum"), b)
                v.tensor_copy(elh[:, :, :], eidi[:, 1:3, :]).then_inc(sem("elh_ready"), 1)
                v.wait_ge(sem("whi_ready"), b + 1)
                v.scalar_tensor_tensor(whl[:, 1, :], ps[:, 0, 256:384], WSCALE, whl[:, 0, :],
                                       ALU.mult, ALU.subtract).then_inc(sem("wlo_ready"), 1)
                if b >= 1:
                    v.wait_ge(sem("W_psum"), b)
                v.wait_ge(sem("iox_ready"), 1)
                link(v.tensor_tensor(Yq[:, :, :], elT[:, 1, :].unsqueeze(1).broadcast_to([P, EH, P]), iox[:, 0:EH, :], ALU.is_equal))
                v.wait_ge(sem("wlo_ready"), b + 1)
                for k in range(2):
                    v.tensor_tensor(Y[:, k, :, :], Yq[:, :, :], whl[:, k, :].unsqueeze(1).broadcast_to([P, EH, P]), ALU.mult)
                link(v.tensor_tensor(elS[:, :, :], elT[:, 0, :].unsqueeze(1).broadcast_to([P, EH, P]),
                                     ld["io16"][:, :].unsqueeze(2).broadcast_to([P, EH, P]), ALU.subtract))
                v.tensor_tensor(X.rearrange("p (c e) t -> p c e t", c=EH), elS[:, :, :].unsqueeze(2).broadcast_to([P, EH, 16, P]),
                                iox[:, :, :].unsqueeze(1).broadcast_to([P, EH, 16, P]), ALU.is_equal).then_inc(sem("X_ready"), 1)

            def mix_experts(b):
                v.wait_ge(sem("W_psum"), b + 1)
                if b == 0:
                    v.wait_ge(sem("G_ready"), 2 * EH)
                v.scalar_tensor_tensor(HD[:, :, :].rearrange("p e t -> p t e"),
                                       ps[:, 0:4, :].rearrange("p a (t e) -> p (a t) e", e=EH), 1.0 / WSCALE,
                                       G[:, :, b * L:b * L + L].rearrange("p e t -> p t e"),
                                       ALU.mult, ALU.mult).then_inc(sem("HD_ready"), 1)
                v.wait_ge(sem("y1_psum"), b + 1)
                x2 = cur[:, 2 * b:2 * b + 2, :]
                link(v.scalar_tensor_tensor(x2, ps[:, 0, 0:256].rearrange("p (t d) -> p t d", t=2), tg[:, 2:3], x2,
                                            ALU.mult, ALU.add))
                layer_norm(xn2, x2, 2, "xn2_ready")

            def rope(src, k, c0):
                for t in range(k):
                    s = src[t].rearrange("p (h a d) -> p h a d", h=H, a=2)
                    cc = cs[:, 0, c0 + t, :].unsqueeze(1).unsqueeze(1).broadcast_to([P, H, 2, 4])
                    ss = cs[:, 1, c0 + t, :].unsqueeze(1).unsqueeze(1).broadcast_to([P, H, 2, 4])
                    v.tensor_tensor(ra[:, t, :].rearrange("p (h a d) -> p h a d", h=H, a=2), s, cc, ALU.mult)
                    link(v.tensor_tensor(rb[:, t, :].rearrange("p (h a d) -> p h a d", h=H, a=2), s, ss, ALU.mult))
                r3 = [w[:, 0:k, :].rearrange("p t (h a d) -> p (t h) a d", h=H, a=2) for w in (rq, ra, rb)]
                v.tensor_tensor(r3[0][:, :, 0, :], r3[1][:, :, 0, :], r3[2][:, :, 1, :], ALU.subtract)
                link(v.tensor_tensor(r3[0][:, :, 1, :], r3[1][:, :, 1, :], r3[2][:, :, 0, :], ALU.add))

            def split(k, keys, signal):
                r = rq[:, 0:k, :].rearrange("p t (h d) -> p (t h) d", h=H)
                s = qs[:, 0:k * H, :, :]
                slots = [s[:, :, 0:7:3, :], s[:, :, 1:8:3, :], s[:, :, 2:6:3, :]] if keys else \
                    [s[:, :, 0:3, :], s[:, :, 3:6, :], s[:, :, 6:8, :]]
                for p, z in enumerate(slots):
                    w = z.shape[2]
                    i = v.tensor_copy(z, r.unsqueeze(2).broadcast_to([P, k * H, w, DK]))
                    if p == 2:
                        i.then_inc(sem(signal), 1)
                    else:
                        link(i)
                        link(v.tensor_tensor(r, r, z[:, :, 0, :], ALU.subtract))

            def ctx_keys(t):
                v.wait_ge(sem("v_psum"), t + 1)
                if t == 0:
                    v.wait_ge(sem("cs_ready"), 1)
                rope([ps[:, 6 + t % 2, 0:128]], 1, NT + t)
                if t >= 1:
                    v.wait_ge(sem("kt_psum"), t)
                split(1, True, "ks_ready")

            def attention(b):
                v.wait_ge(sem("q1_psum"), b + 1)
                rope([ps[:, 7, 256:384], ps[:, 7, 384:512]], 2, 2 * b)
                split(2, False, "qs_ready")
                for g in range(8):
                    v.wait_ge(sem("s1_psum"), b * 8 + g + 1)
                    qt, gg = g // 4, g % 4
                    bk = 4 + 2 * (g % 2)
                    i = v.tensor_reduce(mx[:, qt, 4 * gg:4 * gg + 4],
                                        ps[:, bk:bk + 2, :].rearrange("p e (j k) -> p (e j) k", j=2), AX, ALU.max)
                    i.then_inc(sem("mx_ready"), 1)
                v.wait_ge(sem("mx_ready"), b * 8 + 8)
                v.tensor_scalar(mrep[:, :, 0:H], mx[:, :, :], -1.0, None, ALU.mult)
                v.tensor_scalar(mrep[:, :, 64:64 + H], mx[:, :, :], -1.0, None, ALU.mult).then_inc(sem("mrep_ready"), 1)
                v.wait_ge(sem("av_done"), H * (b + 1))
                o = ps[:, 7, 0:2 * H * 9].rearrange("p (c d) -> p c d", d=9)
                link(v.reciprocal(rcp[:, :], o[:, :, 8]))
                v.tensor_tensor(att[:, :, :].rearrange("p t (h d) -> p (t h) d", h=H), o[:, :, 0:8],
                                rcp[:, :].unsqueeze(2).broadcast_to([P, 2 * H, DK]), ALU.mult).then_inc(sem("att_ready"), 1)
                v.wait_ge(sem("y2_psum"), b + 1)
                x3 = cur[:, 2 * b:2 * b + 2, :]
                link(v.scalar_tensor_tensor(x3, ps[:, 5, 0:256].rearrange("p (t d) -> p t d", t=2), tg[:, 1:2], x3,
                                            ALU.mult, ALU.add))
                layer_norm(xn3, x3, 2, "xn3_ready")

            def moe(b):
                R = [rt[:, k, :].rearrange("p (t e) -> p t e", t=2) for k in range(8)]
                c1, c2, c3 = sm[:, 0:2], sm[:, 2:4], sm[:, 4:6]
                v.wait_ge(sem("al_psum"), b + 1)
                lg = ps[:, 1, 0:16].rearrange("p (t e) -> p t e", t=2)
                link(v.tensor_reduce(c1, lg, AX, ALU.max))
                link(v.tensor_tensor(R[0], lg, c1.unsqueeze(2).broadcast_to([P, 2, 8]), ALU.subtract))
                link(v.tensor_scalar(R[2][:, :, 0:MK], ps[:, 1, 16:28].rearrange("p (t e) -> p t e", t=2), -30.0, 30.0,
                                     ALU.max, ALU.min))
                v.tensor_reduce(c2, R[2][:, :, 0:MK], AX, ALU.max).then_inc(sem("rl_ready"), 1)
                v.wait_ge(sem("rl_ready"), b + 1)
                link(v.tensor_tensor(R[3][:, :, 0:MK], R[2][:, :, 0:MK], c2.unsqueeze(2).broadcast_to([P, 2, MK]), ALU.is_ge))
                link(v.tensor_tensor(R[3][:, :, 0:MK], R[3][:, :, 0:MK], ld["io9"][:, :].unsqueeze(1).broadcast_to([P, 2, MK]), ALU.mult))
                link(v.tensor_reduce(c3, R[3][:, :, 0:MK], AX, ALU.min))
                link(v.tensor_scalar(c3, c3, 10.0, None, ALU.add))
                v.wait_ge(sem("rexp_ready"), b + 1)
                link(v.tensor_reduce(c1, R[1], AX, ALU.add))
                link(v.reciprocal(c1, c1))
                link(v.tensor_tensor(R[4], R[1], c1.unsqueeze(2).broadcast_to([P, 2, 8]), ALU.mult))
                other = R[4].unsqueeze(2).broadcast_to([P, 2, 8, 8])
                own = R[4].unsqueeze(3).broadcast_to([P, 2, 8, 8])
                v.tensor_tensor(cmp[:, 0, :, :, :], other, own, ALU.is_gt)
                link(v.tensor_tensor(cmp[:, 1, :, :, :], other, own, ALU.is_equal))
                link(v.tensor_tensor(cmp[:, 1, :, :, :], cmp[:, 1, :, :, :], ld["tri"][:, :, :].unsqueeze(1).broadcast_to([P, 2, 8, 8]), ALU.mult))
                link(v.tensor_tensor(cmp[:, 0, :, :, :], cmp[:, 0, :, :, :], cmp[:, 1, :, :, :], ALU.add))
                link(v.tensor_reduce(rt[:, 5, :], cmp[:, 0, :, :, :].rearrange("p t e f -> p (t e) f"), AX, ALU.add))
                link(v.tensor_tensor(R[5], R[5], c3.unsqueeze(2).broadcast_to([P, 2, 8]), ALU.is_lt))
                link(v.tensor_tensor(R[6], R[5], R[4], ALU.mult))

                def product(n):
                    m = b * E8 * IT + n
                    v.wait_ge(sem("sg_ready"), m + 1)
                    if m >= 6:
                        v.wait_ge(sem("y3_psum"), (m - 6) // IT + 1)
                    v.tensor_tensor(av[:, n % 6, :], sg[:, n % 2, :], ps[0:IP, n % 3, 256:512], ALU.mult).then_inc(sem("av_ready"), 1)

                def gather(e):
                    v.wait_ge(sem("y3_psum"), b * E8 + e + 1)
                    for t in range(2):
                        y = ps[:, 3, t * D:t * D + D]
                        s = R[6][:, t, e:e + 1]
                        if e == 0:
                            i = v.tensor_scalar(macc[:, t, :], y, s, None, ALU.mult)
                        else:
                            i = v.scalar_tensor_tensor(macc[:, t, :], y, s, macc[:, t, :], ALU.mult, ALU.add)
                    i.then_inc(sem("y3_used"), 1)
                    v.wait_ge(sem("y3_used"), b * E8 + e + 1)

                for e in range(E8):
                    for k in range(IT):
                        product(e * IT + k)
                    if e:
                        gather(e - 1)
                gather(E8 - 1)
                x4 = cur[:, 2 * b:2 * b + 2, :]
                v.scalar_tensor_tensor(x4, macc[:, :, :], tg[:, 3:4], x4, ALU.mult, ALU.add).then_inc(sem("x4_ready"), 1)

            top_keys(0)
            top_keys(1)
            for t in range(NT):
                ctx_keys(t)
            top_weights(0)
            top_weights(1)
            for b in range(B):
                if b + 1 < B:
                    for t in (2 * b + 2, 2 * b + 3):
                        top_keys(t)
                    for t in (2 * b + 2, 2 * b + 3):
                        top_weights(t)
                onehots(b)
                mix_experts(b)
                attention(b)
                moe(b)

        @block.tensor
        def _(pe):
            def mm(o, l, r, start=True, stop=True):
                return pe.matmul(o, l, r, start=start, stop=stop)

            def bias(o, row, w):
                return mm(o, ones[0:1, 0:P], ld["rows"][0:1, row:row + w], False, True)

            BQ, BKV, BO0, BQ1, BKV1, BO1 = 0, 128, 384, 512, 640, 896
            loaded(pe, 0)
            ctxs, dft, idft = ld["ctx"], ld["dft"], ld["idft"]
            for b in range(B):
                for k in range(2):
                    i = mm(ps[:, b, :], ctxs[:, 2 * b + k, :], dft[:, k, :, :].rearrange("p a c -> p (a c)"), k == 0, k == 1)
                i.then_inc(sem("cf_psum"), 1)
            loaded(pe, 1)
            for k in range(2):
                for t in range(4):
                    i = pe.transpose(ps[:, 4 + k, t * P:t * P + P], ctxs[:, 4 * k + t, :], ident[:, :])
                i.then_inc(sem("ctxT_psum"), 1)
            pe.wait_ge(sem("cf_ready"), B)
            for s, (bk, var_, w) in enumerate(((0, VC, 0), (1, VS, 0), (2, VCN, 0), (3, VC, 128), (6, VSN, 128))):
                for b in range(B):
                    o = ps[:, bk, b * P:b * P + P]
                    i = mm(o, cf[:, b, var_ * P:var_ * P + P], ld["wkv0T"][:, w:w + 128], True, var_ != VC)
                    if var_ == VC:
                        i = mm(o, ld["lrow"][0:1, 0:P], ld["rows"][0:1, BKV + w:BKV + w + 128], False, True)
            i.then_inc(sem("kv_psum"), 1)
            pe.wait_ge(sem("xn0_ready"), 1)
            pe.wait_ge(sem("ctxT_ready"), 2)
            pe.wait_ge(sem("kv_ready"), 2)
            for b in range(B):
                o = ps[:, 4 + b // 2, (b % 2) * 256:(b % 2) * 256 + 256]
                for k in range(2):
                    i = mm(o, xn[:, 2 * b + k, :], dft[:, k, 0:2, :].rearrange("p a c -> p (a c)"), k == 0, k == 1)
            i.then_inc(sem("xnf_psum"), 1)
            pe.wait_ge(sem("xnf_ready"), 1)
            for k in range(2):
                for b in range(B):
                    o = ps[:, 2 + k, b * P:b * P + P]
                    i = mm(o, cf[:, b // 2, (b % 2) * 256 + k * P:(b % 2) * 256 + k * P + P], ld["wq0T"][:, :], True, k == 1)
                    if k == 0:
                        i = mm(o, ld["lrow"][0:1, 0:P], ld["rows"][0:1, BQ:BQ + 128], False, True)
            i.then_inc(sem("q_psum"), 1)
            loaded(pe, 2)
            pe.wait_ge(sem("cps_ready"), 1)
            for k in range(2):
                i = mm(ps[0:64, 0, 0:L], cps[:, k, :], idft[:, k, :], k == 0, k == 1)
            i.then_inc(sem("corr_psum"), 1)
            pe.wait_ge(sem("wc_ready"), 1)
            for k in range(2):
                i = pe.transpose(ps[:, 1, k * 64:k * 64 + 64], ew[0:64, k * P:k * P + P], ident[0:64, 0:64])
            i.then_inc(sem("wcT_psum"), 1)
            pe.wait_ge(sem("wcT_ready"), 1)
            for s, var_ in enumerate((VC, VS, VCN)):
                for k in range(2):
                    i = mm(ps[:, 2, s * 64:s * 64 + 64], dft[:, k, var_, :], wcT[:, k, :], k == 0, k == 1)
            i.then_inc(sem("wf_psum"), 1)
            pe.wait_ge(sem("of_ready"), 1)
            for b in range(B):
                o = ps[:, 4 + b // 2, (b % 2) * 256:(b % 2) * 256 + 256]
                for k in range(2):
                    i = mm(o, spec[:, k, b * P:b * P + P], idft[:, k, :], k == 0, k == 1)
            i.then_inc(sem("ao_psum"), 1)
            pe.wait_ge(sem("ao_ready"), 1)
            for t in range(NT):
                o = ps[:, 6 + t // 4, (t % 4) * P:(t % 4) * P + P]
                mm(o, aoT[:, t * P:t * P + P], ld["wo0T"][:, :], True, False)
                i = bias(o, BO0, 128)
            i.then_inc(sem("y0_psum"), 1)

            pe.wait_ge(sem("xn1_ready"), 1)
            for t in range(NT):
                i = mm(ps[:, 7, 0:128], ld["ones"][:, P:2 * P], xn[:, t, :], t == 0, t == NT - 1)
            i.then_inc(sem("mean_psum"), 1)
            for t in range(NT):
                i = pe.transpose(ps[:, t // 4, (t % 4) * P:(t % 4) * P + P], xn[:, t, :], ident[:, :])
            i.then_inc(sem("xn1T_psum"), 1)
            pe.wait_ge(sem("xc_ready"), 1)
            for t in range(NT):
                i = mm(ps[:, 7, 128:256], xc[:, t, :], xc[:, t, :], t == 0, t == NT - 1)
            i.then_inc(sem("cov_psum"), 1)
            for t in range(NT):
                i = pe.transpose(ps[:, 2 + t // 4, (t % 4) * P:(t % 4) * P + P], xc[:, t, :], ident[:, :])
            i.then_inc(sem("xcT_psum"), 1)
            loaded(pe, 3)
            pe.wait_ge(sem("cov_ready"), 1)
            pe.wait_ge(sem("xcT_ready"), 1)
            w_q, w_qT, keysT = ld["w_q"], ld["w_qT"], ld["keysT"]
            for c in range(16):
                i = mm(ps[:, c // 4, (c % 4) * P:(c % 4) * P + P], w_q[:, c * P:c * P + P], cov[:, :])
            i.then_inc(sem("cw_psum"), 1)
            for c in range(16):
                i = mm(ps[32:33, 5, c * NK:c * NK + NK], ld["beta"][:, c:c + 1], keysT[:, c, :])
            pe.wait_ge(sem("keyS_ready"), 1)
            for c in range(16):
                i = mm(ps[:, 4, c * NK:c * NK + NK], w_qT[:, c, :], keyS[:, c, :])
            i.then_inc(sem("M_psum"), 1)
            pe.wait_ge(sem("M_ready"), 2)
            for t in range(NT):
                if t >= 4:
                    pe.wait_ge(sem("sim_ready"), t - 3)
                mm(ps[:, t % 4, :], xcT[:, t * P:t * P + P], M[:, :], True, False)
                mm(ps[:, t % 4, :], ones[32:33, 0:P], crow, False, True).then_inc(sem("sim_psum"), 1)
            for n in range(2 * EH):
                if n >= 4:
                    pe.wait_ge(sem("G_ready"), n - 3)
                mm(ps[:, 4 + n % 4, :], ld["downT"][:, (n // 2) * P:(n // 2) * P + P],
                   xnT[:, (n % 2) * 512:(n % 2) * 512 + 512]).then_inc(sem("G_psum"), 1)
            loaded(pe, 4)
            pe.wait_ge(sem("G_ready"), 2 * EH)
            pe.wait_ge(sem("identb_ready"), 1)

            def ctx_kv(t):
                if t >= 2:
                    pe.wait_ge(sem("v_ready"), t - 1)
                    pe.wait_ge(sem("ks_ready"), t - 1)
                mm(ps[:, 6 + t % 2, 0:256], ctxT[:, t * P:t * P + P], ld["Wkv1"][:, :], True, False)
                bias(ps[:, 6 + t % 2, 0:256], BKV1, 256).then_inc(sem("v_psum"), 1)

            ctx_kv(0)
            for t in range(NT):
                if t + 1 < NT:
                    ctx_kv(t + 1)
                pe.wait_ge(sem("ks_ready"), t + 1)
                if t >= 2:
                    pe.wait_ge(sem("kt_ready"), t - 1)
                for j in range(8):
                    i = pe.transpose(bank16(4 + t % 2)[:, j * P:j * P + P],
                                     qs[:, 2 * j:2 * j + 2, :, :].rearrange("p h s d -> p (h s d)"), identb[:, :])
                i.then_inc(sem("kt_psum"), 1)

            def onehots(b):
                pe.wait_ge(sem("elh_ready"), b + 1)
                if b == 0:
                    pe.wait_ge(sem("sim_ready"), NT)
                if b >= 1:
                    pe.wait_ge(sem("x4_ready"), b)
                pe.transpose(ps[:, 0, 0:128], elh[:, 0, :], ident[:, :])
                pe.transpose(ps[:, 0, 128:256], elh[:, 1, :], ident[:, :])
                pe.transpose(ps[:, 0, 256:384], wts[:, b % 2, :, :].rearrange("p a c -> p (a c)"),
                             ident[:, :]).then_inc(sem("eT_psum"), 1)
                pe.wait_ge(sem("X_ready"), b + 1)
                for t in range(P):
                    for half in range(2):
                        r = slice(64 * half, 64 * half + 64)
                        o = ps[:, 2 * half + t // 64, (t % 64) * EH:(t % 64) * EH + EH]
                        mm(o, X[r, :, t], Y[r, 0, :, t], True, False)
                        i = mm(o, X[r, :, t], Y[r, 1, :, t], False, True)
                i.then_inc(sem("W_psum"), 1)

            def mix_experts(b):
                pe.wait_ge(sem("HD_ready"), b + 1)
                for t in range(2):
                    for e in range(EH):
                        i = mm(ps[:, 0, t * D:t * D + D], HD[:, e, t * P:t * P + P], ld["upl"][:, e, :], e == 0, e == EH - 1)
                i.then_inc(sem("y1_psum"), 1)

            def attention(b):
                pe.wait_ge(sem("xn2_ready"), b + 1)
                if b == 0:
                    pe.wait_ge(sem("kt_ready"), NT)
                    pe.wait_ge(sem("v_ready"), NT)
                for t in range(2):
                    i = pe.transpose(ps[:, 7, t * P:t * P + P], xn2[:, t, :], ident[:, :])
                i.then_inc(sem("xn2T_psum"), 1)
                pe.wait_ge(sem("xn2T_ready"), b + 1)
                for t in range(2):
                    o = ps[:, 7, 256 + t * P:256 + t * P + P]
                    mm(o, xn2T[:, t * P:t * P + P], ld["Wq1"][:, :], True, False)
                    i = bias(o, BQ1, 128)
                i.then_inc(sem("q1_psum"), 1)
                pe.wait_ge(sem("qs_ready"), b + 1)
                for j in range(8):
                    for t in range(2):
                        i = pe.transpose(bank16(4, 2)[:, (2 * j + t) * P:(2 * j + t) * P + P],
                                         qs[:, 16 * t + 2 * j:16 * t + 2 * j + 2, :, :].rearrange("p h s d -> p (h s d)"),
                                         identb[:, :])
                i.then_inc(sem("qT_psum"), 1)
                pe.wait_ge(sem("QT_ready"), b + 1)
                for g in range(8):
                    qt, gg = g // 4, g % 4
                    bk = 4 + 2 * (g % 2)
                    if g >= 2:
                        pe.wait_ge(sem("mx_ready"), b * 8 + g - 1)
                    for jj in range(2):
                        for e in range(2):
                            r = slice(64 * e, 64 * e + 64)
                            i = mm(ps[:, bk + e, jj * 256:jj * 256 + 256], QT[r, 2 * gg + jj, qt * P:qt * P + P],
                                   KT[r, 2 * gg + jj, b * L:b * L + L])
                    i.then_inc(sem("s1_psum"), 1)
                pe.wait_ge(sem("mrep_ready"), b + 1)
                for t in range(2):
                    i = pe.transpose(bank16(6)[:, t * P:t * P + P], mrep[:, t, :], identb[:, :])
                i.then_inc(sem("mT_psum"), 1)
                pe.wait_ge(sem("mT_ready"), b + 1)

                def scores(h):
                    n = b * H + h
                    if h >= 3:
                        pe.wait_ge(sem("p_ready"), n - 2)
                    j, e = h // 2, h % 2
                    r = slice(64 * e, 64 * e + 64)
                    c = 64 * e + (j // 2) * 4 + e * 2 + j % 2
                    for k in range(2):
                        o = ps[:, 4 + h % 3, k * 256:k * 256 + 256]
                        mm(o, KT[r, j, b * L + k * P:b * L + k * P + P], QT[r, j, :], True, False)
                        i = mm(o, identb[r, c:c + 1].broadcast_to([64, P]), mT[r, :], False, True)
                    i.then_inc(sem("s2_psum"), 1)

                def values(h):
                    n = b * H + h
                    pe.wait_ge(sem("p_ready"), n + 1)
                    for t in range(2):
                        for k in range(2):
                            i = mm(ps[:, 7, (t * H + h) * 9:(t * H + h) * 9 + 9], PE_[:, h % 2, k, t * P:t * P + P],
                                   V[:, 2 * b + k, h, :], k == 0, k == 1)
                    i.then_inc(sem("av_done"), 1)

                scores(0)
                scores(1)
                for h in range(H):
                    if h + 2 < H:
                        scores(h + 2)
                    values(h)
                pe.wait_ge(sem("att_ready"), b + 1)
                for t in range(2):
                    i = pe.transpose(ps[:, 4, t * P:t * P + P], att[:, t, :], ident[:, :])
                i.then_inc(sem("attT_psum"), 1)
                pe.wait_ge(sem("attT_ready"), b + 1)
                for t in range(2):
                    o = ps[:, 5, t * P:t * P + P]
                    mm(o, attT[:, t * P:t * P + P], ld["Wo1"][:, :], True, False)
                    i = bias(o, BO1, 128)
                i.then_inc(sem("y2_psum"), 1)

            def moe(b):
                if b == 0:
                    loaded(pe, 5)
                pe.wait_ge(sem("xn3_ready"), b + 1)
                for t in range(2):
                    i = pe.transpose(ps[:, 0, t * P:t * P + P], xn3[:, t, :], ident[:, :])
                i.then_inc(sem("xn3T_psum"), 1)
                pe.wait_ge(sem("xn3T_ready"), b + 1)
                for t in range(2):
                    mm(ps[:, 1, t * 8:t * 8 + 8], xn3T[:, t * P:t * P + P], ld["rw"][:, :])
                mm(ps[0:AH, 1, 256:512], ld["w1T"][:, :], xn3T[:, :]).then_inc(sem("ah_psum"), 1)
                pe.wait_ge(sem("ah_ready"), b + 1)
                for t in range(2):
                    i = mm(ps[:, 1, 16 + t * MK:16 + t * MK + MK], ah[0:AH + 1, t * P:t * P + P], ld["w2T"][:, :])
                i.then_inc(sem("al_psum"), 1)
                pe.wait_ge(sem("rl_ready"), b + 1)

                def gate_up(n):
                    m = b * E8 * IT + n
                    if n >= 3:
                        pe.wait_ge(sem("av_ready"), m - 2)
                    e, k = n // IT, n % IT
                    for s in range(2):
                        i = mm(ps[0:IP, n % 3, s * 256:s * 256 + 256], ld["guT"][:, e, s, k * IP:k * IP + IP], xn3T[:, :])
                    i.then_inc(sem("gu_psum"), 1)

                def down(e):
                    m = b * E8 + e
                    pe.wait_ge(sem("av_ready"), (m + 1) * IT)
                    if m >= 1:
                        pe.wait_ge(sem("y3_used"), m)
                    for t in range(2):
                        for k in range(IT):
                            i = mm(ps[:, 3, t * D:t * D + D], av[:, (e * IT + k) % 6, t * P:t * P + P],
                                   ld["dn"][:, e * IT + k, :], k == 0, k == IT - 1)
                    i.then_inc(sem("y3_psum"), 1)

                for e in range(E8):
                    for k in range(IT):
                        gate_up(e * IT + k)
                    if e:
                        down(e - 1)
                down(E8 - 1)

            for b in range(B):
                onehots(b)
                mix_experts(b)
                attention(b)
                moe(b)


def constants():
    t, f = np.arange(L)[:, None].astype(np.float64), np.arange(P)[None, :].astype(np.float64)
    w = 2 * np.pi / L
    nyq = np.where(np.arange(L) % 2 == 0, 1.0, -1.0)
    c, s = np.cos(w * ((t * f) % L)), np.sin(w * ((t * f) % L))
    sn, cn = s.copy(), c.copy()
    sn[:, 0], cn[:, 0] = nyq, nyq
    dft = np.stack([c, sn, s, cn], 1)
    ic, is_ = 2 * c.T / L, 2 * s.T / L
    ic[0], is_[0] = 1.0 / L, nyq / L
    ones = np.ones((P, 2 * P))
    ones[:, P:] = 1.0 / (NT * P)
    lrow = np.zeros((1, P))
    lrow[0, 0] = L
    tri = np.tile((np.arange(8)[None, :] < np.arange(8)[:, None])[None], (P, 1, 1))
    r = {
        "dft": dft.reshape(2, P, 4, P).transpose(1, 0, 2, 3), "idft": np.stack([ic, is_], 1),
        "ident": np.eye(P), "ones": ones, "lrow": lrow, "tri": tri,
        "io16": np.tile(16 * np.arange(EH)[None], (P, 1)),
        "io20": np.tile(np.arange(CAND)[None], (P, 1)), "io9": np.tile(np.arange(MK)[None] - 9, (P, 1)),
    }
    return {k: np.ascontiguousarray(v, dtype=np.float32) for k, v in r.items()}


def kernel(**inputs):
    import concourse.bacc as bacc
    from concourse.bass_utils import run_bass_kernel_spmd

    i = {k: np.asarray(v) for k, v in inputs.items()}

    def tiles(x):
        return x.reshape(NT, P, D).transpose(1, 0, 2)

    lay = {
        "x": tiles(i["x"]), "ctx": tiles(i["ctx_1024"]),
        "pos": np.concatenate([i["itok_BxS_0_4095"].reshape(NT, P).T, i["itok_BxS2_1_4095"].reshape(NT, P).T], 1),
        "gates": np.concatenate([i["g_xattn"], i["g_ffn"]])[None],
        "wq0T": i["L0_xattn_Wq"].T, "wkv0T": np.concatenate([i["L0_xattn_Wk"].T, i["L0_xattn_Wv"].T], 1),
        "wo0T": i["L0_xattn_Wo"].T,
        "rows": np.concatenate([i["L0_xattn_bq"], i["L0_xattn_bk"], i["L0_xattn_bv"], i["L0_xattn_bo"],
                                i["L1_xattn_b_q"], i["L1_xattn_b_kv"], i["L1_xattn_b_o"]])[None],
        "w_q": i["L0_ffn_w_q"], "w_qT": i["L0_ffn_w_q"].reshape(D, 16, P).transpose(2, 1, 0),
        "keysT": i["L0_ffn_keys"].transpose(3, 2, 0, 1).reshape(P, 16, NK),
        "gamma": i["L0_ffn_bn_gamma"].reshape(16, P).T, "beta": i["L0_ffn_bn_beta"].reshape(16, P).T,
        "downT": i["L0_ffn_down_embed"].T, "upl": i["L0_ffn_up_embed"].reshape(EH, P, D).transpose(1, 0, 2),
        "Wq1": i["L1_xattn_W_q"], "Wkv1": i["L1_xattn_W_kv"], "Wo1": i["L1_xattn_W_o"],
        "rw": i["L1_ffn_router_w"].T, "w1T": i["L1_ffn_actor_w1"].T, "b1": i["L1_ffn_actor_b1"][:, None],
        "w2T": np.concatenate([i["L1_ffn_actor_w2"].T, i["L1_ffn_actor_b2"][None]], 0),
        "guT": np.stack([i["L1_ffn_gate_w"], i["L1_ffn_up_w"]], 1).transpose(3, 0, 1, 2),
        "dn": i["L1_ffn_down_w"].reshape(E8, D, IT, IP).transpose(3, 0, 2, 1).reshape(IP, E8 * IT, D),
    }
    lay.update(constants())
    nc = bacc.Bacc("TRN2", target_bir_lowering=False, num_devices=1)
    arrays, aps = {}, {}
    for name, x in lay.items():
        x = np.ascontiguousarray(x)
        arrays["in_" + name] = x
        aps[name] = nc.dram_tensor("in_" + name, x.shape, mybir.dt.from_np(x.dtype), kind="ExternalInput").ap()
    out = nc.dram_tensor("out_0", (B, L, D), F32, kind="ExternalOutput").ap()
    program(nc, aps, out)
    r = run_bass_kernel_spmd(nc, [arrays], core_ids=[0])
    return r.results[0]["out_0"]
```

```python
from contextlib import ExitStack

import numpy as np

import concourse.bass as bass
from concourse import mybir

F32 = mybir.dt.float32
BF16 = mybir.dt.bfloat16
F16 = mybir.dt.float16
I32 = mybir.dt.int32
U32 = mybir.dt.uint32
ALU = mybir.AluOpType
ACT = mybir.ActivationFunctionType
AX = mybir.AxisListType.X

P = 128
B, L, D = 4, 256, 128
NT = B * L // P
H, DK = 16, 8
TOP = 5
PH, NK = 8, 32
KT8 = 8
NE = NK * NK
EH = NE // P
CAND = 20
E8, I, IT, IP = 8, 336, 3, 112
AH, MK = 50, 6
EPS = 1e-5
WSCALE = 1024.0
TC, NC = 16, 8
VW = H * (DK + 1) + 24
SL = 8
TWO_PI = 6.283185307179586
C1 = 6.28125
C2 = float(np.float32(TWO_PI - C1))
C3 = float(TWO_PI - C1 - float(np.float32(TWO_PI - C1)))
ROUND = 12582912.0
AHEAD = {
    -1: "gate silu times down gather moe_out",
    0: "turn_q by_query max neg_max score prob value out_turn attend route1 route2",
    1: "look_a look_b look_c look_d soft weight number onehots groups place token weigh mix norms turn_x rope split",
    2: "best where pair",
}
AHEAD = {stage: k for k, stages in AHEAD.items() for stage in stages.split()}
PERIOD = """
look_a0 gate0 look_b0 silu0 gate1 look_c0 look_d0 times0 silu1 times1 turn_q look_a1 soft0 gate2 by_query0 weight0
max0 silu2 by_query1 gate3 silu3 by_query2 times2 gate4 look_b1 look_c1 look_d1 max1 by_query3 down0 max2 silu4 max3
gather0 by_query4 times3 by_query5 times4 max4 gate5 silu5 max5 gate6 by_query6 by_query7 times5 gate7 soft1 down1
silu6 max6 weight1 number max7 silu7 onehots neg_max score0 score1 prob0 prob1 gather1 times6 gate8 score2 value0
prob2 score3 prob3 value1 times7 groups gate9 silu8 place0 times8 value2 score4 place1 prob4 value3 score5 prob5
score6 value4 silu9 token0 weigh0 value5 score7 token1 place2 prob6 down2 weigh1 value6 gather2 prob7 times9 score8
prob8 token2 value7 score9 gate10 place3 prob9 weigh2 score10 value8 token3 silu10 value9 place4 prob10 weigh3 place5
score11 prob11 gate11 silu11 token4 score12 value10 times10 value11 weigh4 score13 prob12 gate12 token5 prob13 times11
value12 silu12 place6 score14 value13 score15 prob14 weigh5 down3 place7 token6 gather3 value14 prob15 times12 value15
weigh6 gate13 gate14 token7 out_turn silu13 weigh7 best0 mix silu14 where0 attend times13 gate15 times14 gate16 silu15
silu16 down4 norms route1 gather4 times15 times16 route2 turn_x gate17 silu17 gate18 times17 rope silu18 pair0 gate19
down5 silu19 gather5 times18 times19 gate20 silu20 gate21 best1 times20 down6 silu21 gather6 times21 gate22 gate23
silu22 times22 silu23 times23 split where1 down7 gather7 pair1 moe_out
"""


def steps():
    for s in range(-1, B + 1):
        for word in PERIOD.split():
            name = word.rstrip("0123456789") if word not in AHEAD else word
            if 0 <= s + AHEAD[name] < B + (name == "norms"):
                yield name, s + AHEAD[name], int(word[len(name):] or 0)


VC, VSN, VS, VCN = range(4)


def program(nc, a, out):
    with ExitStack() as ctx:
        def sb(name, shape, dt=F32):
            return ctx.enter_context(nc.sbuf_tensor(name, shape, dt))

        sems = {}

        def sem(name):
            if name not in sems:
                sems[name] = ctx.enter_context(nc.semaphore(name))
            return sems[name]

        ps = ctx.enter_context(nc.psum_tensor("ps", [P, 8, 512], F32))

        def bank16(n, k=1):
            return ps[:, n:n + k, :].rearrange("p a c -> p (a c)").bitcast(BF16)

        Gb, Xb, HDb = sb("Gb", [P, EH * NT * P]), sb("Xb", [P, 4096]), sb("HDb", [P, EH * 2 * P])
        Sb = sb("Sb", [P, 5888])
        KTb, xnb, ctxTb = sb("KTb", [P, H // 4 * NT * P]), sb("xnb", [P, NT * D]), sb("ctxTb", [P, NT * P])
        taken = {}

        def over(base, shape):
            n, at = int(np.prod(shape[1:])), taken.get(id(base), 0)
            taken[id(base)] = at + n
            w = base[:, at:at + n]
            if len(shape) == 3:
                return w.rearrange("p (a c) -> p a c", a=shape[1])
            if len(shape) == 4:
                return w.rearrange("p (a c d) -> p a c d", a=shape[1], c=shape[2])
            return w

        ld = {}
        for name, ap in a.items():
            shape = list(ap.shape)
            if name == "gates":
                shape = [P, 4]
            if name == "rows":
                shape = [33, shape[1]]
            if name == "dn":
                dnb = sb("dnb", [P, E8 * IT * D])
                ld[name] = dnb[0:IP, :].rearrange("p (a c) -> p a c", a=E8 * IT)
            elif name in ("w_q", "w_qT"):
                ld[name] = over(KTb, shape)
            elif name in ("dft", "idft", "keysT", "ctx", "wkv0T", "wq0T", "wo0T"):
                ld[name] = over(Gb, shape)
            else:
                ld[name] = sb("sb_" + name, shape, ap.dtype)
        ident, ones, cur = ld["ident"], ld["ones"], ld["x"]
        identb = sb("identb", [P, P], BF16)
        tg = sb("tg", [P, 6])

        cf = over(Xb, [P, B, 4 * P])
        ctxT = ctxTb
        kv = over(Sb, [P, 5, B * P])
        KC, KS, KCN, VVC, VVS = range(5)
        qf = over(Xb, [P, 2, B * P])
        tmp = over(Gb, [P, 2048])
        spec = over(Xb, [P, 2, B * P])
        cps = over(Gb, [P, 2, B * H])
        corr = over(Gb, [P, L])
        ew = over(Gb, [P, L])
        sm = sb("sm", [P, 64])
        wcT = over(Gb, [P, 2, B * H])
        wf = over(Gb, [P, 3, B * H])
        aoT = over(Sb, [P, NT * P])

        xn = xnb[:, :].rearrange("p (t d) -> p t d", t=NT)
        xnT = over(dnb, [P, NT * P])
        st = sb("st", [P, NT, 6])
        mv = sb("mv", [P, NT, 2])
        rs = sb("rs", [P, 4, NT])

        xc = over(HDb, [P, NT, D])
        xcT = over(HDb, [P, NT * P])
        cov = over(Gb, [P, D])
        var = sb("var", [P, 4, 16])
        keyS = over(Gb, [P, 16, NK])
        M = over(dnb, [P, 512])
        crow = ld["rows"][32:33, 0:512]
        sim = sb("sim", [P, NT, 512])
        top = sb("top", [P, 2, 16, 8])
        tix = sb("tix", [P, 2, 16, 8], U32)
        tixf = sb("tixf", [P, 2, 16, 8])
        cand = sb("cand", [P, 2, PH, CAND])
        candi = sb("candi", [P, 2, PH, CAND])
        sc = sb("sc", [P, 2, PH, 8])
        pk = sb("pk", [P, 2, PH, 8], U32)
        pkf = sb("pkf", [P, PH * 8])
        hot = sb("hot", [P, PH * 8, CAND], F16)
        dd = sb("dd", [P, 2, PH, 8])
        zz = sb("zz", [P, 2, PH])
        ex_ = sb("ex_", [P, 2, PH, 8])
        wts = sb("wts", [P, 2, 2, 64])
        eid = sb("eid", [P, 2, 2, 64])
        eidi = sb("eidi", [P, 3, P], I32)
        elh = sb("elh", [P, 2, P])
        elT = sb("elT", [P, 2, P], F16)
        whl = sb("whl", [P, 2, P], F16)
        iox = sb("iox", [P, 16, TC], F16)
        elS = sb("elS", [P, EH, P], F16)
        X = Xb[:, 0:P * TC].bitcast(F16).rearrange("p (b e t) -> p b e t", b=2, e=P)
        Yq = Xb[:, 2304:2816].bitcast(F16).rearrange("p (e t) -> p e t", e=EH)
        Y = sb("Y", [P, EH, 2, P], F16)
        W = Xb[:, 2048:2048 + 2 * TC * EH].rearrange("p (s c) -> p s c", s=2)
        G = Gb[:, :].rearrange("p (e t) -> p e t", e=EH)
        HD = HDb[:, :].rearrange("p (e t) -> p e t", e=EH)

        cs = sb("cs", [P, 2, 2 * NT, 4])
        ang = sb("ang", [P, 3, 2 * NT * 4])
        posf = sb("posf", [P, 2 * NT])
        qs = Sb[:, 3072:4096].bitcast(BF16).rearrange("p (h s d) -> p h s d", s=SL, d=DK)
        KT = KTb[:, :].bitcast(BF16).rearrange("p (j t) -> p j t", j=H // 2)
        QT = Sb[:, 4096:5120].bitcast(BF16).rearrange("p (j t) -> p j t", j=H // 2)
        oT = Sb[:, 4096:5120].rearrange("p (g t) -> p g t", g=4)
        V = sb("V", [P, NT, VW])
        ra = Sb[:, 5120:5376].rearrange("p (t d) -> p t d", t=2)
        rb = Sb[:, 5376:5632].rearrange("p (t d) -> p t d", t=2)
        rq = Sb[:, 5632:5888].rearrange("p (t d) -> p t d", t=2)
        mx = sb("mx", [P, 2, H])
        mrep = sb("mrep", [P, 2, P], BF16)
        mT = sb("mT", [P, 2 * P], BF16)
        PE_ = Sb[:, 0:1024].rearrange("p (a k c) -> p a k c", a=2, k=2)
        rcp = sb("rcp", [P, 2 * H])
        att = xnb[:, 256:512].rearrange("p (t d) -> p t d", t=2)
        attT = ctxTb[:, 0:256]
        xn2 = xnb[:, 0:256].rearrange("p (t d) -> p t d", t=2)
        xn2T = ctxTb[:, 256:512]

        xn3 = xnb[:, 512:768].rearrange("p (t d) -> p t d", t=2)
        xn3T = [ctxTb[:, 512:768], Xb[:, 3584:3840]]
        score = sb("score", [P, 2, 16])
        ah = sb("ah", [64, 2 * P])
        rt = sb("rt", [P, 8, 16])
        cmp = ctxTb[:, 768:1024].rearrange("p (a t e f) -> p a t e f", a=2, t=2, e=8)
        sg = [Xb[0:IP, 2816 + 256 * k:3072 + 256 * k] for k in range(3)]
        up = [Sb[0:IP, 1024:1280], Sb[0:IP, 1280:1536], Xb[0:IP, 3840:4096]]
        av = Sb[0:IP, 1536:3072].rearrange("p (a c) -> p a c", a=6)
        macc = xnb[:, 768:1024].rearrange("p (t d) -> p t d", t=2)

        assert all(v <= n for v, n in ((taken[id(Gb)], EH * NT * P), (taken[id(Xb)], 4096), (taken[id(Sb)], 5888)))

        block = ctx.enter_context(nc.Block())

        groups = [
            ["ctx", "dft"], ["x", "wkv0T", "wq0T", "rows", "ident", "ones", "lrow"],
            ["idft", "wo0T", "gates", "gamma", "beta", "pos", "io20", "tri", "io9", "io16"],
            ["w_q", "w_qT", "keysT", "downT"],
            ["upl", "Wq1", "Wkv1", "Wo1"],
            ["rw", "w1T", "b1", "w2T", "guT", "dn"],
        ]

        def loaded(eng, g):
            eng.wait_ge(sem(f"load{g}"), 16 * len(groups[g]))

        @block.sync
        def _(sp):
            for g, names in enumerate(groups):
                for n in names:
                    if n == "dn":
                        sp.wait_ge(sem("G_psum"), 2 * EH)
                    src = a[n]
                    if n == "gates":
                        src = src.broadcast_to([P, 4])
                    idx = (slice(None),) * len(ld[n].shape)
                    dst = ld[n][0:1, :] if n == "rows" else ld[n][idx]
                    sp.dma_start(dst, src[idx]).then_inc(sem(f"load{g}"), 16)
            for t in range(NT):
                if t % 2 == 0:
                    sp.wait_ge(sem("x4_ready"), t // 2 + 1)
                sp.dma_start(out.rearrange("b (j p) d -> (b j) p d", p=P)[t], cur[:, t, :]).then_inc(sem("stored"), 16)
            sp.wait_ge(sem("stored"), 16 * NT)

        @block.gpsimd
        def _(g):
            g.iota(iox[:, :, :], pattern=[[1, 16], [0, TC]], base=0, channel_multiplier=0,
                   allow_small_or_imprecise_dtypes=True).then_inc(sem("iox_ready"), 1)

            n = [0]

            def link(ins):
                ins.then_inc(sem("pool_chain"), 1)
                n[0] += 1
                g.wait_ge(sem("pool_chain"), n[0])

            loaded(g, 2)
            def look_a(b, q):
                t = 2 * b + q
                g.wait_ge(sem("tix_ready"), t + 1)
                g.tensor_scalar(tixf[:, q, 0:8, :], tix[:, q, 0:8, :], float(NK), None, ALU.mult)
                link(g.tensor_copy(tixf[:, q, 8:16, :], tix[:, q, 8:16, :]))
                xi, yi = tixf[:, q, 0:8, :], tixf[:, q, 8:16, :]
                g.tensor_tensor(candi[:, q, :, 0:8], yi, xi[:, :, 0:1].broadcast_to([P, PH, 8]), ALU.add)
                g.tensor_tensor(candi[:, q, :, 8:12], yi[:, :, 0:4], xi[:, :, 1:2].broadcast_to([P, PH, 4]), ALU.add)
                g.tensor_tensor(candi[:, q, :, 12:16].rearrange("p h (a b) -> p h a b", a=2),
                                yi[:, :, 0:2].unsqueeze(2).broadcast_to([P, PH, 2, 2]),
                                xi[:, :, 2:4].unsqueeze(3).broadcast_to([P, PH, 2, 2]), ALU.add)
                link(g.tensor_tensor(candi[:, q, :, 16:20], xi[:, :, 4:8], yi[:, :, 0:1].broadcast_to([P, PH, 4]), ALU.add))
                g.wait_ge(sem("pk_ready"), t + 1)
                link(g.tensor_copy(pkf[:, :], pk[:, q, :, :].rearrange("p h k -> p (h k)")))

            def look_b(b, q):
                if b + q >= 1:
                    g.wait_ge(sem("hot_used"), 2 * b + q)
                link(g.tensor_tensor(hot[:, :, :], pkf[:, :].unsqueeze(2).broadcast_to([P, 64, CAND]),
                                     ld["io20"][:, :].unsqueeze(1).broadcast_to([P, 64, CAND]), ALU.subtract))

            def look_c(b, q):
                link(g.tensor_scalar(hot[:, :, :], hot[:, :, :], 0.0, None, ALU.is_equal))

            def look_d(b, q):
                h4 = hot[:, :, :].rearrange("p (h k) c -> p h k c", h=PH)
                g.tensor_tensor(h4, h4, candi[:, q, :, :].unsqueeze(2).broadcast_to([P, PH, 8, CAND]),
                                ALU.mult).then_inc(sem("hot_ready"), 1)

            def times(b, n):
                m = b * E8 * IT + n
                g.wait_ge(sem("gate_ready"), m + 1)
                g.wait_ge(sem("up_ready"), m + 1)
                if m >= 6:
                    g.wait_ge(sem("y3_psum"), (m - 6) // IT + 1)
                g.tensor_tensor(av[:, m % 6, :], sg[m % 3], up[m % 3], ALU.mult).then_inc(sem("av_ready"), 1)

            stages = {"look_a": look_a, "look_b": look_b, "look_c": look_c, "look_d": look_d, "times": times}
            for name, b, k in steps():
                if name in stages:
                    stages[name](b, k)

        @block.scalar
        def _(act):
            def copy(dst, src, s, scale=1.0):
                act.activation(dst, src, ACT.Copy, scale=scale).then_inc(sem(s), 1)

            loaded(act, 1)
            act.activation(identb[:, :], ident[:, :], ACT.Copy).then_inc(sem("identb_ready"), 1)
            loaded(act, 2)
            act.activation(tg[:, 0:4], ld["gates"][:, :], ACT.Tanh).then_inc(sem("tg_ready"), 1)
            for b in range(B):
                act.wait_ge(sem("cf_psum"), b + 1)
                copy(cf[:, b, :], ps[:, b, :], "cf_ready")
            for k in range(2):
                act.wait_ge(sem("ctxT_psum"), k + 1)
                copy(ctxT[:, 512 * k:512 * k + 512], ps[:, 4 + k, :], "ctxT_ready")
            act.wait_ge(sem("kv_psum"), 1)
            copy(kv[:, 0:4, :], ps[:, 0:4, :], "kv_ready")
            copy(kv[:, 4, :], ps[:, 6, :], "kv_ready")
            act.wait_ge(sem("ang_ready"), 1)
            act.activation(cs[:, :, :, :].rearrange("p a t f -> p (a t f)"),
                           ang[:, 0:2, :].rearrange("p a t -> p (a t)"), ACT.Sin).then_inc(sem("cs_ready"), 1)
            act.wait_ge(sem("xnf_psum"), 1)
            copy(cf[:, 0:2, :], ps[:, 4:6, :], "xnf_ready")
            act.wait_ge(sem("corr_psum"), 1)
            copy(corr[0:64, :], ps[0:64, 0, 0:L], "corr_ready", 1.0 / DK)
            act.wait_ge(sem("corr_max"), 1)
            act.activation(ew[0:64, :], corr[0:64, :], ACT.Exp, bias=sm[0:64, 8:9]).then_inc(sem("ew_ready"), 1)
            act.wait_ge(sem("wcT_psum"), 1)
            copy(wcT[:, :, :].rearrange("p a c -> p (a c)"), ps[:, 1, 0:128], "wcT_ready")
            act.wait_ge(sem("wf_psum"), 1)
            copy(wf[:, :, :].rearrange("p a c -> p (a c)"), ps[:, 2, 0:192], "wf_ready")
            act.wait_ge(sem("ao_psum"), 1)
            copy(aoT[:, :], ps[:, 4:6, :].rearrange("p a c -> p (a c)"), "ao_ready")
            act.wait_ge(sem("xn1T_psum"), 1)
            copy(xnT[:, :], ps[:, 0:2, :].rearrange("p a c -> p (a c)"), "xn1T_ready")
            act.wait_ge(sem("xcT_psum"), 1)
            copy(xcT[:, :], ps[:, 2:4, :].rearrange("p a c -> p (a c)"), "xcT_ready")
            act.wait_ge(sem("cov_psum"), 1)
            copy(cov[:, :], ps[:, 7, 128:256], "cov_ready", 1.0 / (NT * P))
            act.wait_ge(sem("M_psum"), 1)
            copy(M[:, :], ps[:, 4, :], "M_ready")
            copy(crow, ps[32:33, 5, :], "M_ready")
            for t in range(NT):
                act.wait_ge(sem("sim_psum"), t + 1)
                copy(sim[:, t, :], ps[:, t % 4, :], "sim_ready")
            for n in range(2 * EH):
                act.wait_ge(sem("G_psum"), n + 1)
                act.activation(G[:, n // 2, 512 * (n % 2):512 * (n % 2) + 512], ps[:, 4 + n % 4, :],
                               ACT.Gelu_apprx_tanh).then_inc(sem("G_ready"), 1)
            for t in range(NT):
                act.wait_ge(sem("v_psum"), t + 1)
                act.wait_ge(sem("ks_ready"), t + 1)
                act.activation(V[:, t, 0:9 * H].rearrange("p (h d) -> p h d", h=H)[:, :, 0:DK], ps[:, 6 + t % 2, 128:256].rearrange("p (h d) -> p h d", h=H),
                               ACT.Copy).then_inc(sem("v_ready"), 1)
                act.wait_ge(sem("kt_psum"), t + 1)
                act.activation(KT[:, :, t * P:t * P + P], bank16(4 + t % 2).rearrange("p (j c) -> p j c", j=8),
                               ACT.Copy).then_inc(sem("kt_ready"), 1)

            def soft(b, q):
                act.wait_ge(sem("dd_ready"), 2 * b + q + 1)
                act.activation(ex_[:, q, :, :], dd[:, q, :, :], ACT.Exp).then_inc(sem("ex_ready"), 1)

            def onehots(b, _):
                act.wait_ge(sem("eT_psum"), b + 1)
                copy(elT[:, :, :].rearrange("p a c -> p (a c)"), ps[:, 3, 0:256], "elT_ready")
                copy(whl[:, 0, :], ps[:, 3, 256:384], "whi_ready", WSCALE)

            def turn_x(b, _):
                act.wait_ge(sem("xn2T_psum"), b + 1)
                copy(xn2T[:, :], ps[:, 4, 0:256], "xn2T_ready")

            def turn_q(b, _):
                act.wait_ge(sem("qT_psum"), b + 1)
                for k in range(2):
                    act.activation(QT[:, 4 * k:4 * k + 4, :].rearrange("p j c -> p (j c)"), bank16(6 + k),
                                   ACT.Copy).then_inc(sem("QT_ready"), 1)

            def neg_max(b, _):
                act.wait_ge(sem("mT_psum"), b + 1)
                act.activation(mT[:, :], bank16(4)[:, 0:256], ACT.Copy).then_inc(sem("mT_ready"), 1)

            def prob(b, h):
                n = b * H + h
                act.wait_ge(sem("s2_psum"), n + 1)
                if n >= 2:
                    act.wait_ge(sem("av_done"), n - 1)
                act.activation(PE_[:, h % 2, :, :].rearrange("p a c -> p (a c)"), ps[:, 4 + (h + 1) % 2, :], ACT.Exp,
                               scale=float(1.0 / np.sqrt(DK))).then_inc(sem("p_ready"), 1)

            def out_turn(b, _):
                act.wait_ge(sem("av_done"), H * (b + 1))
                copy(oT[:, :, :].rearrange("p (a g) c -> p a (g c)", a=2), ps[:, 6:8, :], "oT_ready")

            def attend(b, _):
                act.wait_ge(sem("attT_psum"), b + 1)
                copy(attT[:, :], ps[:, 6, 0:256], "attT_ready")

            def route1(b, _):
                act.wait_ge(sem("xn3T_psum"), b + 1)
                copy(xn3T[b % 2], ps[:, 6, 0:256], "xn3T_ready")
                act.wait_ge(sem("ah_psum"), b + 1)
                act.activation(ah[0:AH, :], ps[0:AH, 7, 0:256], ACT.Gelu_apprx_tanh,
                               bias=ld["b1"][:, 0:1]).then_inc(sem("ah_ready"), 1)

            def route2(b, _):
                act.wait_ge(sem("rl_ready"), b + 1)
                act.activation(rt[:, 1, :], rt[:, 0, :], ACT.Exp).then_inc(sem("rexp_ready"), 1)

            def silu(b, n):
                m = b * E8 * IT + n
                act.wait_ge(sem("gu_psum"), m + 1)
                if m >= 3:
                    act.wait_ge(sem("av_ready"), m - 2)
                act.activation(sg[m % 3], ps[0:IP, m % 2, 0:256], ACT.Tanh, scale=0.5)
                copy(up[m % 3], ps[0:IP, m % 2, 256:512], "up_ready")

            stages = {"soft": soft, "onehots": onehots, "turn_x": turn_x, "turn_q": turn_q, "neg_max": neg_max,
                      "prob": prob, "out_turn": out_turn, "attend": attend, "route1": route1, "route2": route2,
                      "silu": silu}
            for name, b, k in steps():
                if name in stages:
                    stages[name](b, k)

        @block.vector
        def _(v):
            n = [0]

            def link(ins):
                ins.then_inc(sem("dve_chain"), 1)
                n[0] += 1
                v.wait_ge(sem("dve_chain"), n[0])

            def layer_norm(dst, src, k, signal):
                for t in range(k):
                    i = v.bn_stats(st[:, t, :], src[:, t, :])
                link(i)
                for t in range(k):
                    i = v.bn_aggr(mv[:, t, :], st[:, t, :])
                link(i)
                rsqrt(rs, mv[:, 0:k, 1], k)
                for t in range(k):
                    i = v.tensor_scalar(dst[:, t, :], src[:, t, :], mv[:, t, 0:1], rs[:, 1, t:t + 1],
                                        ALU.subtract, ALU.mult)
                i.then_inc(sem(signal), 1)

            def norm_tiles(tiles):
                k = len(tiles)
                for t, (x, _, _) in enumerate(tiles):
                    i = v.bn_stats(st[:, t, :], x)
                link(i)
                for t in range(k):
                    i = v.bn_aggr(mv[:, t, :], st[:, t, :])
                link(i)
                x, y, u = rs[:, 0, 0:k], rs[:, 1, 0:k], rs[:, 2, 0:k]
                link(v.tensor_scalar(x, mv[:, 0:k, 1], EPS, None, ALU.add))
                link(v.tensor_scalar(u.bitcast(I32), x.bitcast(I32), 1, None, ALU.logical_shift_right))
                v.tensor_scalar(x, x, -0.5, None, ALU.mult)
                link(v.tensor_scalar(y.bitcast(I32), u.bitcast(I32), -1.0, float(0x5f3759df), ALU.mult, ALU.add))
                for _ in range(3):
                    for t in range(k):
                        i = v.scalar_tensor_tensor(u[:, t:t + 1], y[:, t:t + 1], x[:, t:t + 1], y[:, t:t + 1],
                                                   ALU.mult, ALU.mult)
                    link(i)
                    link(v.scalar_tensor_tensor(y, u, 1.5, y, ALU.add, ALU.mult))
                for t, (src, dst, signal) in enumerate(tiles):
                    i = v.tensor_scalar(dst, src, mv[:, t, 0:1], rs[:, 1, t:t + 1], ALU.subtract, ALU.mult)
                    if t % 2:
                        i.then_inc(sem(signal), 1)

            def rsqrt(w, src, k):
                x, y, u = w[:, 0, 0:k], w[:, 1, 0:k], w[:, 2, 0:k]
                link(v.tensor_scalar(x, src, EPS, None, ALU.add))
                link(v.tensor_scalar(u.bitcast(I32), x.bitcast(I32), 1, None, ALU.logical_shift_right))
                link(v.tensor_scalar(y.bitcast(I32), u.bitcast(I32), -1.0, float(0x5f3759df), ALU.mult, ALU.add))
                for _ in range(3):
                    link(v.scalar_tensor_tensor(u, y, -0.5, y, ALU.mult, ALU.mult))
                    link(v.tensor_tensor(u, u, x, ALU.mult))
                    link(v.scalar_tensor_tensor(y, u, 1.5, y, ALU.add, ALU.mult))

            v.memset(V[:, :, :], 1.0)
            v.memset(ah[:, :], 1.0)
            v.memset(mrep[:, :, :], 0.0).then_inc(sem("consts"), 1)
            v.wait_ge(sem("consts"), 1)
            loaded(v, 1)
            loaded(v, 2)
            link(v.tensor_copy(posf[:, :], ld["pos"][:, :]))
            A0, A1, A2 = ang[:, 0, :], ang[:, 1, :], ang[:, 2, :]
            inv = [float(x) for x in (np.float32(1.0) / np.float32(10000.0) ** (np.arange(0, DK, 2, dtype=np.float32) / np.float32(DK)))]
            for f in range(4):
                i = v.tensor_scalar(A2.rearrange("p (t f) -> p t f", f=4)[:, :, f], posf[:, :], inv[f], None, ALU.mult)
            link(i)
            for dst, turn, shift in ((A0, 0.25, TWO_PI / 4), (A1, 0.0, 0.0)):
                k = sm[:, :]
                link(v.tensor_scalar(k, A2, 1.0 / TWO_PI, turn, ALU.mult, ALU.add))
                link(v.tensor_scalar(k, k, ROUND, None, ALU.add))
                link(v.tensor_scalar(k, k, ROUND, None, ALU.subtract))
                link(v.scalar_tensor_tensor(dst, k, -C1, A2, ALU.mult, ALU.add))
                link(v.scalar_tensor_tensor(dst, k, -C2, dst, ALU.mult, ALU.add))
                link(v.scalar_tensor_tensor(dst, k, -C3, dst, ALU.mult, ALU.add))
                link(v.tensor_scalar(dst, dst, shift, None, ALU.add))
                i = v.tensor_scalar(dst, dst, 3.1415925, -3.1415925, ALU.min, ALU.max)
                if turn:
                    link(i)
            i.then_inc(sem("ang_ready"), 1)

            layer_norm(xn, cur, NT, "xn0_ready")
            v.wait_ge(sem("q_psum"), 1)
            link(v.tensor_copy(qf[:, :, :], ps[:, 2:4, :]))
            v.wait_ge(sem("kv_ready"), 2)
            t0, t1 = tmp[:, 0:512], tmp[:, 512:1024]

            def cross(dst, x0, y0, x1, y1, op, last=None):
                v.tensor_tensor(t0, x0, y0, ALU.mult)
                link(v.tensor_tensor(t1, x1, y1, ALU.mult))
                i = v.tensor_tensor(dst, t0, t1, op)
                if last:
                    i.then_inc(sem(last), 1)
                else:
                    link(i)

            cross(spec[:, 0, :], qf[:, 0, :], kv[:, KC, :], qf[:, 1, :], kv[:, KS, :], ALU.add)
            cross(spec[:, 1, :], qf[:, 1, :], kv[:, KCN, :], qf[:, 0, :], kv[:, KS, :], ALU.subtract)
            v.tensor_reduce(cps[:, :, :].rearrange("p a c -> p (a c)"),
                            spec[:, :, :].rearrange("p a (c d) -> p (a c) d", d=DK), AX, ALU.add).then_inc(sem("cps_ready"), 1)
            v.wait_ge(sem("corr_ready"), 1)
            link(v.max(sm[0:64, 0:8], corr[0:64, :]))
            v.tensor_scalar(sm[0:64, 8:9], sm[0:64, 0:1], -1.0, None, ALU.mult).then_inc(sem("corr_max"), 1)
            v.wait_ge(sem("ew_ready"), 1)
            link(v.scalar_tensor_tensor(ew[0:64, :], corr[0:64, :], sm[0:64, TOP - 1:TOP], ew[0:64, :], ALU.is_ge, ALU.mult))
            link(v.tensor_reduce(sm[0:64, 9:10], ew[0:64, :], AX, ALU.add))
            link(v.reciprocal(sm[0:64, 10:11], sm[0:64, 9:10]))
            v.tensor_scalar(ew[0:64, :], ew[0:64, :], sm[0:64, 10:11], None, ALU.mult).then_inc(sem("wc_ready"), 1)
            v.wait_ge(sem("wf_ready"), 1)

            def spread(k):
                return wf[:, k, :].unsqueeze(2).broadcast_to([P, B * H, DK])

            def wide(x):
                return x.rearrange("p (c d) -> p c d", d=DK)

            t0, t1 = wide(tmp[:, 0:512]), wide(tmp[:, 512:1024])
            vc, vs = wide(kv[:, VVC, :]), wide(kv[:, VVS, :])
            cross(wide(spec[:, 0, :]), vc, spread(0), vs, spread(1), ALU.subtract)
            cross(wide(spec[:, 1, :]), vc, spread(1), vs, spread(2), ALU.add, "of_ready")
            v.wait_ge(sem("tg_ready"), 1)
            v.tensor_scalar(tg[:, 5:6], tg[:, 3:4], 0.5, None, ALU.mult)
            link(v.tensor_scalar(tg[:, 4:5], tg[:, 2:3], 1.0 / WSCALE, None, ALU.mult))
            v.wait_ge(sem("y0_psum"), 1)
            link(v.scalar_tensor_tensor(cur[:, :, :], ps[:, 6:8, :].rearrange("p a (t d) -> p (a t) d", t=4), tg[:, 0:1],
                                        cur[:, :, :], ALU.mult, ALU.add))

            layer_norm(xn, cur, NT, "xn1_ready")
            v.wait_ge(sem("xn1_ready"), 1)
            v.wait_ge(sem("mean_psum"), 1)
            v.tensor_tensor(xc[:, :, :], xn[:, :, :], ps[:, 7, 0:128].unsqueeze(1).broadcast_to([P, NT, D]),
                            ALU.subtract).then_inc(sem("xc_ready"), 1)
            v.wait_ge(sem("cw_psum"), 1)
            loaded(v, 3)
            link(v.tensor_tensor(tmp[:, :], ps[:, 0:4, :].rearrange("p a c -> p (a c)"),
                                 ld["w_qT"][:, :, :].rearrange("p a c -> p (a c)"), ALU.mult))
            link(v.tensor_reduce(var[:, 3, :], tmp[:, :].rearrange("p (c d) -> p c d", d=D), AX, ALU.add))
            rsqrt(var, var[:, 3, :], 16)
            link(v.tensor_tensor(var[:, 1, :], var[:, 1, :], ld["gamma"][:, :], ALU.mult))
            v.tensor_tensor(keyS[:, :, :], ld["keysT"][:, :, :], var[:, 1, :].unsqueeze(2).broadcast_to([P, 16, NK]),
                            ALU.mult).then_inc(sem("keyS_ready"), 1)

            def best(b, q):
                t = 2 * b + q
                v.wait_ge(sem("sim_ready"), t + 1)
                if t >= 2:
                    v.wait_ge(sem("hot_ready"), t - 1)
                s3 = sim[:, t, :].rearrange("p (g k) -> p g k", k=NK)
                for g in range(16):
                    i = v.max(top[:, q, g, :], s3[:, g, :])
                link(i)

            def where(b, q):
                s3 = sim[:, 2 * b + q, :].rearrange("p (g k) -> p g k", k=NK)
                for g in range(16):
                    i = v.max_index(tix[:, q, g, :], top[:, q, g, :], s3[:, g, :])
                i.then_inc(sem("tix_ready"), 1)

            def pair(b, q):
                xs, ys = top[:, q, 0:8, :], top[:, q, 8:16, :]
                v.tensor_tensor(cand[:, q, :, 0:8], ys, xs[:, :, 0:1].broadcast_to([P, PH, 8]), ALU.add)
                v.tensor_tensor(cand[:, q, :, 8:12], ys[:, :, 0:4], xs[:, :, 1:2].broadcast_to([P, PH, 4]), ALU.add)
                v.tensor_tensor(cand[:, q, :, 12:16].rearrange("p h (a b) -> p h a b", a=2),
                                ys[:, :, 0:2].unsqueeze(2).broadcast_to([P, PH, 2, 2]),
                                xs[:, :, 2:4].unsqueeze(3).broadcast_to([P, PH, 2, 2]), ALU.add)
                link(v.tensor_tensor(cand[:, q, :, 16:20], xs[:, :, 4:8], ys[:, :, 0:1].broadcast_to([P, PH, 4]), ALU.add))
                for h in range(PH):
                    i = v.max(sc[:, q, h, :], cand[:, q, h, :])
                link(i)
                for h in range(PH):
                    i = v.max_index(pk[:, q, h, :], sc[:, q, h, :], cand[:, q, h, :])
                i.then_inc(sem("pk_ready"), 1)
                v.tensor_tensor(dd[:, q, :, :], sc[:, q, :, :], sc[:, q, :, 0:1].broadcast_to([P, PH, 8]),
                                ALU.subtract).then_inc(sem("dd_ready"), 1)

            def weight(b, q):
                t = 2 * b + q
                v.wait_ge(sem("ex_ready"), t + 1)
                if b >= 2:
                    v.wait_ge(sem("eT_psum"), b - 1)
                link(v.tensor_reduce(zz[:, q, :], ex_[:, q, :, :], AX, ALU.add))
                link(v.reciprocal(zz[:, q, :], zz[:, q, :]))
                v.tensor_tensor(wts[:, b % 2, q, :].rearrange("p (h k) -> p h k", h=PH), ex_[:, q, :, :],
                                zz[:, q, :].unsqueeze(2).broadcast_to([P, PH, 8]), ALU.mult)
                v.wait_ge(sem("hot_ready"), t + 1)
                v.tensor_reduce(eid[:, b % 2, q, :], hot[:, :, :], AX, ALU.add).then_inc(sem("hot_used"), 1)

            def number(b, _):
                v.wait_ge(sem("hot_used"), 2 * b + 2)
                e = eid[:, b % 2, :, :].rearrange("p a c -> p (a c)")
                link(v.tensor_copy(eidi[:, 0, :], e))
                v.tensor_scalar(eidi[:, 1, :], eidi[:, 0, :], P - 1, None, ALU.bitwise_and)
                link(v.tensor_scalar(eidi[:, 2, :], eidi[:, 0, :], 7, None, ALU.logical_shift_right))
                if b >= 1:
                    v.wait_ge(sem("eT_psum"), b)
                v.tensor_copy(elh[:, :, :], eidi[:, 1:3, :]).then_inc(sem("elh_ready"), 1)

            def groups(b, _):
                v.wait_ge(sem("whi_ready"), b + 1)
                v.scalar_tensor_tensor(whl[:, 1, :], ps[:, 3, 256:384], WSCALE, whl[:, 0, :],
                                       ALU.mult, ALU.subtract).then_inc(sem("wlo_ready"), 1)
                v.wait_ge(sem("iox_ready"), 1)
                v.tensor_tensor(Yq[:, :, :].rearrange("p e (c t) -> p e c t", t=TC),
                                elT[:, 1, :].rearrange("p (c t) -> p c t", t=TC).unsqueeze(1).broadcast_to([P, EH, NC, TC]),
                                iox[:, 0:EH, :].unsqueeze(2).broadcast_to([P, EH, NC, TC]), ALU.is_equal)
                link(v.tensor_tensor(elS[:, :, :], elT[:, 0, :].unsqueeze(1).broadcast_to([P, EH, P]),
                                     ld["io16"][:, :].unsqueeze(2).broadcast_to([P, EH, P]), ALU.subtract))
                v.wait_ge(sem("wlo_ready"), b + 1)
                if b >= 1:
                    v.wait_ge(sem("W_psum"), NC * b)
                for k in range(2):
                    v.tensor_tensor(Y[:, :, k, :], Yq[:, :, :], whl[:, k, :].unsqueeze(1).broadcast_to([P, EH, P]), ALU.mult)

            def place(b, c):
                m = b * NC + c
                if m >= 2:
                    v.wait_ge(sem("W_psum"), m - 1)
                v.tensor_tensor(X[:, c % 2, :, :].rearrange("p (c e) t -> p c e t", c=EH),
                                elS[:, :, c * TC:c * TC + TC].unsqueeze(2).broadcast_to([P, EH, 16, TC]),
                                iox[:, :, :].unsqueeze(1).broadcast_to([P, EH, 16, TC]), ALU.is_equal)\
                    .then_inc(sem("X_ready"), 1)

            def weigh(b, c):
                m = b * NC + c
                v.wait_ge(sem("W_psum"), m + 1)
                if m == 0:
                    v.wait_ge(sem("G_ready"), 2 * EH)
                else:
                    v.wait_ge(sem("HD_ready"), m)
                v.tensor_reduce(W[:, :, :].rearrange("p s c -> p (s c)"),
                                ps[:, 3, :].rearrange("p (c a) -> p c a", a=2), AX, ALU.add).then_inc(sem("W_taken"), 1)
                v.wait_ge(sem("W_taken"), m + 1)
                v.tensor_tensor(
                    HD.rearrange("p e (s t) -> p s t e", s=2)[:, :, c * TC:c * TC + TC, :],
                    W[:, :, :].rearrange("p s (t e) -> p s t e", e=EH),
                    G[:, :, b * L:b * L + L].rearrange("p e (s t) -> p s t e", s=2)[:, :, c * TC:c * TC + TC, :],
                    ALU.mult).then_inc(sem("HD_ready"), 1)

            def norms(b, _):
                work = []
                if b < B:
                    v.wait_ge(sem("y1_psum"), b + 1)
                    if b >= 1:
                        v.wait_ge(sem("xn2T_psum"), b)
                    work.append((ps[:, 3, 0:256], tg[:, 4:5], cur[:, 2 * b:2 * b + 2, :], xn2, "xn2_ready"))
                if b >= 1:
                    v.wait_ge(sem("y2_psum"), b)
                    work.append((ps[:, 7, 0:256], tg[:, 1:2], cur[:, 2 * b - 2:2 * b, :], xn3, "xn3_ready"))
                for y, w, x, _, _ in work:
                    i = v.scalar_tensor_tensor(x, y.rearrange("p (t d) -> p t d", t=2), w, x, ALU.mult, ALU.add)
                link(i)
                tiles = [(x[:, t, :], dst[:, t, :], signal) for _, _, x, dst, signal in work for t in range(2)]
                norm_tiles(tiles)

            def rotate(src, k, c0):
                for t in range(k):
                    s = src[t].rearrange("p (h a d) -> p h a d", h=H, a=2)
                    cc = cs[:, 0, c0 + t, :].unsqueeze(1).unsqueeze(1).broadcast_to([P, H, 2, 4])
                    ss = cs[:, 1, c0 + t, :].unsqueeze(1).unsqueeze(1).broadcast_to([P, H, 2, 4])
                    v.tensor_tensor(ra[:, t, :].rearrange("p (h a d) -> p h a d", h=H, a=2), s, cc, ALU.mult)
                    link(v.tensor_tensor(rb[:, t, :].rearrange("p (h a d) -> p h a d", h=H, a=2), s, ss, ALU.mult))
                r3 = [w[:, 0:k, :].rearrange("p t (h a d) -> p (t h) a d", h=H, a=2) for w in (rq, ra, rb)]
                v.tensor_tensor(r3[0][:, :, 0, :], r3[1][:, :, 0, :], r3[2][:, :, 1, :], ALU.subtract)
                link(v.tensor_tensor(r3[0][:, :, 1, :], r3[1][:, :, 1, :], r3[2][:, :, 0, :], ALU.add))

            def parts(k, keys, signal):
                r = rq[:, 0:k, :].rearrange("p t (h d) -> p (t h) d", h=H)
                s = qs[:, 0:k * H, :, :]
                slots = [s[:, :, 0:7:3, :], s[:, :, 1:8:3, :], s[:, :, 2:6:3, :]] if keys else \
                    [s[:, :, 0:3, :], s[:, :, 3:6, :], s[:, :, 6:8, :]]
                for p, z in enumerate(slots):
                    w = z.shape[2]
                    i = v.tensor_copy(z, r.unsqueeze(2).broadcast_to([P, k * H, w, DK]))
                    if p == 2:
                        i.then_inc(sem(signal), 1)
                    else:
                        link(i)
                        link(v.tensor_tensor(r, r, z[:, :, 0, :], ALU.subtract))

            def ctx_keys(t):
                v.wait_ge(sem("v_psum"), t + 1)
                if t == 0:
                    v.wait_ge(sem("cs_ready"), 1)
                rotate([ps[:, 6 + t % 2, 0:128]], 1, NT + t)
                if t >= 1:
                    v.wait_ge(sem("kt_psum"), t)
                parts(1, True, "ks_ready")

            def rope(b, _):
                v.wait_ge(sem("q1_psum"), b + 1)
                rotate([ps[:, 4, 256:384], ps[:, 4, 384:512]], 2, 2 * b)

            def split(b, _):
                parts(2, False, "qs_ready")

            def max_(b, g):
                v.wait_ge(sem("s1_psum"), b * 8 + g + 1)
                qt, gg = g // 4, g % 4
                bk = 4 + 2 * (g % 2)
                v.tensor_reduce(mx[:, qt, 4 * gg:4 * gg + 4],
                                ps[:, bk:bk + 2, :].rearrange("p e (j k) -> p (e j) k", j=2), AX, ALU.max)\
                    .then_inc(sem("mx_ready"), 1)

            def neg_max(b, _):
                v.wait_ge(sem("mx_ready"), b * 8 + 8)
                v.tensor_scalar(mrep[:, :, 0:H], mx[:, :, :], -1.0, None, ALU.mult)
                v.tensor_scalar(mrep[:, :, 64:64 + H], mx[:, :, :], -1.0, None, ALU.mult).then_inc(sem("mrep_ready"), 1)

            def attend(b, _):
                v.wait_ge(sem("o_psum"), b + 1)
                o = ps[:, 4:6, :].rearrange("p t (c d) -> p (t c) d", d=32)
                link(v.reciprocal(rcp[:, :], o[:, :, 8]))
                v.tensor_tensor(att[:, :, :].rearrange("p t (h d) -> p (t h) d", h=H), o[:, :, 0:8],
                                rcp[:, :].unsqueeze(2).broadcast_to([P, 2 * H, DK]), ALU.mult).then_inc(sem("att_ready"), 1)

            R = [rt[:, k, :].rearrange("p (t e) -> p t e", t=2) for k in range(8)]

            def route2(b, _):
                c1, c2, c3 = sm[:, 0:2], sm[:, 2:4], sm[:, 4:6]
                v.wait_ge(sem("al_psum"), b + 1)
                lg = ps[:, 6, 256:272].rearrange("p (t e) -> p t e", t=2)
                link(v.tensor_reduce(c1, lg, AX, ALU.max))
                link(v.tensor_tensor(R[0], lg, c1.unsqueeze(2).broadcast_to([P, 2, 8]), ALU.subtract))
                link(v.tensor_scalar(R[2][:, :, 0:MK], ps[:, 6, 272:284].rearrange("p (t e) -> p t e", t=2), -30.0, 30.0,
                                     ALU.max, ALU.min))
                v.tensor_reduce(c2, R[2][:, :, 0:MK], AX, ALU.max).then_inc(sem("rl_ready"), 1)
                v.wait_ge(sem("rl_ready"), b + 1)
                link(v.tensor_tensor(R[3][:, :, 0:MK], R[2][:, :, 0:MK], c2.unsqueeze(2).broadcast_to([P, 2, MK]), ALU.is_ge))
                link(v.tensor_tensor(R[3][:, :, 0:MK], R[3][:, :, 0:MK], ld["io9"][:, :].unsqueeze(1).broadcast_to([P, 2, MK]), ALU.mult))
                link(v.tensor_reduce(c3, R[3][:, :, 0:MK], AX, ALU.min))
                link(v.tensor_scalar(c3, c3, 10.0, None, ALU.add))
                v.wait_ge(sem("rexp_ready"), b + 1)
                link(v.tensor_reduce(c1, R[1], AX, ALU.add))
                link(v.reciprocal(c1, c1))
                link(v.tensor_tensor(R[4], R[1], c1.unsqueeze(2).broadcast_to([P, 2, 8]), ALU.mult))
                other = R[4].unsqueeze(2).broadcast_to([P, 2, 8, 8])
                own = R[4].unsqueeze(3).broadcast_to([P, 2, 8, 8])
                v.tensor_tensor(cmp[:, 0, :, :, :], other, own, ALU.is_gt)
                link(v.tensor_tensor(cmp[:, 1, :, :, :], other, own, ALU.is_equal))
                link(v.tensor_tensor(cmp[:, 1, :, :, :], cmp[:, 1, :, :, :], ld["tri"][:, :, :].unsqueeze(1).broadcast_to([P, 2, 8, 8]), ALU.mult))
                link(v.tensor_tensor(cmp[:, 0, :, :, :], cmp[:, 0, :, :, :], cmp[:, 1, :, :, :], ALU.add))
                link(v.tensor_reduce(rt[:, 5, :], cmp[:, 0, :, :, :].rearrange("p t e f -> p (t e) f"), AX, ALU.add))
                link(v.tensor_tensor(R[5], R[5], c3.unsqueeze(2).broadcast_to([P, 2, 8]), ALU.is_lt))
                link(v.tensor_tensor(score[:, b % 2, :].rearrange("p (t e) -> p t e", t=2), R[5], R[4], ALU.mult))

            def gather(b, e):
                v.wait_ge(sem("y3_psum"), b * E8 + e + 1)
                for t in range(2):
                    y = ps[:, 2, t * D:t * D + D]
                    w = score[:, b % 2, t * E8 + e:t * E8 + e + 1]
                    if e == 0:
                        i = v.tensor_scalar(macc[:, t, :], y, w, None, ALU.mult)
                    else:
                        i = v.scalar_tensor_tensor(macc[:, t, :], y, w, macc[:, t, :], ALU.mult, ALU.add)
                i.then_inc(sem("y3_used"), 1)
                v.wait_ge(sem("y3_used"), b * E8 + e + 1)

            def silu(b, n):
                m = b * E8 * IT + n
                v.wait_ge(sem("up_ready"), m + 1)
                v.scalar_tensor_tensor(sg[m % 3], sg[m % 3], 1.0, ps[0:IP, m % 2, 0:256], ALU.add,
                                       ALU.mult).then_inc(sem("gate_ready"), 1)

            def moe_out(b, _):
                x4 = cur[:, 2 * b:2 * b + 2, :]
                v.scalar_tensor_tensor(x4, macc[:, :, :], tg[:, 5:6], x4, ALU.mult, ALU.add).then_inc(sem("x4_ready"), 1)

            for q in range(2):
                best(0, q)
                where(0, q)
                pair(0, q)
            for t in range(NT):
                ctx_keys(t)
            stages = {"best": best, "where": where, "pair": pair, "weight": weight, "number": number,
                      "groups": groups, "place": place, "weigh": weigh, "norms": norms, "rope": rope, "split": split,
                      "max": max_, "neg_max": neg_max, "attend": attend, "route2": route2,
                      "times": silu, "gather": gather, "moe_out": moe_out}
            for name, b, k in steps():
                if name in stages:
                    stages[name](b, k)

        @block.tensor
        def _(pe):
            def mm(o, l, r, start=True, stop=True):
                return pe.matmul(o, l, r, start=start, stop=stop)

            def bias(o, row, w):
                return mm(o, ones[0:1, 0:P], ld["rows"][0:1, row:row + w], False, True)

            BQ, BKV, BO0, BQ1, BKV1, BO1 = 0, 128, 384, 512, 640, 896
            loaded(pe, 0)
            ctxs, dft, idft = ld["ctx"], ld["dft"], ld["idft"]
            for b in range(B):
                for k in range(2):
                    i = mm(ps[:, b, :], ctxs[:, 2 * b + k, :], dft[:, k, :, :].rearrange("p a c -> p (a c)"), k == 0, k == 1)
                i.then_inc(sem("cf_psum"), 1)
            loaded(pe, 1)
            for k in range(2):
                for t in range(4):
                    i = pe.transpose(ps[:, 4 + k, t * P:t * P + P], ctxs[:, 4 * k + t, :], ident[:, :])
                i.then_inc(sem("ctxT_psum"), 1)
            pe.wait_ge(sem("cf_ready"), B)
            for s, (bk, var_, w) in enumerate(((0, VC, 0), (1, VS, 0), (2, VCN, 0), (3, VC, 128), (6, VSN, 128))):
                for b in range(B):
                    o = ps[:, bk, b * P:b * P + P]
                    i = mm(o, cf[:, b, var_ * P:var_ * P + P], ld["wkv0T"][:, w:w + 128], True, var_ != VC)
                    if var_ == VC:
                        i = mm(o, ld["lrow"][0:1, 0:P], ld["rows"][0:1, BKV + w:BKV + w + 128], False, True)
            i.then_inc(sem("kv_psum"), 1)
            pe.wait_ge(sem("xn0_ready"), 1)
            pe.wait_ge(sem("ctxT_ready"), 2)
            pe.wait_ge(sem("kv_ready"), 2)
            for b in range(B):
                o = ps[:, 4 + b // 2, (b % 2) * 256:(b % 2) * 256 + 256]
                for k in range(2):
                    i = mm(o, xn[:, 2 * b + k, :], dft[:, k, 0:2, :].rearrange("p a c -> p (a c)"), k == 0, k == 1)
            i.then_inc(sem("xnf_psum"), 1)
            pe.wait_ge(sem("xnf_ready"), 1)
            for k in range(2):
                for b in range(B):
                    o = ps[:, 2 + k, b * P:b * P + P]
                    i = mm(o, cf[:, b // 2, (b % 2) * 256 + k * P:(b % 2) * 256 + k * P + P], ld["wq0T"][:, :], True, k == 1)
                    if k == 0:
                        i = mm(o, ld["lrow"][0:1, 0:P], ld["rows"][0:1, BQ:BQ + 128], False, True)
            i.then_inc(sem("q_psum"), 1)
            loaded(pe, 2)
            pe.wait_ge(sem("cps_ready"), 1)
            for k in range(2):
                i = mm(ps[0:64, 0, 0:L], cps[:, k, :], idft[:, k, :], k == 0, k == 1)
            i.then_inc(sem("corr_psum"), 1)
            pe.wait_ge(sem("wc_ready"), 1)
            for k in range(2):
                i = pe.transpose(ps[:, 1, k * 64:k * 64 + 64], ew[0:64, k * P:k * P + P], ident[0:64, 0:64])
            i.then_inc(sem("wcT_psum"), 1)
            pe.wait_ge(sem("wcT_ready"), 1)
            for s, var_ in enumerate((VC, VS, VCN)):
                for k in range(2):
                    i = mm(ps[:, 2, s * 64:s * 64 + 64], dft[:, k, var_, :], wcT[:, k, :], k == 0, k == 1)
            i.then_inc(sem("wf_psum"), 1)
            pe.wait_ge(sem("of_ready"), 1)
            for b in range(B):
                o = ps[:, 4 + b // 2, (b % 2) * 256:(b % 2) * 256 + 256]
                for k in range(2):
                    i = mm(o, spec[:, k, b * P:b * P + P], idft[:, k, :], k == 0, k == 1)
            i.then_inc(sem("ao_psum"), 1)
            pe.wait_ge(sem("ao_ready"), 1)
            for t in range(NT):
                o = ps[:, 6 + t // 4, (t % 4) * P:(t % 4) * P + P]
                mm(o, aoT[:, t * P:t * P + P], ld["wo0T"][:, :], True, False)
                i = bias(o, BO0, 128)
            i.then_inc(sem("y0_psum"), 1)

            pe.wait_ge(sem("xn1_ready"), 1)
            for t in range(NT):
                i = mm(ps[:, 7, 0:128], ld["ones"][:, P:2 * P], xn[:, t, :], t == 0, t == NT - 1)
            i.then_inc(sem("mean_psum"), 1)
            for t in range(NT):
                i = pe.transpose(ps[:, t // 4, (t % 4) * P:(t % 4) * P + P], xn[:, t, :], ident[:, :])
            i.then_inc(sem("xn1T_psum"), 1)
            pe.wait_ge(sem("xc_ready"), 1)
            for t in range(NT):
                i = mm(ps[:, 7, 128:256], xc[:, t, :], xc[:, t, :], t == 0, t == NT - 1)
            i.then_inc(sem("cov_psum"), 1)
            for t in range(NT):
                i = pe.transpose(ps[:, 2 + t // 4, (t % 4) * P:(t % 4) * P + P], xc[:, t, :], ident[:, :])
            i.then_inc(sem("xcT_psum"), 1)
            loaded(pe, 3)
            pe.wait_ge(sem("cov_ready"), 1)
            pe.wait_ge(sem("xcT_ready"), 1)
            w_q, w_qT, keysT = ld["w_q"], ld["w_qT"], ld["keysT"]
            for c in range(16):
                i = mm(ps[:, c // 4, (c % 4) * P:(c % 4) * P + P], w_q[:, c * P:c * P + P], cov[:, :])
            i.then_inc(sem("cw_psum"), 1)
            for c in range(16):
                i = mm(ps[32:33, 5, c * NK:c * NK + NK], ld["beta"][:, c:c + 1], keysT[:, c, :])
            pe.wait_ge(sem("keyS_ready"), 1)
            for c in range(16):
                i = mm(ps[:, 4, c * NK:c * NK + NK], w_qT[:, c, :], keyS[:, c, :])
            i.then_inc(sem("M_psum"), 1)
            pe.wait_ge(sem("M_ready"), 2)
            for t in range(NT):
                if t >= 4:
                    pe.wait_ge(sem("sim_ready"), t - 3)
                mm(ps[:, t % 4, :], xcT[:, t * P:t * P + P], M[:, :], True, False)
                mm(ps[:, t % 4, :], ones[32:33, 0:P], crow, False, True).then_inc(sem("sim_psum"), 1)
            for n in range(2 * EH):
                if n >= 4:
                    pe.wait_ge(sem("G_ready"), n - 3)
                mm(ps[:, 4 + n % 4, :], ld["downT"][:, (n // 2) * P:(n // 2) * P + P],
                   xnT[:, (n % 2) * 512:(n % 2) * 512 + 512]).then_inc(sem("G_psum"), 1)
            loaded(pe, 4)
            pe.wait_ge(sem("G_ready"), 2 * EH)
            pe.wait_ge(sem("identb_ready"), 1)

            def ctx_kv(t):
                if t >= 2:
                    pe.wait_ge(sem("v_ready"), t - 1)
                    pe.wait_ge(sem("ks_ready"), t - 1)
                mm(ps[:, 6 + t % 2, 0:256], ctxT[:, t * P:t * P + P], ld["Wkv1"][:, :], True, False)
                bias(ps[:, 6 + t % 2, 0:256], BKV1, 256).then_inc(sem("v_psum"), 1)

            ctx_kv(0)
            for t in range(NT):
                if t + 1 < NT:
                    ctx_kv(t + 1)
                pe.wait_ge(sem("ks_ready"), t + 1)
                if t >= 2:
                    pe.wait_ge(sem("kt_ready"), t - 1)
                for j in range(8):
                    i = pe.transpose(bank16(4 + t % 2)[:, j * P:j * P + P],
                                     qs[:, 2 * j:2 * j + 2, :, :].rearrange("p h s d -> p (h s d)"), identb[:, :])
                i.then_inc(sem("kt_psum"), 1)

            def onehots(b, _):
                pe.wait_ge(sem("elh_ready"), b + 1)
                if b == 0:
                    pe.wait_ge(sem("sim_ready"), NT)
                else:
                    pe.wait_ge(sem("xn2_ready"), b)
                pe.transpose(ps[:, 3, 0:128], elh[:, 0, :], ident[:, :])
                pe.transpose(ps[:, 3, 128:256], elh[:, 1, :], ident[:, :])
                pe.transpose(ps[:, 3, 256:384], wts[:, b % 2, :, :].rearrange("p a c -> p (a c)"),
                             ident[:, :]).then_inc(sem("eT_psum"), 1)

            def token(b, c):
                m = b * NC + c
                pe.wait_ge(sem("X_ready"), m + 1)
                if c == 0:
                    pe.wait_ge(sem("wlo_ready"), b + 1)
                else:
                    pe.wait_ge(sem("W_taken"), m)
                for half in range(2):
                    if half:
                        pe.wait_ge(sem("half_done"), m + 1)
                    for t in range(TC):
                        r = slice(64 * half, 64 * half + 64)
                        o = (half * TC + t) * 2 * EH
                        i = mm(ps[:, 3, o:o + 2 * EH], X[r, c % 2, :, t], Y[r, :, :, c * TC + t])
                    i.then_inc(sem("W_psum" if half else "half_done"), 1)

            def mix(b, _):
                pe.wait_ge(sem("HD_ready"), NC * b + NC)
                for t in range(2):
                    for e in range(EH):
                        i = mm(ps[:, 3, t * D:t * D + D], HD[:, e, t * P:t * P + P], ld["upl"][:, e, :], e == 0, e == EH - 1)
                i.then_inc(sem("y1_psum"), 1)

            def turn_x(b, _):
                pe.wait_ge(sem("xn2_ready"), b + 1)
                if b == 0:
                    pe.wait_ge(sem("kt_ready"), NT)
                    pe.wait_ge(sem("v_ready"), NT)
                else:
                    pe.wait_ge(sem("att_ready"), b)
                for t in range(2):
                    i = pe.transpose(ps[:, 4, t * P:t * P + P], xn2[:, t, :], ident[:, :])
                i.then_inc(sem("xn2T_psum"), 1)
                pe.wait_ge(sem("xn2T_ready"), b + 1)
                for t in range(2):
                    o = ps[:, 4, 256 + t * P:256 + t * P + P]
                    mm(o, xn2T[:, t * P:t * P + P], ld["Wq1"][:, :], True, False)
                    i = bias(o, BQ1, 128)
                i.then_inc(sem("q1_psum"), 1)

            def turn_q(b, _):
                pe.wait_ge(sem("qs_ready"), b + 1)
                if b >= 1:
                    pe.wait_ge(sem("rl_ready"), b)
                for j in range(8):
                    for t in range(2):
                        i = pe.transpose(bank16(6, 2)[:, (2 * j + t) * P:(2 * j + t) * P + P],
                                         qs[:, 16 * t + 2 * j:16 * t + 2 * j + 2, :, :].rearrange("p h s d -> p (h s d)"),
                                         identb[:, :])
                i.then_inc(sem("qT_psum"), 1)

            def by_query(b, g):
                if g < 2:
                    pe.wait_ge(sem("QT_ready"), 2 * b + g + 1)
                qt, gg = g // 4, g % 4
                bk = 4 + 2 * (g % 2)
                if g >= 2:
                    pe.wait_ge(sem("mx_ready"), b * 8 + g - 1)
                for jj in range(2):
                    for e in range(2):
                        r = slice(64 * e, 64 * e + 64)
                        i = mm(ps[:, bk + e, jj * 256:jj * 256 + 256], QT[r, 2 * gg + jj, qt * P:qt * P + P],
                               KT[r, 2 * gg + jj, b * L:b * L + L])
                i.then_inc(sem("s1_psum"), 1)

            def neg_max(b, _):
                pe.wait_ge(sem("mrep_ready"), b + 1)
                for t in range(2):
                    i = pe.transpose(bank16(4)[:, t * P:t * P + P], mrep[:, t, :], identb[:, :])
                i.then_inc(sem("mT_psum"), 1)

            def score_(b, h):
                n = b * H + h
                if h == 0:
                    pe.wait_ge(sem("mT_ready"), b + 1)
                if h >= 2:
                    pe.wait_ge(sem("p_ready"), n - 1)
                j, e = h // 2, h % 2
                r = slice(64 * e, 64 * e + 64)
                c = 64 * e + (j // 2) * 4 + e * 2 + j % 2
                for k in range(2):
                    o = ps[:, 4 + (h + 1) % 2, k * 256:k * 256 + 256]
                    mm(o, KT[r, j, b * L + k * P:b * L + k * P + P], QT[r, j, :], True, False)
                    i = mm(o, identb[r, c:c + 1].broadcast_to([64, P]), mT[r, :], False, True)
                i.then_inc(sem("s2_psum"), 1)

            def value(b, h):
                pe.wait_ge(sem("p_ready"), b * H + h + 1)
                r = 32 * (h % 4)
                for k in range(2):
                    i = mm(ps[r:r + 32, 6 + h // 8, (h // 4 % 2) * 256:(h // 4 % 2) * 256 + 256],
                           V[:, 2 * b + k, 9 * h:9 * h + 32], PE_[:, h % 2, k, :], k == 0, k == 1)
                i.then_inc(sem("av_done"), 1)

            def out_turn(b, _):
                pe.wait_ge(sem("oT_ready"), b + 1)
                for t in range(2):
                    for g in range(4):
                        i = pe.transpose(ps[:, 4 + t, g * P:g * P + P], oT[:, g, t * P:t * P + P], ident[:, :])
                i.then_inc(sem("o_psum"), 1)

            def attend(b, _):
                pe.wait_ge(sem("att_ready"), b + 1)
                for t in range(2):
                    i = pe.transpose(ps[:, 6, t * P:t * P + P], att[:, t, :], ident[:, :])
                i.then_inc(sem("attT_psum"), 1)
                pe.wait_ge(sem("attT_ready"), b + 1)
                for t in range(2):
                    o = ps[:, 7, t * P:t * P + P]
                    mm(o, attT[:, t * P:t * P + P], ld["Wo1"][:, :], True, False)
                    i = bias(o, BO1, 128)
                i.then_inc(sem("y2_psum"), 1)

            def route1(b, _):
                if b == 0:
                    loaded(pe, 5)
                pe.wait_ge(sem("xn3_ready"), b + 1)
                for t in range(2):
                    i = pe.transpose(ps[:, 6, t * P:t * P + P], xn3[:, t, :], ident[:, :])
                i.then_inc(sem("xn3T_psum"), 1)
                pe.wait_ge(sem("xn3T_ready"), b + 1)
                for t in range(2):
                    mm(ps[:, 6, 256 + t * 8:256 + t * 8 + 8], xn3T[b % 2][:, t * P:t * P + P], ld["rw"][:, :])
                mm(ps[0:AH, 7, 0:256], ld["w1T"][:, :], xn3T[b % 2]).then_inc(sem("ah_psum"), 1)

            def route2(b, _):
                pe.wait_ge(sem("ah_ready"), b + 1)
                for t in range(2):
                    i = mm(ps[:, 6, 272 + t * MK:272 + t * MK + MK], ah[0:AH + 1, t * P:t * P + P], ld["w2T"][:, :])
                i.then_inc(sem("al_psum"), 1)

            def gate(b, n):
                m = b * E8 * IT + n
                if m >= 2:
                    pe.wait_ge(sem("gate_ready"), m - 1)
                e, k = n // IT, n % IT
                for s in range(2):
                    i = mm(ps[0:IP, m % 2, s * 256:s * 256 + 256], ld["guT"][:, e, s, k * IP:k * IP + IP], xn3T[b % 2])
                i.then_inc(sem("gu_psum"), 1)

            def down(b, e):
                m = b * E8 + e
                pe.wait_ge(sem("av_ready"), (m + 1) * IT)
                if m >= 1:
                    pe.wait_ge(sem("y3_used"), m)
                for t in range(2):
                    for k in range(IT):
                        i = mm(ps[:, 2, t * D:t * D + D], av[:, (m * IT + k) % 6, t * P:t * P + P],
                               ld["dn"][:, e * IT + k, :], k == 0, k == IT - 1)
                i.then_inc(sem("y3_psum"), 1)

            stages = {"onehots": onehots, "token": token, "mix": mix, "turn_x": turn_x, "turn_q": turn_q,
                      "by_query": by_query, "neg_max": neg_max, "score": score_, "value": value, "out_turn": out_turn,
                      "attend": attend, "route1": route1, "route2": route2, "gate": gate, "down": down}
            for name, b, k in steps():
                if name in stages:
                    stages[name](b, k)


def constants():
    t, f = np.arange(L)[:, None].astype(np.float64), np.arange(P)[None, :].astype(np.float64)
    w = 2 * np.pi / L
    nyq = np.where(np.arange(L) % 2 == 0, 1.0, -1.0)
    c, s = np.cos(w * ((t * f) % L)), np.sin(w * ((t * f) % L))
    sn, cn = s.copy(), c.copy()
    sn[:, 0], cn[:, 0] = nyq, nyq
    dft = np.stack([c, sn, s, cn], 1)
    ic, is_ = 2 * c.T / L, 2 * s.T / L
    ic[0], is_[0] = 1.0 / L, nyq / L
    ones = np.ones((P, 2 * P))
    ones[:, P:] = 1.0 / (NT * P)
    lrow = np.zeros((1, P))
    lrow[0, 0] = L
    tri = np.tile((np.arange(8)[None, :] < np.arange(8)[:, None])[None], (P, 1, 1))
    r = {
        "dft": dft.reshape(2, P, 4, P).transpose(1, 0, 2, 3), "idft": np.stack([ic, is_], 1),
        "ident": np.eye(P), "ones": ones, "lrow": lrow, "tri": tri,
        "io16": np.tile(16 * np.arange(EH)[None], (P, 1)),
        "io20": np.tile(np.arange(CAND)[None], (P, 1)), "io9": np.tile(np.arange(MK)[None] - 9, (P, 1)),
    }
    return {k: np.ascontiguousarray(v, dtype=np.float32) for k, v in r.items()}


def kernel(**inputs):
    import concourse.bacc as bacc
    from concourse.bass_utils import run_bass_kernel_spmd

    i = {k: np.asarray(v) for k, v in inputs.items()}

    def tiles(x):
        return x.reshape(NT, P, D).transpose(1, 0, 2)

    lay = {
        "x": tiles(i["x"]), "ctx": tiles(i["ctx_1024"]),
        "pos": np.concatenate([i["itok_BxS_0_4095"].reshape(NT, P).T, i["itok_BxS2_1_4095"].reshape(NT, P).T], 1),
        "gates": np.concatenate([i["g_xattn"], i["g_ffn"]])[None],
        "wq0T": i["L0_xattn_Wq"].T, "wkv0T": np.concatenate([i["L0_xattn_Wk"].T, i["L0_xattn_Wv"].T], 1),
        "wo0T": i["L0_xattn_Wo"].T,
        "rows": np.concatenate([i["L0_xattn_bq"], i["L0_xattn_bk"], i["L0_xattn_bv"], i["L0_xattn_bo"],
                                i["L1_xattn_b_q"], i["L1_xattn_b_kv"], i["L1_xattn_b_o"]])[None],
        "w_q": i["L0_ffn_w_q"], "w_qT": i["L0_ffn_w_q"].reshape(D, 16, P).transpose(2, 1, 0),
        "keysT": i["L0_ffn_keys"].transpose(3, 2, 0, 1).reshape(P, 16, NK),
        "gamma": i["L0_ffn_bn_gamma"].reshape(16, P).T, "beta": i["L0_ffn_bn_beta"].reshape(16, P).T,
        "downT": i["L0_ffn_down_embed"].T, "upl": i["L0_ffn_up_embed"].reshape(EH, P, D).transpose(1, 0, 2),
        "Wq1": i["L1_xattn_W_q"], "Wkv1": i["L1_xattn_W_kv"], "Wo1": i["L1_xattn_W_o"],
        "rw": i["L1_ffn_router_w"].T, "w1T": i["L1_ffn_actor_w1"].T, "b1": i["L1_ffn_actor_b1"][:, None],
        "w2T": np.concatenate([i["L1_ffn_actor_w2"].T, i["L1_ffn_actor_b2"][None]], 0),
        "guT": np.stack([i["L1_ffn_gate_w"], i["L1_ffn_up_w"]], 1).transpose(3, 0, 1, 2),
        "dn": i["L1_ffn_down_w"].reshape(E8, D, IT, IP).transpose(3, 0, 2, 1).reshape(IP, E8 * IT, D),
    }
    lay.update(constants())
    nc = bacc.Bacc("TRN2", target_bir_lowering=False, num_devices=1)
    arrays, aps = {}, {}
    for name, x in lay.items():
        x = np.ascontiguousarray(x)
        arrays["in_" + name] = x
        aps[name] = nc.dram_tensor("in_" + name, x.shape, mybir.dt.from_np(x.dtype), kind="ExternalInput").ap()
    out = nc.dram_tensor("out_0", (B, L, D), F32, kind="ExternalOutput").ap()
    program(nc, aps, out)
    r = run_bass_kernel_spmd(nc, [arrays], core_ids=[0])
    return r.results[0]["out_0"]
```

```python
from contextlib import ExitStack

import numpy as np

import concourse.bass as bass
from concourse import mybir

F32 = mybir.dt.float32
BF16 = mybir.dt.bfloat16
F16 = mybir.dt.float16
I32 = mybir.dt.int32
U32 = mybir.dt.uint32
ALU = mybir.AluOpType
ACT = mybir.ActivationFunctionType
AX = mybir.AxisListType.X

P = 128
B, L, D = 4, 256, 128
NT = B * L // P
H, DK = 16, 8
TOP = 5
PH, NK = 8, 32
KT8 = 8
NE = NK * NK
EH = NE // P
CAND = 20
E8, I, IT, IP = 8, 336, 3, 112
AH, MK = 50, 6
EPS = 1e-5
WSCALE = 1024.0
TC, NC = 16, 8
VW = H * (DK + 1) + 24
SL = 8
TWO_PI = 6.283185307179586
C1 = 6.28125
C2 = float(np.float32(TWO_PI - C1))
C3 = float(TWO_PI - C1 - float(np.float32(TWO_PI - C1)))
ROUND = 12582912.0
AHEAD = {
    -1: "gate silu times down gather moe_out",
    0: "turn_q by_query max neg_max score prob value out_turn attend project turn_3 route1 route2",
    1: "look_a look_b look_c look_d soft weight number onehots groups place token weigh mix norms turn_2 query rope split",
    2: "best where pair",
}
AHEAD = {stage: k for k, stages in AHEAD.items() for stage in stages.split()}
EARLY = {"look_a0", "look_b0", "look_c0", "look_d0"}
FIRST = """
look_a1 soft0 look_b1 weight0 soft1 look_c1 look_d1 weight1 number onehots groups place0 place1 token0 weigh0 place2
token1 token2 weigh1 place3 token3 weigh2 place4 weigh3 place5 token4 weigh4 token5 place6 token6 weigh5 place7 token7
weigh6 best0 weigh7 mix norms turn_2 where0 query rope pair0 look_a0 look_b0 look_c0 best1 look_d0 split where1 pair1
"""
SECOND = """
soft0 turn_q by_query0 by_query1 look_a1 by_query2 max0 by_query3 max1 look_b1 by_query4 max2 weight0 best0 max3 max4
by_query5 by_query6 max5 max6 by_query7 max7 soft1 neg_max look_c1 look_d1 score0 prob0 score1 score2 weight1 number
onehots prob1 value0 value1 score3 prob2 score4 prob3 score5 value2 value3 prob4 score6 groups value4 prob5 prob6
score7 prob7 place0 value5 token0 place1 weigh0 score8 place2 prob8 value6 value7 token1 score9 weigh1 prob9 score10
value8 token2 prob10 score11 place3 weigh2 value9 place4 score12 value10 prob11 value11 token3 weigh3 prob12 place5
score13 token4 prob13 score14 value12 weigh4 score15 place6 token5 prob14 prob15 value13 value14 weigh5 value15 token6
place7 out_turn token7 weigh6 attend weigh7 project mix norms turn_2 turn_3 route1 where0 route2 query rope pair0
best1 look_a0 look_b0 look_c0 split where1 pair1 look_d0
"""
PERIOD = """
turn_q gate0 by_query0 silu0 soft0 gate1 by_query1 gate2 max0 look_a1 silu1 soft1 weight0 by_query2 gate3 look_b1
times0 max1 by_query3 times1 silu2 gate4 by_query4 max2 times2 max3 silu3 by_query5 max4 down0 look_c1 times3 max5
by_query6 look_d1 gate5 silu4 by_query7 silu5 gate6 gather0 max6 max7 neg_max times4 gate7 times5 score0 prob0 score1
prob1 weight1 score2 down1 silu6 silu7 number best0 value0 prob2 onehots value1 value2 score3 gather1 prob3 score4
gate8 times6 prob4 score5 prob5 silu8 groups value3 times7 score6 place0 value4 score7 value5 prob6 prob7 gate9 score8
silu9 value6 times8 prob8 token0 down2 score9 value7 place1 weigh0 prob9 gather2 gate10 score10 silu10 token1 value8
place2 prob10 times9 value9 gate11 silu11 weigh1 token2 score11 place3 score12 value10 weigh2 times10 prob11 prob12
gate12 token3 score13 value11 times11 place4 weigh3 score14 silu12 prob13 value12 prob14 down3 score15 token4 prob15
place5 gather3 weigh4 value13 gate13 place6 value14 token5 value15 gate14 times12 out_turn token6 silu13 weigh5 place7
silu14 times13 attend weigh6 token7 project weigh7 mix times14 gate15 gate16 silu15 norms silu16 down4 gather4 times15
gate17 times16 where0 turn_3 route1 turn_2 route2 silu17 times17 gate18 query gate19 silu18 gate20 rope pair0 down5
silu19 best1 gather5 look_a0 silu20 look_b0 times18 times19 gate21 times20 where1 pair1 look_c0 look_d0 silu21 split
gate22 down6 gather6 times21 silu22 gate23 silu23 times22 times23 down7 gather7 moe_out
"""
LAST = """
gate0 silu0 gate1 silu1 times0 gate2 silu2 times1 gate3 silu3 times2 gate4 silu4 times3 gate5 down0 silu5 times4 gate6
silu6 times5 gather0 gate7 silu7 times6 gate8 down1 silu8 times7 gate9 silu9 times8 gather1 gate10 silu10 times9
gate11 down2 silu11 times10 gate12 silu12 times11 gather2 gate13 silu13 times12 gate14 down3 silu14 times13 gate15
silu15 times14 gather3 gate16 silu16 times15 gate17 down4 silu17 times16 gate18 silu18 times17 gather4 gate19 silu19
times18 gate20 down5 silu20 times19 gate21 silu21 times20 gather5 gate22 silu22 times21 gate23 down6 silu23 times22
times23 gather6 down7 gather7 moe_out
"""


def steps():
    for s in range(-1, B + 1):
        for word in {-1: FIRST, 0: SECOND, B: LAST}.get(s, PERIOD).split():
            name = word.rstrip("0123456789") if word not in AHEAD else word
            b = s + AHEAD[name] + (word in EARLY)
            if 0 <= b < B + (name == "norms"):
                yield name, b, int(word[len(name):] or 0)


VC, VSN, VS, VCN = range(4)


def program(nc, a, out):
    with ExitStack() as ctx:
        def sb(name, shape, dt=F32):
            return ctx.enter_context(nc.sbuf_tensor(name, shape, dt))

        sems = {}

        def sem(name):
            if name not in sems:
                sems[name] = ctx.enter_context(nc.semaphore(name))
            return sems[name]

        ps = ctx.enter_context(nc.psum_tensor("ps", [P, 8, 512], F32))

        def bank16(n, k=1):
            return ps[:, n:n + k, :].rearrange("p a c -> p (a c)").bitcast(BF16)

        Gb, Xb, HDb = sb("Gb", [P, EH * NT * P]), sb("Xb", [P, 4096]), sb("HDb", [P, EH * 2 * P])
        Sb, simb = sb("Sb", [P, 5888]), sb("simb", [P, NT * 512])
        Glow, Ghigh = Gb[:, 0:EH * NT * P // 2], Gb[:, EH * NT * P // 2:]
        KTb, xnb, ctxTb = sb("KTb", [P, H // 4 * NT * P]), sb("xnb", [P, NT * D]), sb("ctxTb", [P, NT * P])
        taken = {}

        def over(base, shape):
            n, at = int(np.prod(shape[1:])), taken.get(id(base), 0)
            taken[id(base)] = at + n
            w = base[:, at:at + n]
            if len(shape) == 3:
                return w.rearrange("p (a c) -> p a c", a=shape[1])
            if len(shape) == 4:
                return w.rearrange("p (a c d) -> p a c d", a=shape[1], c=shape[2])
            return w

        ld = {}
        for name, ap in a.items():
            shape = list(ap.shape)
            if name == "gates":
                shape = [P, 4]
            if name == "dn":
                dnb = sb("dnb", [P, E8 * IT * D])
                ld[name] = dnb[0:IP, :].rearrange("p (a c) -> p a c", a=E8 * IT)
            elif name in ("w_q", "w_qT"):
                ld[name] = over(simb, shape)
            elif name == "keysT":
                ld[name] = over(Ghigh, shape)
            elif name in ("dft", "idft", "ctx", "wkv0T", "wq0T", "wo0T"):
                ld[name] = over(Glow, shape)
            else:
                ld[name] = sb("sb_" + name, shape, ap.dtype)
        ident, ones, cur = ld["ident"], ld["ones"], ld["x"]
        identb = sb("identb", [P, P], BF16)
        tg = sb("tg", [P, 6])

        cf = over(Xb, [P, B, 4 * P])
        ctxT = ctxTb
        kv = over(Sb, [P, 5, B * P])
        KC, KS, KCN, VVC, VVS = range(5)
        qf = over(Xb, [P, 2, B * P])
        tmp = over(Ghigh, [P, 2048])
        spec = over(Xb, [P, 2, B * P])
        cps = over(Glow, [P, 2, B * H])
        corr = over(Glow, [P, L])
        ew = over(Glow, [P, L])
        sm = sb("sm", [P, 64])
        wcT = over(Glow, [P, 2, B * H])
        wf = over(Glow, [P, 3, B * H])
        aoT = HDb[:, 0:NT * P]
        xnf = spec

        xn = xnb[:, :].rearrange("p (t d) -> p t d", t=NT)
        xnT = over(dnb, [P, NT * P])
        st = sb("st", [P, NT, 6])
        mv = sb("mv", [P, NT, 2])
        rs = sb("rs", [P, 4, NT])

        xc = over(HDb, [P, NT, D])
        xcT = over(HDb, [P, NT * P])
        cov = over(Ghigh, [P, D])
        var = sb("var", [P, 4, 16])
        keyS = over(Ghigh, [P, 16, NK])
        M = over(dnb, [P, 512])
        bshift = over(Ghigh, [P, 512])
        sim = simb[:, :].rearrange("p (t c) -> p t c", t=NT)
        top = sb("top", [P, 2, 16, 8])
        tix = sb("tix", [P, 2, 16, 8], U32)
        tixf = sb("tixf", [P, 2, 16, 8])
        cand = sb("cand", [P, 2, PH, CAND])
        candi = sb("candi", [P, 2, PH, CAND])
        sc = sb("sc", [P, 2, PH, 8])
        pk = sb("pk", [P, 2, PH, 8], U32)
        pkf = sb("pkf", [P, PH * 8])
        hot = sb("hot", [P, PH * 8, CAND], F16)
        dd = sb("dd", [P, 2, PH, 8])
        zz = sb("zz", [P, 2, PH])
        ex_ = sb("ex_", [P, 2, PH, 8])
        wts = sb("wts", [P, 2, 2, 64])
        eid = sb("eid", [P, 2, 2, 64])
        eidi = sb("eidi", [P, 3, P], I32)
        elh = sb("elh", [P, 2, P])
        elT = sb("elT", [P, 2, P], F16)
        whl = sb("whl", [P, 2, P], F16)
        iox = sb("iox", [P, 16, TC], F16)
        elS = sb("elS", [P, EH, P], F16)
        X = Xb[:, 0:P * TC].bitcast(F16).rearrange("p (b e t) -> p b e t", b=2, e=P)
        Yq = Xb[:, 2304:2816].bitcast(F16).rearrange("p (e t) -> p e t", e=EH)
        Y = sb("Y", [P, EH, 2, P], F16)
        W = Xb[:, 2048:2048 + 2 * TC * EH].rearrange("p (s c) -> p s c", s=2)
        G = Gb[:, :].rearrange("p (e t) -> p e t", e=EH)
        HD = HDb[:, :].rearrange("p (e t) -> p e t", e=EH)

        cs = sb("cs", [P, 2, 2 * NT, 4])
        ang = sb("ang", [P, 3, 2 * NT * 4])
        posf = sb("posf", [P, 2 * NT])
        qs = Sb[:, 3072:4096].bitcast(BF16).rearrange("p (h s d) -> p h s d", s=SL, d=DK)
        KT = KTb[:, :].bitcast(BF16).rearrange("p (j t) -> p j t", j=H // 2)
        QT = Sb[:, 4096:5120].bitcast(BF16).rearrange("p (j t) -> p j t", j=H // 2)
        oT = Sb[:, 4096:5120].rearrange("p (g t) -> p g t", g=4)
        V = sb("V", [P, NT, VW])
        ra = Sb[:, 5120:5376].rearrange("p (t d) -> p t d", t=2)
        rb = Sb[:, 5376:5632].rearrange("p (t d) -> p t d", t=2)
        rq = Sb[:, 5632:5888].rearrange("p (t d) -> p t d", t=2)
        mx = sb("mx", [P, 2, H])
        mrep = sb("mrep", [P, 2, P], BF16)
        mT = sb("mT", [P, 2 * P], BF16)
        PE_ = Sb[:, 0:1024].rearrange("p (a k c) -> p a k c", a=2, k=2)
        rcp = sb("rcp", [P, 2 * H])
        att = xnb[:, 256:512].rearrange("p (t d) -> p t d", t=2)
        attT = ctxTb[:, 0:256]
        xn2 = xnb[:, 0:256].rearrange("p (t d) -> p t d", t=2)
        xn2T = ctxTb[:, 256:512]

        xn3 = xnb[:, 512:768].rearrange("p (t d) -> p t d", t=2)
        xn3T = [ctxTb[:, 512:768], Xb[:, 3840:4096]]
        score = sb("score", [P, 2, 16])
        ah = sb("ah", [64, 2 * P])
        rt = sb("rt", [P, 8, 16])
        cmp = ctxTb[:, 768:1024].rearrange("p (a t e f) -> p a t e f", a=2, t=2, e=8)
        gu = [Sb[0:IP, 1024:1536], Xb[0:IP, 2816:3328], Xb[0:IP, 3328:3840]]
        av = Sb[0:IP, 1536:3072].rearrange("p (a c) -> p a c", a=6)
        macc = xnb[:, 768:1024].rearrange("p (t d) -> p t d", t=2)

        assert all(v <= n for v, n in ((taken[id(Glow)], 4096), (taken[id(Ghigh)], 4096), (taken[id(Xb)], 4096), (taken[id(Sb)], 5888)))

        G_BANK = [6 + n % 2 if n < EH else 4 + n % 4 for n in range(2 * EH)]

        block = ctx.enter_context(nc.Block())

        groups = [
            ["ctx", "dft"], ["x", "wkv0T", "wq0T", "rows", "ident", "ones", "lrow"],
            ["idft", "wo0T", "gates", "gamma", "beta", "pos", "io20", "tri", "io9", "io16", "Wkv1"],
            ["w_q", "w_qT", "keysT", "downT"],
            ["upl", "Wq1", "Wo1"],
            ["rw", "w1T", "b1", "w2T", "guT", "dn"],
        ]

        def loaded(eng, g):
            eng.wait_ge(sem(f"load{g}"), 16 * len(groups[g]))

        @block.sync
        def _(sp):
            for g, names in enumerate(groups):
                for n in names:
                    if n == "dn":
                        sp.wait_ge(sem("G_psum"), 2 * EH)
                    src = a[n]
                    if n == "gates":
                        src = src.broadcast_to([P, 4])
                    idx = (slice(None),) * len(ld[n].shape)
                    sp.dma_start(ld[n][idx], src[idx]).then_inc(sem(f"load{g}"), 16)
            for t in range(NT):
                if t % 2 == 0:
                    sp.wait_ge(sem("x4_ready"), t // 2 + 1)
                sp.dma_start(out.rearrange("b (j p) d -> (b j) p d", p=P)[t], cur[:, t, :]).then_inc(sem("stored"), 16)
            sp.wait_ge(sem("stored"), 16 * NT)

        @block.gpsimd
        def _(g):
            g.iota(iox[:, :, :], pattern=[[1, 16], [0, TC]], base=0, channel_multiplier=0,
                   allow_small_or_imprecise_dtypes=True).then_inc(sem("iox_ready"), 1)

            n = [0]

            def link(ins):
                ins.then_inc(sem("pool_chain"), 1)
                n[0] += 1
                g.wait_ge(sem("pool_chain"), n[0])

            loaded(g, 2)
            def look_a(b, q):
                t = 2 * b + q
                g.wait_ge(sem("tix_ready"), t + 1)
                g.tensor_scalar(tixf[:, q, 0:8, :], tix[:, q, 0:8, :], float(NK), None, ALU.mult)
                link(g.tensor_copy(tixf[:, q, 8:16, :], tix[:, q, 8:16, :]))
                xi, yi = tixf[:, q, 0:8, :], tixf[:, q, 8:16, :]
                g.tensor_tensor(candi[:, q, :, 0:8], yi, xi[:, :, 0:1].broadcast_to([P, PH, 8]), ALU.add)
                g.tensor_tensor(candi[:, q, :, 8:12], yi[:, :, 0:4], xi[:, :, 1:2].broadcast_to([P, PH, 4]), ALU.add)
                g.tensor_tensor(candi[:, q, :, 12:16].rearrange("p h (a b) -> p h a b", a=2),
                                yi[:, :, 0:2].unsqueeze(2).broadcast_to([P, PH, 2, 2]),
                                xi[:, :, 2:4].unsqueeze(3).broadcast_to([P, PH, 2, 2]), ALU.add)
                i = g.tensor_tensor(candi[:, q, :, 16:20], xi[:, :, 4:8], yi[:, :, 0:1].broadcast_to([P, PH, 4]), ALU.add)
                i.then_inc(sem("candi_ready"), 1)
                g.wait_ge(sem("candi_ready"), t + 1)
                if b == 0:
                    return
                g.wait_ge(sem("pk_ready"), t + 1)
                link(g.tensor_copy(pkf[:, :], pk[:, q, :, :].rearrange("p h k -> p (h k)")))

            def look_b(b, q):
                if b == 0:
                    return
                g.wait_ge(sem("hot_used"), 2 * b + q)
                link(g.tensor_tensor(hot[:, :, :], pkf[:, :].unsqueeze(2).broadcast_to([P, 64, CAND]),
                                     ld["io20"][:, :].unsqueeze(1).broadcast_to([P, 64, CAND]), ALU.subtract))

            def look_c(b, q):
                if b == 0:
                    return
                link(g.tensor_scalar(hot[:, :, :], hot[:, :, :], 0.0, None, ALU.is_equal))

            def look_d(b, q):
                if b == 0:
                    return
                h4 = hot[:, :, :].rearrange("p (h k) c -> p h k c", h=PH)
                g.tensor_tensor(h4, h4, candi[:, q, :, :].unsqueeze(2).broadcast_to([P, PH, 8, CAND]),
                                ALU.mult).then_inc(sem("hot_ready"), 1)

            def times(b, n):
                m = b * E8 * IT + n
                g.wait_ge(sem("gate_ready"), m + 1)
                g.tensor_tensor(av[:, m % 6, :], av[:, m % 6, :], gu[m % 3][:, 256:512], ALU.mult).then_inc(sem("av_ready"), 1)

            stages = {"look_a": look_a, "look_b": look_b, "look_c": look_c, "look_d": look_d, "times": times}
            look_a(0, 0)
            for name, b, k in steps():
                if name in stages:
                    stages[name](b, k)

        @block.scalar
        def _(act):
            def copy(dst, src, s, scale=1.0):
                act.activation(dst, src, ACT.Copy, scale=scale).then_inc(sem(s), 1)

            loaded(act, 1)
            act.activation(identb[:, :], ident[:, :], ACT.Copy).then_inc(sem("identb_ready"), 1)
            for b in range(B):
                act.wait_ge(sem("cf_psum"), b + 1)
                copy(cf[:, b, :], ps[:, b, :], "cf_ready")
            act.wait_ge(sem("xnf_psum"), 1)
            copy(xnf[:, :, :], ps[:, 4:6, :], "xnf_ready")
            loaded(act, 2)
            act.activation(tg[:, 0:4], ld["gates"][:, :], ACT.Tanh).then_inc(sem("tg_ready"), 1)
            act.wait_ge(sem("ang_ready"), 1)
            act.activation(cs[:, :, :, :].rearrange("p a t f -> p (a t f)"),
                           ang[:, 0:2, :].rearrange("p a t -> p (a t)"), ACT.Sin).then_inc(sem("cs_ready"), 1)
            act.wait_ge(sem("kv_psum"), 1)
            copy(kv[:, 0:4, :], ps[:, 0:4, :], "kv_ready")
            copy(kv[:, 4, :], ps[:, 6, :], "kv_ready")
            for k in range(2):
                act.wait_ge(sem("ctxT_psum"), k + 1)
                copy(ctxT[:, 512 * k:512 * k + 512], ps[:, 7 * (1 - k), :], "ctxT_ready")

            def ctx_out(t):
                act.wait_ge(sem("v_psum"), t + 1)
                act.wait_ge(sem("ks_ready"), t + 1)
                act.activation(V[:, t, 0:9 * H].rearrange("p (h d) -> p h d", h=H)[:, :, 0:DK],
                               ps[:, 6, 128:256].rearrange("p (h d) -> p h d", h=H), ACT.Copy).then_inc(sem("v_ready"), 1)
                act.wait_ge(sem("kt_psum"), t + 1)
                act.activation(KT[:, :, t * P:t * P + P], bank16(7).rearrange("p (j c) -> p j c", j=8),
                               ACT.Copy).then_inc(sem("kt_ready"), 1)

            act.wait_ge(sem("corr_psum"), 1)
            copy(corr[0:64, :], ps[0:64, 0, 0:L], "corr_ready", 1.0 / DK)
            ctx_out(0)
            act.wait_ge(sem("corr_max"), 1)
            act.activation(ew[0:64, :], corr[0:64, :], ACT.Exp, bias=sm[0:64, 8:9]).then_inc(sem("ew_ready"), 1)
            ctx_out(1)
            act.wait_ge(sem("wcT_psum"), 1)
            copy(wcT[:, :, :].rearrange("p a c -> p (a c)"), ps[:, 1, 0:128], "wcT_ready")
            act.wait_ge(sem("wf_psum"), 1)
            copy(wf[:, :, :].rearrange("p a c -> p (a c)"), ps[:, 2, 0:192], "wf_ready")
            ctx_out(2)
            ctx_out(3)
            act.wait_ge(sem("ao_psum"), 1)
            copy(aoT, ps[:, 4:6, :].rearrange("p a c -> p (a c)"), "ao_ready")
            ctx_out(4)
            act.wait_ge(sem("xn1T_psum"), 1)
            copy(xnT[:, :], ps[:, 0:2, :].rearrange("p a c -> p (a c)"), "xn1T_ready")
            ctx_out(5)
            act.wait_ge(sem("cov_psum"), 1)
            copy(cov[:, :], ps[:, 5, 128:256], "cov_ready", 1.0 / (NT * P))
            act.wait_ge(sem("xcT_psum"), 1)
            copy(xcT[:, :], ps[:, 2:4, :].rearrange("p a c -> p (a c)"), "xcT_ready")
            ctx_out(6)
            act.wait_ge(sem("shift_psum"), 1)
            copy(bshift[:, :], ps[:, 5, :], "shift_ready")

            def gelu(n):
                act.wait_ge(sem("G_psum"), n + 1)
                if n == EH:
                    act.wait_ge(sem("sim_ready"), NT)
                act.activation(G[:, n // 2, 512 * (n % 2):512 * (n % 2) + 512], ps[:, G_BANK[n], :],
                               ACT.Gelu_apprx_tanh).then_inc(sem("G_ready"), 1)

            act.wait_ge(sem("MT_psum"), 1)
            copy(tmp[:, 0:512], ps[:, 4, :], "MT_ready")
            act.wait_ge(sem("M_psum"), 1)
            copy(M[:, :], ps[:, 4, :], "M_ready")
            ctx_out(7)
            def soft(b, q):
                act.wait_ge(sem("dd_ready"), 2 * b + q + 1)
                act.activation(ex_[:, q, :, :], dd[:, q, :, :], ACT.Exp).then_inc(sem("ex_ready"), 1)

            for n in range(EH):
                gelu(n)
            soft(0, 0)
            soft(0, 1)
            for n in range(EH, 2 * EH):
                gelu(n)

            def onehots(b, _):
                act.wait_ge(sem("eT_psum"), b + 1)
                copy(elT[:, :, :].rearrange("p a c -> p (a c)"), ps[:, 3, 0:256], "elT_ready")
                copy(whl[:, 0, :], ps[:, 3, 256:384], "whi_ready", WSCALE)

            def turn_2(b, _):
                act.wait_ge(sem("xn2T_psum"), b + 1)
                copy(xn2T[:, :], ps[:, 4, 0:256], "xn2T_ready")

            def turn_q(b, _):
                act.wait_ge(sem("qT_psum"), b + 1)
                for k in range(2):
                    act.activation(QT[:, 4 * k:4 * k + 4, :].rearrange("p j c -> p (j c)"), bank16(6 + k),
                                   ACT.Copy).then_inc(sem("QT_ready"), 1)

            def neg_max(b, _):
                act.wait_ge(sem("mT_psum"), b + 1)
                act.activation(mT[:, :], bank16(4)[:, 0:256], ACT.Copy).then_inc(sem("mT_ready"), 1)

            def prob(b, h):
                n = b * H + h
                act.wait_ge(sem("s2_psum"), n + 1)
                if n >= 2:
                    act.wait_ge(sem("av_done"), n - 1)
                act.activation(PE_[:, h % 2, :, :].rearrange("p a c -> p (a c)"), ps[:, 4 + (h + 1) % 2, :], ACT.Exp,
                               scale=float(1.0 / np.sqrt(DK))).then_inc(sem("p_ready"), 1)

            def out_turn(b, _):
                act.wait_ge(sem("av_done"), H * (b + 1))
                copy(oT[:, :, :].rearrange("p (a g) c -> p a (g c)", a=2), ps[:, 6:8, :], "oT_ready")

            def attend(b, _):
                act.wait_ge(sem("attT_psum"), b + 1)
                copy(attT[:, :], ps[:, 6, 0:256], "attT_ready")

            def turn_3(b, _):
                act.wait_ge(sem("xn3T_psum"), b + 1)
                copy(xn3T[b % 2], ps[:, 6, 0:256], "xn3T_ready")

            def route1(b, _):
                act.wait_ge(sem("ah_psum"), b + 1)
                act.activation(ah[0:AH, :], ps[0:AH, 7, 0:256], ACT.Gelu_apprx_tanh,
                               bias=ld["b1"][:, 0:1]).then_inc(sem("ah_ready"), 1)

            def route2(b, _):
                act.wait_ge(sem("rl_ready"), b + 1)
                act.activation(rt[:, 1, :], rt[:, 0, :], ACT.Exp).then_inc(sem("rexp_ready"), 1)

            def silu(b, n):
                m = b * E8 * IT + n
                act.wait_ge(sem("gu_psum"), m + 1)
                if m >= 3:
                    act.wait_ge(sem("av_ready"), m - 2)
                copy(gu[m % 3], ps[0:IP, m % 2, :], "gu_ready")
                act.wait_ge(sem("gu_ready"), m + 1)
                if m >= 6:
                    act.wait_ge(sem("y3_psum"), (m - 6) // IT + 1)
                act.activation(av[:, m % 6, :], gu[m % 3][:, 0:256], ACT.Tanh, scale=0.5).then_inc(sem("tanh_ready"), 1)

            stages = {"soft": lambda b, q: soft(b, q) if b else None, "onehots": onehots, "turn_2": turn_2, "turn_3": turn_3, "turn_q": turn_q, "neg_max": neg_max,
                      "prob": prob, "out_turn": out_turn, "attend": attend, "route1": route1, "route2": route2,
                      "silu": silu}
            for name, b, k in steps():
                if name in stages:
                    stages[name](b, k)

        @block.vector
        def _(v):
            n = [0]

            def link(ins):
                ins.then_inc(sem("dve_chain"), 1)
                n[0] += 1
                v.wait_ge(sem("dve_chain"), n[0])

            def layer_norm(dst, src, k, signal):
                for t in range(k):
                    i = v.bn_stats(st[:, t, :], src[:, t, :])
                link(i)
                for t in range(k):
                    i = v.bn_aggr(mv[:, t, :], st[:, t, :])
                link(i)
                rsqrt(rs, mv[:, 0:k, 1], k)
                for t in range(k):
                    i = v.tensor_scalar(dst[:, t, :], src[:, t, :], mv[:, t, 0:1], rs[:, 1, t:t + 1],
                                        ALU.subtract, ALU.mult)
                i.then_inc(sem(signal), 1)

            def norm_tiles(tiles):
                k = len(tiles)
                for t, (x, _, _) in enumerate(tiles):
                    i = v.bn_stats(st[:, t, :], x)
                link(i)
                for t in range(k):
                    i = v.bn_aggr(mv[:, t, :], st[:, t, :])
                link(i)
                x, y, u = rs[:, 0, 0:k], rs[:, 1, 0:k], rs[:, 2, 0:k]
                link(v.tensor_scalar(x, mv[:, 0:k, 1], EPS, None, ALU.add))
                link(v.tensor_scalar(u.bitcast(I32), x.bitcast(I32), 1, None, ALU.logical_shift_right))
                v.tensor_scalar(x, x, -0.5, None, ALU.mult)
                link(v.tensor_scalar(y.bitcast(I32), u.bitcast(I32), -1.0, float(0x5f3759df), ALU.mult, ALU.add))
                for _ in range(3):
                    for t in range(k):
                        i = v.scalar_tensor_tensor(u[:, t:t + 1], y[:, t:t + 1], x[:, t:t + 1], y[:, t:t + 1],
                                                   ALU.mult, ALU.mult)
                    link(i)
                    link(v.scalar_tensor_tensor(y, u, 1.5, y, ALU.add, ALU.mult))
                for t, (src, dst, signal) in enumerate(tiles):
                    i = v.tensor_scalar(dst, src, mv[:, t, 0:1], rs[:, 1, t:t + 1], ALU.subtract, ALU.mult)
                    if t % 2:
                        i.then_inc(sem(signal), 1)

            def rsqrt(w, src, k):
                x, y, u = w[:, 0, 0:k], w[:, 1, 0:k], w[:, 2, 0:k]
                link(v.tensor_scalar(x, src, EPS, None, ALU.add))
                link(v.tensor_scalar(u.bitcast(I32), x.bitcast(I32), 1, None, ALU.logical_shift_right))
                link(v.tensor_scalar(y.bitcast(I32), u.bitcast(I32), -1.0, float(0x5f3759df), ALU.mult, ALU.add))
                for _ in range(3):
                    link(v.scalar_tensor_tensor(u, y, -0.5, y, ALU.mult, ALU.mult))
                    link(v.tensor_tensor(u, u, x, ALU.mult))
                    link(v.scalar_tensor_tensor(y, u, 1.5, y, ALU.add, ALU.mult))

            v.memset(V[:, :, :], 1.0)
            v.memset(ah[:, :], 1.0)
            v.memset(mrep[:, :, :], 0.0).then_inc(sem("consts"), 1)
            v.wait_ge(sem("consts"), 1)
            loaded(v, 1)
            layer_norm(xn, cur, NT, "xn0_ready")
            loaded(v, 2)
            link(v.tensor_copy(posf[:, :], ld["pos"][:, :]))
            A0, A1, A2 = ang[:, 0, :], ang[:, 1, :], ang[:, 2, :]
            inv = [float(x) for x in (np.float32(1.0) / np.float32(10000.0) ** (np.arange(0, DK, 2, dtype=np.float32) / np.float32(DK)))]
            for f in range(4):
                i = v.tensor_scalar(A2.rearrange("p (t f) -> p t f", f=4)[:, :, f], posf[:, :], inv[f], None, ALU.mult)
            link(i)
            for dst, turn, shift in ((A0, 0.25, TWO_PI / 4), (A1, 0.0, 0.0)):
                k = sm[:, :]
                link(v.tensor_scalar(k, A2, 1.0 / TWO_PI, turn, ALU.mult, ALU.add))
                link(v.tensor_scalar(k, k, ROUND, None, ALU.add))
                link(v.tensor_scalar(k, k, ROUND, None, ALU.subtract))
                link(v.scalar_tensor_tensor(dst, k, -C1, A2, ALU.mult, ALU.add))
                link(v.scalar_tensor_tensor(dst, k, -C2, dst, ALU.mult, ALU.add))
                link(v.scalar_tensor_tensor(dst, k, -C3, dst, ALU.mult, ALU.add))
                link(v.tensor_scalar(dst, dst, shift, None, ALU.add))
                i = v.tensor_scalar(dst, dst, 3.1415925, -3.1415925, ALU.min, ALU.max)
                if turn:
                    link(i)
            i.then_inc(sem("ang_ready"), 1)

            def rotate(src, k, c0):
                for t in range(k):
                    s = src[t].rearrange("p (h a d) -> p h a d", h=H, a=2)
                    cc = cs[:, 0, c0 + t, :].unsqueeze(1).unsqueeze(1).broadcast_to([P, H, 2, 4])
                    ss = cs[:, 1, c0 + t, :].unsqueeze(1).unsqueeze(1).broadcast_to([P, H, 2, 4])
                    v.tensor_tensor(ra[:, t, :].rearrange("p (h a d) -> p h a d", h=H, a=2), s, cc, ALU.mult)
                    link(v.tensor_tensor(rb[:, t, :].rearrange("p (h a d) -> p h a d", h=H, a=2), s, ss, ALU.mult))
                r3 = [w[:, 0:k, :].rearrange("p t (h a d) -> p (t h) a d", h=H, a=2) for w in (rq, ra, rb)]
                v.tensor_tensor(r3[0][:, :, 0, :], r3[1][:, :, 0, :], r3[2][:, :, 1, :], ALU.subtract)
                link(v.tensor_tensor(r3[0][:, :, 1, :], r3[1][:, :, 1, :], r3[2][:, :, 0, :], ALU.add))

            def parts(k, keys, signal):
                r = rq[:, 0:k, :].rearrange("p t (h d) -> p (t h) d", h=H)
                s = qs[:, 0:k * H, :, :]
                slots = [s[:, :, 0:7:3, :], s[:, :, 1:8:3, :], s[:, :, 2:6:3, :]] if keys else \
                    [s[:, :, 0:3, :], s[:, :, 3:6, :], s[:, :, 6:8, :]]
                for p, z in enumerate(slots):
                    w = z.shape[2]
                    i = v.tensor_copy(z, r.unsqueeze(2).broadcast_to([P, k * H, w, DK]))
                    if p == 2:
                        i.then_inc(sem(signal), 1)
                    else:
                        link(i)
                        link(v.tensor_tensor(r, r, z[:, :, 0, :], ALU.subtract))

            def ctx_keys(t):
                v.wait_ge(sem("v_psum"), t + 1)
                if t == 0:
                    v.wait_ge(sem("cs_ready"), 1)
                rotate([ps[:, 6, 0:128]], 1, NT + t)
                if t >= 1:
                    v.wait_ge(sem("kt_psum"), t)
                parts(1, True, "ks_ready")

            v.wait_ge(sem("q_psum"), 1)
            link(v.tensor_copy(qf[:, :, :], ps[:, 4:6, :]))
            v.wait_ge(sem("kv_ready"), 2)
            t0, t1 = tmp[:, 0:512], tmp[:, 512:1024]

            def cross(dst, x0, y0, x1, y1, op, last=None):
                v.tensor_tensor(t0, x0, y0, ALU.mult)
                link(v.tensor_tensor(t1, x1, y1, ALU.mult))
                i = v.tensor_tensor(dst, t0, t1, op)
                if last:
                    i.then_inc(sem(last), 1)
                else:
                    link(i)

            cross(spec[:, 0, :], qf[:, 0, :], kv[:, KC, :], qf[:, 1, :], kv[:, KS, :], ALU.add)
            cross(spec[:, 1, :], qf[:, 1, :], kv[:, KCN, :], qf[:, 0, :], kv[:, KS, :], ALU.subtract)
            v.tensor_reduce(cps[:, :, :].rearrange("p a c -> p (a c)"),
                            spec[:, :, :].rearrange("p a (c d) -> p (a c) d", d=DK), AX, ALU.add).then_inc(sem("cps_ready"), 1)
            ctx_keys(0)
            v.wait_ge(sem("corr_ready"), 1)
            link(v.max(sm[0:64, 0:8], corr[0:64, :]))
            v.tensor_scalar(sm[0:64, 8:9], sm[0:64, 0:1], -1.0, None, ALU.mult).then_inc(sem("corr_max"), 1)
            ctx_keys(1)
            v.wait_ge(sem("ew_ready"), 1)
            link(v.scalar_tensor_tensor(ew[0:64, :], corr[0:64, :], sm[0:64, TOP - 1:TOP], ew[0:64, :], ALU.is_ge, ALU.mult))
            link(v.tensor_reduce(sm[0:64, 9:10], ew[0:64, :], AX, ALU.add))
            link(v.reciprocal(sm[0:64, 10:11], sm[0:64, 9:10]))
            v.tensor_scalar(ew[0:64, :], ew[0:64, :], sm[0:64, 10:11], None, ALU.mult).then_inc(sem("wc_ready"), 1)
            ctx_keys(2)
            v.wait_ge(sem("wf_ready"), 1)

            def spread(k):
                return wf[:, k, :].unsqueeze(2).broadcast_to([P, B * H, DK])

            def wide(x):
                return x.rearrange("p (c d) -> p c d", d=DK)

            t0, t1 = wide(tmp[:, 0:512]), wide(tmp[:, 512:1024])
            vc, vs = wide(kv[:, VVC, :]), wide(kv[:, VVS, :])
            cross(wide(spec[:, 0, :]), vc, spread(0), vs, spread(1), ALU.subtract)
            cross(wide(spec[:, 1, :]), vc, spread(1), vs, spread(2), ALU.add, "of_ready")
            ctx_keys(3)
            v.wait_ge(sem("tg_ready"), 1)
            v.wait_ge(sem("bo_psum"), 1)
            v.scalar_tensor_tensor(cur[:, :, :], ps[:, 3, 0:128].unsqueeze(1).broadcast_to([P, NT, D]), tg[:, 0:1],
                                   cur[:, :, :], ALU.mult, ALU.add).then_inc(sem("bo_used"), 1)
            ctx_keys(4)
            v.wait_ge(sem("tg_ready"), 1)
            v.tensor_scalar(tg[:, 5:6], tg[:, 3:4], 0.5, None, ALU.mult)
            link(v.tensor_scalar(tg[:, 4:5], tg[:, 2:3], 1.0 / WSCALE, None, ALU.mult))
            v.wait_ge(sem("y0_psum"), 1)
            link(v.scalar_tensor_tensor(cur[:, :, :], ps[:, 2:4, :].rearrange("p a (t d) -> p (a t) d", t=4), tg[:, 0:1],
                                        cur[:, :, :], ALU.mult, ALU.add))

            layer_norm(xn, cur, NT, "xn1_ready")
            ctx_keys(5)
            v.wait_ge(sem("xn1_ready"), 1)
            v.wait_ge(sem("mean_psum"), 1)
            v.tensor_tensor(xc[:, :, :], xn[:, :, :], ps[:, 5, 0:128].unsqueeze(1).broadcast_to([P, NT, D]),
                            ALU.subtract).then_inc(sem("xc_ready"), 1)
            ctx_keys(6)
            loaded(v, 3)
            for k in range(4):
                v.wait_ge(sem("cw_psum"), k + 1)
                link(v.tensor_tensor(tmp[:, 512 * k:512 * k + 512], ps[:, k, :],
                                     ld["w_qT"][:, 4 * k:4 * k + 4, :].rearrange("p a c -> p (a c)"), ALU.mult))
                i = v.tensor_reduce(var[:, 3, 4 * k:4 * k + 4], tmp[:, 512 * k:512 * k + 512].rearrange("p (c d) -> p c d", d=D), AX, ALU.add)
            link(i)
            rsqrt(var, var[:, 3, :], 16)
            link(v.tensor_tensor(var[:, 1, :], var[:, 1, :], ld["gamma"][:, :], ALU.mult))
            v.tensor_tensor(keyS[:, :, :], ld["keysT"][:, :, :], var[:, 1, :].unsqueeze(2).broadcast_to([P, 16, NK]),
                            ALU.mult).then_inc(sem("keyS_ready"), 1)
            ctx_keys(7)

            def similar(t):
                v.wait_ge(sem("sim_psum"), t + 1)
                if t == 0:
                    v.wait_ge(sem("shift_ready"), 1)
                v.tensor_tensor(sim[:, t, :], ps[:, t % 4, :], bshift[:, :], ALU.add).then_inc(sem("sim_ready"), 1)

            def best(b, q):
                t = 2 * b + q
                v.wait_ge(sem("sim_ready"), t + 1)
                if t >= 2:
                    v.wait_ge(sem("hot_ready"), t - 1)
                s3 = sim[:, t, :].rearrange("p (g k) -> p g k", k=NK)
                for g in range(16):
                    i = v.max(top[:, q, g, :], s3[:, g, :])
                link(i)

            def where(b, q):
                s3 = sim[:, 2 * b + q, :].rearrange("p (g k) -> p g k", k=NK)
                for g in range(16):
                    i = v.max_index(tix[:, q, g, :], top[:, q, g, :], s3[:, g, :])
                i.then_inc(sem("tix_ready"), 1)

            def pair(b, q):
                xs, ys = top[:, q, 0:8, :], top[:, q, 8:16, :]
                v.tensor_tensor(cand[:, q, :, 0:8], ys, xs[:, :, 0:1].broadcast_to([P, PH, 8]), ALU.add)
                v.tensor_tensor(cand[:, q, :, 8:12], ys[:, :, 0:4], xs[:, :, 1:2].broadcast_to([P, PH, 4]), ALU.add)
                v.tensor_tensor(cand[:, q, :, 12:16].rearrange("p h (a b) -> p h a b", a=2),
                                ys[:, :, 0:2].unsqueeze(2).broadcast_to([P, PH, 2, 2]),
                                xs[:, :, 2:4].unsqueeze(3).broadcast_to([P, PH, 2, 2]), ALU.add)
                link(v.tensor_tensor(cand[:, q, :, 16:20], xs[:, :, 4:8], ys[:, :, 0:1].broadcast_to([P, PH, 4]), ALU.add))
                for h in range(PH):
                    i = v.max(sc[:, q, h, :], cand[:, q, h, :])
                link(i)
                for h in range(PH):
                    i = v.max_index(pk[:, q, h, :], sc[:, q, h, :], cand[:, q, h, :])
                i.then_inc(sem("pk_ready"), 1)
                v.tensor_tensor(dd[:, q, :, :], sc[:, q, :, :], sc[:, q, :, 0:1].broadcast_to([P, PH, 8]),
                                ALU.subtract).then_inc(sem("dd_ready"), 1)

            def look(q):
                v.wait_ge(sem("candi_ready"), q + 1)
                v.wait_ge(sem("pk_ready"), q + 1)
                link(v.tensor_copy(pkf[:, :], pk[:, q, :, :].rearrange("p h k -> p (h k)")))
                if q:
                    v.wait_ge(sem("hot_used"), q)
                link(v.tensor_tensor(hot[:, :, :], pkf[:, :].unsqueeze(2).broadcast_to([P, 64, CAND]),
                                     ld["io20"][:, :].unsqueeze(1).broadcast_to([P, 64, CAND]), ALU.is_equal))
                h4 = hot[:, :, :].rearrange("p (h k) c -> p h k c", h=PH)
                v.tensor_tensor(h4, h4, candi[:, q, :, :].unsqueeze(2).broadcast_to([P, PH, 8, CAND]),
                                ALU.mult).then_inc(sem("hot_ready"), 1)

            def weight(b, q):
                t = 2 * b + q
                if b == 0:
                    look(q)
                v.wait_ge(sem("hot_ready"), t + 1)
                v.tensor_reduce(eid[:, b % 2, q, :], hot[:, :, :], AX, ALU.add).then_inc(sem("hot_used"), 1)
                v.wait_ge(sem("ex_ready"), t + 1)
                if b >= 2:
                    v.wait_ge(sem("eT_psum"), b - 1)
                link(v.tensor_reduce(zz[:, q, :], ex_[:, q, :, :], AX, ALU.add))
                link(v.reciprocal(zz[:, q, :], zz[:, q, :]))
                v.tensor_tensor(wts[:, b % 2, q, :].rearrange("p (h k) -> p h k", h=PH), ex_[:, q, :, :],
                                zz[:, q, :].unsqueeze(2).broadcast_to([P, PH, 8]), ALU.mult).then_inc(sem("wts_ready"), 1)

            def number(b, _):
                v.wait_ge(sem("hot_used"), 2 * b + 2)
                e = eid[:, b % 2, :, :].rearrange("p a c -> p (a c)")
                link(v.tensor_copy(eidi[:, 0, :], e))
                v.tensor_scalar(eidi[:, 1, :], eidi[:, 0, :], P - 1, None, ALU.bitwise_and)
                link(v.tensor_scalar(eidi[:, 2, :], eidi[:, 0, :], 7, None, ALU.logical_shift_right))
                if b >= 1:
                    v.wait_ge(sem("eT_psum"), b)
                v.tensor_copy(elh[:, :, :], eidi[:, 1:3, :]).then_inc(sem("elh_ready"), 1)

            def groups(b, _):
                v.wait_ge(sem("whi_ready"), b + 1)
                v.scalar_tensor_tensor(whl[:, 1, :], ps[:, 3, 256:384], WSCALE, whl[:, 0, :],
                                       ALU.mult, ALU.subtract).then_inc(sem("wlo_ready"), 1)
                v.wait_ge(sem("iox_ready"), 1)
                v.tensor_tensor(Yq[:, :, :].rearrange("p e (c t) -> p e c t", t=TC),
                                elT[:, 1, :].rearrange("p (c t) -> p c t", t=TC).unsqueeze(1).broadcast_to([P, EH, NC, TC]),
                                iox[:, 0:EH, :].unsqueeze(2).broadcast_to([P, EH, NC, TC]), ALU.is_equal)
                link(v.tensor_tensor(elS[:, :, :], elT[:, 0, :].unsqueeze(1).broadcast_to([P, EH, P]),
                                     ld["io16"][:, :].unsqueeze(2).broadcast_to([P, EH, P]), ALU.subtract))
                v.wait_ge(sem("wlo_ready"), b + 1)
                if b >= 1:
                    v.wait_ge(sem("W_psum"), NC * b)
                for k in range(2):
                    v.tensor_tensor(Y[:, :, k, :], Yq[:, :, :], whl[:, k, :].unsqueeze(1).broadcast_to([P, EH, P]), ALU.mult)

            def place(b, c):
                m = b * NC + c
                if m >= 2:
                    v.wait_ge(sem("W_psum"), m - 1)
                v.tensor_tensor(X[:, c % 2, :, :].rearrange("p (c e) t -> p c e t", c=EH),
                                elS[:, :, c * TC:c * TC + TC].unsqueeze(2).broadcast_to([P, EH, 16, TC]),
                                iox[:, :, :].unsqueeze(1).broadcast_to([P, EH, 16, TC]), ALU.is_equal)\
                    .then_inc(sem("X_ready"), 1)

            def weigh(b, c):
                m = b * NC + c
                v.wait_ge(sem("W_psum"), m + 1)
                if m == 0:
                    v.wait_ge(sem("G_ready"), 2 * EH)
                else:
                    v.wait_ge(sem("HD_ready"), m)
                v.tensor_reduce(W[:, :, :].rearrange("p s c -> p (s c)"),
                                ps[:, 3, :].rearrange("p (c a) -> p c a", a=2), AX, ALU.add).then_inc(sem("W_taken"), 1)
                v.wait_ge(sem("W_taken"), m + 1)
                v.tensor_tensor(
                    HD.rearrange("p e (s t) -> p s t e", s=2)[:, :, c * TC:c * TC + TC, :],
                    W[:, :, :].rearrange("p s (t e) -> p s t e", e=EH),
                    G[:, :, b * L:b * L + L].rearrange("p e (s t) -> p s t e", s=2)[:, :, c * TC:c * TC + TC, :],
                    ALU.mult).then_inc(sem("HD_ready"), 1)

            def norms(b, _):
                work = []
                if b < B:
                    v.wait_ge(sem("y1_psum"), b + 1)
                    if b >= 1:
                        v.wait_ge(sem("xn2T_psum"), b)
                    work.append((ps[:, 3, 0:256], tg[:, 4:5], cur[:, 2 * b:2 * b + 2, :], xn2, "xn2_ready"))
                if b >= 1:
                    v.wait_ge(sem("y2_psum"), b)
                    work.append((ps[:, 7, 0:256], tg[:, 1:2], cur[:, 2 * b - 2:2 * b, :], xn3, "xn3_ready"))
                for y, w, x, _, _ in work:
                    i = v.scalar_tensor_tensor(x, y.rearrange("p (t d) -> p t d", t=2), w, x, ALU.mult, ALU.add)
                link(i)
                tiles = [(x[:, t, :], dst[:, t, :], signal) for _, _, x, dst, signal in work for t in range(2)]
                norm_tiles(tiles)

            def rope(b, _):
                v.wait_ge(sem("q1_psum"), b + 1)
                rotate([ps[:, 4, 256:384], ps[:, 4, 384:512]], 2, 2 * b)

            def split(b, _):
                parts(2, False, "qs_ready")

            def max_(b, g):
                v.wait_ge(sem("s1_psum"), b * 8 + g + 1)
                qt, gg = g // 4, g % 4
                bk = 4 + 2 * (g % 2)
                v.tensor_reduce(mx[:, qt, 4 * gg:4 * gg + 4],
                                ps[:, bk:bk + 2, :].rearrange("p e (j k) -> p (e j) k", j=2), AX, ALU.max)\
                    .then_inc(sem("mx_ready"), 1)

            def neg_max(b, _):
                v.wait_ge(sem("mx_ready"), b * 8 + 8)
                v.tensor_scalar(mrep[:, :, 0:H], mx[:, :, :], -1.0, None, ALU.mult)
                v.tensor_scalar(mrep[:, :, 64:64 + H], mx[:, :, :], -1.0, None, ALU.mult).then_inc(sem("mrep_ready"), 1)

            def attend(b, _):
                v.wait_ge(sem("o_psum"), b + 1)
                o = ps[:, 4:6, :].rearrange("p t (c d) -> p (t c) d", d=32)
                link(v.reciprocal(rcp[:, :], o[:, :, 8]))
                v.tensor_tensor(att[:, :, :].rearrange("p t (h d) -> p (t h) d", h=H), o[:, :, 0:8],
                                rcp[:, :].unsqueeze(2).broadcast_to([P, 2 * H, DK]), ALU.mult).then_inc(sem("att_ready"), 1)

            R = [rt[:, k, :].rearrange("p (t e) -> p t e", t=2) for k in range(8)]

            def route2(b, _):
                c1, c2, c3 = sm[:, 0:2], sm[:, 2:4], sm[:, 4:6]
                v.wait_ge(sem("al_psum"), b + 1)
                lg = ps[:, 6, 256:272].rearrange("p (t e) -> p t e", t=2)
                link(v.tensor_reduce(c1, lg, AX, ALU.max))
                link(v.tensor_tensor(R[0], lg, c1.unsqueeze(2).broadcast_to([P, 2, 8]), ALU.subtract))
                link(v.tensor_scalar(R[2][:, :, 0:MK], ps[:, 6, 272:284].rearrange("p (t e) -> p t e", t=2), -30.0, 30.0,
                                     ALU.max, ALU.min))
                v.tensor_reduce(c2, R[2][:, :, 0:MK], AX, ALU.max).then_inc(sem("rl_ready"), 1)
                v.wait_ge(sem("rl_ready"), b + 1)
                link(v.tensor_tensor(R[3][:, :, 0:MK], R[2][:, :, 0:MK], c2.unsqueeze(2).broadcast_to([P, 2, MK]), ALU.is_ge))
                link(v.tensor_tensor(R[3][:, :, 0:MK], R[3][:, :, 0:MK], ld["io9"][:, :].unsqueeze(1).broadcast_to([P, 2, MK]), ALU.mult))
                link(v.tensor_reduce(c3, R[3][:, :, 0:MK], AX, ALU.min))
                link(v.tensor_scalar(c3, c3, 10.0, None, ALU.add))
                v.wait_ge(sem("rexp_ready"), b + 1)
                link(v.tensor_reduce(c1, R[1], AX, ALU.add))
                link(v.reciprocal(c1, c1))
                link(v.tensor_tensor(R[4], R[1], c1.unsqueeze(2).broadcast_to([P, 2, 8]), ALU.mult))
                other = R[4].unsqueeze(2).broadcast_to([P, 2, 8, 8])
                own = R[4].unsqueeze(3).broadcast_to([P, 2, 8, 8])
                v.tensor_tensor(cmp[:, 0, :, :, :], other, own, ALU.is_gt)
                link(v.tensor_tensor(cmp[:, 1, :, :, :], other, own, ALU.is_equal))
                link(v.tensor_tensor(cmp[:, 1, :, :, :], cmp[:, 1, :, :, :], ld["tri"][:, :, :].unsqueeze(1).broadcast_to([P, 2, 8, 8]), ALU.mult))
                link(v.tensor_tensor(cmp[:, 0, :, :, :], cmp[:, 0, :, :, :], cmp[:, 1, :, :, :], ALU.add))
                link(v.tensor_reduce(rt[:, 5, :], cmp[:, 0, :, :, :].rearrange("p t e f -> p (t e) f"), AX, ALU.add))
                link(v.tensor_tensor(R[5], R[5], c3.unsqueeze(2).broadcast_to([P, 2, 8]), ALU.is_lt))
                link(v.tensor_tensor(score[:, b % 2, :].rearrange("p (t e) -> p t e", t=2), R[5], R[4], ALU.mult))

            def gather(b, e):
                v.wait_ge(sem("y3_psum"), b * E8 + e + 1)
                for t in range(2):
                    y = ps[:, 2, t * D:t * D + D]
                    w = score[:, b % 2, t * E8 + e:t * E8 + e + 1]
                    if e == 0:
                        i = v.tensor_scalar(macc[:, t, :], y, w, None, ALU.mult)
                    else:
                        i = v.scalar_tensor_tensor(macc[:, t, :], y, w, macc[:, t, :], ALU.mult, ALU.add)
                i.then_inc(sem("y3_used"), 1)
                v.wait_ge(sem("y3_used"), b * E8 + e + 1)

            def silu(b, n):
                m = b * E8 * IT + n
                v.wait_ge(sem("tanh_ready"), m + 1)
                v.scalar_tensor_tensor(av[:, m % 6, :], av[:, m % 6, :], 1.0, gu[m % 3][:, 0:256], ALU.add,
                                       ALU.mult).then_inc(sem("gate_ready"), 1)

            def moe_out(b, _):
                x4 = cur[:, 2 * b:2 * b + 2, :]
                v.scalar_tensor_tensor(x4, macc[:, :, :], tg[:, 5:6], x4, ALU.mult, ALU.add).then_inc(sem("x4_ready"), 1)

            similar(0)
            similar(1)
            best(0, 0)
            where(0, 0)
            pair(0, 0)
            best(0, 1)
            where(0, 1)
            pair(0, 1)
            for t in range(2, NT):
                similar(t)
            stages = {"best": best, "where": where, "pair": pair, "weight": weight, "number": number,
                      "groups": groups, "place": place, "weigh": weigh, "norms": norms, "rope": rope, "split": split,
                      "max": max_, "neg_max": neg_max, "attend": attend, "route2": route2,
                      "times": silu, "gather": gather, "moe_out": moe_out}
            for name, b, k in steps():
                if name in stages:
                    stages[name](b, k)

        @block.tensor
        def _(pe):
            def mm(o, l, r, start=True, stop=True):
                return pe.matmul(o, l, r, start=start, stop=stop)

            def bias(o, row, w):
                return mm(o, ones[0:1, 0:P], ld["rows"][0:1, row:row + w], False, True)

            BQ, BKV, BO0, BQ1, BKV1, BO1 = 0, 128, 384, 512, 640, 896
            loaded(pe, 0)
            ctxs, dft, idft = ld["ctx"], ld["dft"], ld["idft"]
            for b in range(B):
                for k in range(2):
                    i = mm(ps[:, b, :], ctxs[:, 2 * b + k, :], dft[:, k, :, :].rearrange("p a c -> p (a c)"), k == 0, k == 1)
                i.then_inc(sem("cf_psum"), 1)
            loaded(pe, 1)
            pe.wait_ge(sem("xn0_ready"), 1)
            for b in range(B):
                o = ps[:, 4 + b // 2, (b % 2) * 256:(b % 2) * 256 + 256]
                for k in range(2):
                    i = mm(o, xn[:, 2 * b + k, :], dft[:, k, 0:2, :].rearrange("p a c -> p (a c)"), k == 0, k == 1)
            i.then_inc(sem("xnf_psum"), 1)
            pe.wait_ge(sem("cf_ready"), B)
            for s, (bk, var_, w) in enumerate(((0, VC, 0), (1, VS, 0), (2, VCN, 0), (3, VC, 128), (6, VSN, 128))):
                for b in range(B):
                    o = ps[:, bk, b * P:b * P + P]
                    i = mm(o, cf[:, b, var_ * P:var_ * P + P], ld["wkv0T"][:, w:w + 128], True, var_ != VC)
                    if var_ == VC:
                        i = mm(o, ld["lrow"][0:1, 0:P], ld["rows"][0:1, BKV + w:BKV + w + 128], False, True)
            i.then_inc(sem("kv_psum"), 1)
            pe.wait_ge(sem("xnf_ready"), 1)
            for k in range(2):
                for b in range(B):
                    o = ps[:, 4 + k, b * P:b * P + P]
                    i = mm(o, xnf[:, b // 2, (b % 2) * 256 + k * P:(b % 2) * 256 + k * P + P], ld["wq0T"][:, :], True, k == 1)
                    if k == 0:
                        i = mm(o, ld["lrow"][0:1, 0:P], ld["rows"][0:1, BQ:BQ + 128], False, True)
            i.then_inc(sem("q_psum"), 1)
            for k in range(2):
                if k:
                    pe.wait_ge(sem("kv_ready"), 1)
                for t in range(4):
                    i = pe.transpose(ps[:, 7 * (1 - k), t * P:t * P + P], ctxs[:, 4 * k + t, :], ident[:, :])
                i.then_inc(sem("ctxT_psum"), 1)
            loaded(pe, 2)
            pe.wait_ge(sem("ctxT_ready"), 2)
            pe.wait_ge(sem("kv_ready"), 2)
            pe.wait_ge(sem("identb_ready"), 1)

            def ctx_kv(t):
                if t >= 1:
                    pe.wait_ge(sem("v_ready"), t)
                mm(ps[:, 6, 0:256], ctxT[:, t * P:t * P + P], ld["Wkv1"][:, :], True, False)
                bias(ps[:, 6, 0:256], BKV1, 256).then_inc(sem("v_psum"), 1)

            def ctx_turn(t):
                pe.wait_ge(sem("ks_ready"), t + 1)
                if t >= 1:
                    pe.wait_ge(sem("kt_ready"), t)
                for j in range(8):
                    i = pe.transpose(bank16(7)[:, j * P:j * P + P],
                                     qs[:, 2 * j:2 * j + 2, :, :].rearrange("p h s d -> p (h s d)"), identb[:, :])
                i.then_inc(sem("kt_psum"), 1)

            ctx_kv(0)
            pe.wait_ge(sem("cps_ready"), 1)
            for k in range(2):
                i = mm(ps[0:64, 0, 0:L], cps[:, k, :], idft[:, k, :], k == 0, k == 1)
            i.then_inc(sem("corr_psum"), 1)
            ctx_turn(0)
            ctx_kv(1)
            ctx_turn(1)
            ctx_kv(2)
            pe.wait_ge(sem("wc_ready"), 1)
            for k in range(2):
                i = pe.transpose(ps[:, 1, k * 64:k * 64 + 64], ew[0:64, k * P:k * P + P], ident[0:64, 0:64])
            i.then_inc(sem("wcT_psum"), 1)
            pe.wait_ge(sem("wcT_ready"), 1)
            for s, var_ in enumerate((VC, VS, VCN)):
                for k in range(2):
                    i = mm(ps[:, 2, s * 64:s * 64 + 64], dft[:, k, var_, :], wcT[:, k, :], k == 0, k == 1)
            i.then_inc(sem("wf_psum"), 1)
            mm(ps[:, 3, 0:128], ones[0:1, 0:P], ld["rows"][0:1, BO0:BO0 + 128]).then_inc(sem("bo_psum"), 1)
            ctx_turn(2)
            ctx_kv(3)
            pe.wait_ge(sem("of_ready"), 1)
            for b in range(B):
                o = ps[:, 4 + b // 2, (b % 2) * 256:(b % 2) * 256 + 256]
                for k in range(2):
                    i = mm(o, spec[:, k, b * P:b * P + P], idft[:, k, :], k == 0, k == 1)
                if b == 1:
                    ctx_turn(3)
                    ctx_kv(4)
            i.then_inc(sem("ao_psum"), 1)
            pe.wait_ge(sem("ao_ready"), 1)
            pe.wait_ge(sem("wf_ready"), 1)
            pe.wait_ge(sem("bo_used"), 1)
            for t in range(NT):
                o = ps[:, 2 + t // 4, (t % 4) * P:(t % 4) * P + P]
                i = mm(o, aoT[:, t * P:t * P + P], ld["wo0T"][:, :])
            i.then_inc(sem("y0_psum"), 1)
            ctx_turn(4)
            ctx_kv(5)

            pe.wait_ge(sem("xn1_ready"), 1)
            for t in range(NT):
                i = mm(ps[:, 5, 0:128], ld["ones"][:, P:2 * P], xn[:, t, :], t == 0, t == NT - 1)
            i.then_inc(sem("mean_psum"), 1)
            for t in range(NT):
                i = pe.transpose(ps[:, t // 4, (t % 4) * P:(t % 4) * P + P], xn[:, t, :], ident[:, :])
            i.then_inc(sem("xn1T_psum"), 1)
            ctx_turn(5)
            ctx_kv(6)
            pe.wait_ge(sem("xc_ready"), 1)
            for t in range(NT):
                i = mm(ps[:, 5, 128:256], xc[:, t, :], xc[:, t, :], t == 0, t == NT - 1)
            i.then_inc(sem("cov_psum"), 1)
            for t in range(NT):
                i = pe.transpose(ps[:, 2 + t // 4, (t % 4) * P:(t % 4) * P + P], xc[:, t, :], ident[:, :])
            i.then_inc(sem("xcT_psum"), 1)
            ctx_turn(6)
            ctx_kv(7)
            loaded(pe, 3)
            pe.wait_ge(sem("cov_ready"), 1)
            pe.wait_ge(sem("xcT_ready"), 1)
            w_q, w_qT, keysT = ld["w_q"], ld["w_qT"], ld["keysT"]
            for c in range(16):
                i = mm(ps[:, c // 4, (c % 4) * P:(c % 4) * P + P], w_q[:, c * P:c * P + P], cov[:, :])
                if c % 4 == 3:
                    i.then_inc(sem("cw_psum"), 1)
            for c in range(16):
                i = mm(ps[:, 5, c * NK:c * NK + NK], ld["beta"][:, c:c + 1].broadcast_to([P, P]), keysT[:, c, :])
            i.then_inc(sem("shift_psum"), 1)

            def down_all(n):
                if n == 0:
                    pe.wait_ge(sem("kt_ready"), NT)
                elif 2 <= n < EH:
                    pe.wait_ge(sem("G_ready"), n - 1)
                elif n >= EH:
                    pe.wait_ge(sem("G_ready"), n - 3)
                mm(ps[:, G_BANK[n], :], ld["downT"][:, (n // 2) * P:(n // 2) * P + P],
                   xnT[:, (n % 2) * 512:(n % 2) * 512 + 512]).then_inc(sem("G_psum"), 1)

            def similar(t):
                if t >= 4:
                    pe.wait_ge(sem("sim_ready"), t - 3)
                mm(ps[:, t % 4, :], xcT[:, t * P:t * P + P], M[:, :]).then_inc(sem("sim_psum"), 1)

            pe.wait_ge(sem("keyS_ready"), 1)
            for c in range(16):
                i = mm(ps[NK * (c % 4):NK * (c % 4) + NK, 4, (c // 4) * P:(c // 4) * P + P], keyS[:, c, :], w_qT[:, c, :])
            i.then_inc(sem("MT_psum"), 1)
            pe.wait_ge(sem("MT_ready"), 1)
            for c in range(4):
                i = pe.transpose(ps[:, 4, c * P:c * P + P], tmp[:, c * P:c * P + P], ident[:, :])
            i.then_inc(sem("M_psum"), 1)
            ctx_turn(7)
            pe.wait_ge(sem("M_ready"), 1)
            for t in range(4):
                similar(t)
            for n in range(EH):
                down_all(n)
            for t in range(4, NT):
                similar(t)
            for n in range(EH, 2 * EH):
                down_all(n)

            loaded(pe, 4)

            def onehots(b, _):
                pe.wait_ge(sem("elh_ready"), b + 1)
                pe.wait_ge(sem("wts_ready"), 2 * b + 2)
                if b == 0:
                    pe.wait_ge(sem("sim_ready"), NT)
                else:
                    pe.wait_ge(sem("xn2_ready"), b)
                pe.transpose(ps[:, 3, 0:128], elh[:, 0, :], ident[:, :])
                pe.transpose(ps[:, 3, 128:256], elh[:, 1, :], ident[:, :])
                pe.transpose(ps[:, 3, 256:384], wts[:, b % 2, :, :].rearrange("p a c -> p (a c)"),
                             ident[:, :]).then_inc(sem("eT_psum"), 1)

            def token(b, c):
                m = b * NC + c
                pe.wait_ge(sem("X_ready"), m + 1)
                if c == 0:
                    pe.wait_ge(sem("wlo_ready"), b + 1)
                else:
                    pe.wait_ge(sem("W_taken"), m)
                for half in range(2):
                    if half:
                        pe.wait_ge(sem("half_done"), m + 1)
                    for t in range(TC):
                        r = slice(64 * half, 64 * half + 64)
                        o = (half * TC + t) * 2 * EH
                        i = mm(ps[:, 3, o:o + 2 * EH], X[r, c % 2, :, t], Y[r, :, :, c * TC + t])
                    i.then_inc(sem("W_psum" if half else "half_done"), 1)

            def mix(b, _):
                pe.wait_ge(sem("HD_ready"), NC * b + NC)
                for t in range(2):
                    for e in range(EH):
                        i = mm(ps[:, 3, t * D:t * D + D], HD[:, e, t * P:t * P + P], ld["upl"][:, e, :], e == 0, e == EH - 1)
                i.then_inc(sem("y1_psum"), 1)

            def turn_2(b, _):
                pe.wait_ge(sem("xn2_ready"), b + 1)
                if b == 0:
                    pe.wait_ge(sem("kt_ready"), NT)
                    pe.wait_ge(sem("v_ready"), NT)
                else:
                    pe.wait_ge(sem("att_ready"), b)
                for t in range(2):
                    i = pe.transpose(ps[:, 4, t * P:t * P + P], xn2[:, t, :], ident[:, :])
                i.then_inc(sem("xn2T_psum"), 1)

            def query(b, _):
                pe.wait_ge(sem("xn2T_ready"), b + 1)
                for t in range(2):
                    o = ps[:, 4, 256 + t * P:256 + t * P + P]
                    mm(o, xn2T[:, t * P:t * P + P], ld["Wq1"][:, :], True, False)
                    i = bias(o, BQ1, 128)
                i.then_inc(sem("q1_psum"), 1)

            def turn_q(b, _):
                pe.wait_ge(sem("qs_ready"), b + 1)
                if b >= 1:
                    pe.wait_ge(sem("rl_ready"), b)
                for j in range(8):
                    for t in range(2):
                        i = pe.transpose(bank16(6, 2)[:, (2 * j + t) * P:(2 * j + t) * P + P],
                                         qs[:, 16 * t + 2 * j:16 * t + 2 * j + 2, :, :].rearrange("p h s d -> p (h s d)"),
                                         identb[:, :])
                i.then_inc(sem("qT_psum"), 1)

            def by_query(b, g):
                if g < 2:
                    pe.wait_ge(sem("QT_ready"), 2 * b + g + 1)
                qt, gg = g // 4, g % 4
                bk = 4 + 2 * (g % 2)
                if g >= 2:
                    pe.wait_ge(sem("mx_ready"), b * 8 + g - 1)
                for jj in range(2):
                    for e in range(2):
                        r = slice(64 * e, 64 * e + 64)
                        i = mm(ps[:, bk + e, jj * 256:jj * 256 + 256], QT[r, 2 * gg + jj, qt * P:qt * P + P],
                               KT[r, 2 * gg + jj, b * L:b * L + L])
                i.then_inc(sem("s1_psum"), 1)

            def neg_max(b, _):
                pe.wait_ge(sem("mrep_ready"), b + 1)
                for t in range(2):
                    i = pe.transpose(bank16(4)[:, t * P:t * P + P], mrep[:, t, :], identb[:, :])
                i.then_inc(sem("mT_psum"), 1)

            def score_(b, h):
                n = b * H + h
                if h == 0:
                    pe.wait_ge(sem("mT_ready"), b + 1)
                if h >= 2:
                    pe.wait_ge(sem("p_ready"), n - 1)
                j, e = h // 2, h % 2
                r = slice(64 * e, 64 * e + 64)
                c = 64 * e + (j // 2) * 4 + e * 2 + j % 2
                for k in range(2):
                    o = ps[:, 4 + (h + 1) % 2, k * 256:k * 256 + 256]
                    mm(o, KT[r, j, b * L + k * P:b * L + k * P + P], QT[r, j, :], True, False)
                    i = mm(o, identb[r, c:c + 1].broadcast_to([64, P]), mT[r, :], False, True)
                i.then_inc(sem("s2_psum"), 1)

            def value(b, h):
                pe.wait_ge(sem("p_ready"), b * H + h + 1)
                r = 32 * (h % 4)
                for k in range(2):
                    i = mm(ps[r:r + 32, 6 + h // 8, (h // 4 % 2) * 256:(h // 4 % 2) * 256 + 256],
                           V[:, 2 * b + k, 9 * h:9 * h + 32], PE_[:, h % 2, k, :], k == 0, k == 1)
                i.then_inc(sem("av_done"), 1)

            def out_turn(b, _):
                pe.wait_ge(sem("oT_ready"), b + 1)
                for t in range(2):
                    for g in range(4):
                        i = pe.transpose(ps[:, 4 + t, g * P:g * P + P], oT[:, g, t * P:t * P + P], ident[:, :])
                i.then_inc(sem("o_psum"), 1)

            def attend(b, _):
                pe.wait_ge(sem("att_ready"), b + 1)
                for t in range(2):
                    i = pe.transpose(ps[:, 6, t * P:t * P + P], att[:, t, :], ident[:, :])
                i.then_inc(sem("attT_psum"), 1)

            def project(b, _):
                pe.wait_ge(sem("attT_ready"), b + 1)
                for t in range(2):
                    o = ps[:, 7, t * P:t * P + P]
                    mm(o, attT[:, t * P:t * P + P], ld["Wo1"][:, :], True, False)
                    i = bias(o, BO1, 128)
                i.then_inc(sem("y2_psum"), 1)

            def turn_3(b, _):
                pe.wait_ge(sem("xn3_ready"), b + 1)
                for t in range(2):
                    i = pe.transpose(ps[:, 6, t * P:t * P + P], xn3[:, t, :], ident[:, :])
                i.then_inc(sem("xn3T_psum"), 1)

            def route1(b, _):
                if b == 0:
                    loaded(pe, 5)
                pe.wait_ge(sem("xn3T_ready"), b + 1)
                for t in range(2):
                    mm(ps[:, 6, 256 + t * 8:256 + t * 8 + 8], xn3T[b % 2][:, t * P:t * P + P], ld["rw"][:, :])
                mm(ps[0:AH, 7, 0:256], ld["w1T"][:, :], xn3T[b % 2]).then_inc(sem("ah_psum"), 1)

            def route2(b, _):
                pe.wait_ge(sem("ah_ready"), b + 1)
                for t in range(2):
                    i = mm(ps[:, 6, 272 + t * MK:272 + t * MK + MK], ah[0:AH + 1, t * P:t * P + P], ld["w2T"][:, :])
                i.then_inc(sem("al_psum"), 1)

            def gate(b, n):
                m = b * E8 * IT + n
                if m >= 2:
                    pe.wait_ge(sem("gu_ready"), m - 1)
                e, k = n // IT, n % IT
                for s in range(2):
                    i = mm(ps[0:IP, m % 2, s * 256:s * 256 + 256], ld["guT"][:, e, s, k * IP:k * IP + IP], xn3T[b % 2])
                i.then_inc(sem("gu_psum"), 1)

            def down(b, e):
                m = b * E8 + e
                pe.wait_ge(sem("av_ready"), (m + 1) * IT)
                if m >= 1:
                    pe.wait_ge(sem("y3_used"), m)
                for t in range(2):
                    for k in range(IT):
                        i = mm(ps[:, 2, t * D:t * D + D], av[:, (m * IT + k) % 6, t * P:t * P + P],
                               ld["dn"][:, e * IT + k, :], k == 0, k == IT - 1)
                i.then_inc(sem("y3_psum"), 1)

            stages = {"onehots": onehots, "token": token, "mix": mix, "turn_2": turn_2, "query": query, "turn_q": turn_q,
                      "by_query": by_query, "neg_max": neg_max, "score": score_, "value": value, "out_turn": out_turn,
                      "attend": attend, "project": project, "turn_3": turn_3, "route1": route1, "route2": route2, "gate": gate, "down": down}
            for name, b, k in steps():
                if name in stages:
                    stages[name](b, k)


def constants():
    t, f = np.arange(L)[:, None].astype(np.float64), np.arange(P)[None, :].astype(np.float64)
    w = 2 * np.pi / L
    nyq = np.where(np.arange(L) % 2 == 0, 1.0, -1.0)
    c, s = np.cos(w * ((t * f) % L)), np.sin(w * ((t * f) % L))
    sn, cn = s.copy(), c.copy()
    sn[:, 0], cn[:, 0] = nyq, nyq
    dft = np.stack([c, sn, s, cn], 1)
    ic, is_ = 2 * c.T / L, 2 * s.T / L
    ic[0], is_[0] = 1.0 / L, nyq / L
    ones = np.ones((P, 2 * P))
    ones[:, P:] = 1.0 / (NT * P)
    lrow = np.zeros((1, P))
    lrow[0, 0] = L
    tri = np.tile((np.arange(8)[None, :] < np.arange(8)[:, None])[None], (P, 1, 1))
    r = {
        "dft": dft.reshape(2, P, 4, P).transpose(1, 0, 2, 3), "idft": np.stack([ic, is_], 1),
        "ident": np.eye(P), "ones": ones, "lrow": lrow, "tri": tri,
        "io16": np.tile(16 * np.arange(EH)[None], (P, 1)),
        "io20": np.tile(np.arange(CAND)[None], (P, 1)), "io9": np.tile(np.arange(MK)[None] - 9, (P, 1)),
    }
    return {k: np.ascontiguousarray(v, dtype=np.float32) for k, v in r.items()}


def kernel(**inputs):
    import concourse.bacc as bacc
    from concourse.bass_utils import run_bass_kernel_spmd

    i = {k: np.asarray(v) for k, v in inputs.items()}

    def tiles(x):
        return x.reshape(NT, P, D).transpose(1, 0, 2)

    lay = {
        "x": tiles(i["x"]), "ctx": tiles(i["ctx_1024"]),
        "pos": np.concatenate([i["itok_BxS_0_4095"].reshape(NT, P).T, i["itok_BxS2_1_4095"].reshape(NT, P).T], 1),
        "gates": np.concatenate([i["g_xattn"], i["g_ffn"]])[None],
        "wq0T": i["L0_xattn_Wq"].T, "wkv0T": np.concatenate([i["L0_xattn_Wk"].T, i["L0_xattn_Wv"].T], 1),
        "wo0T": i["L0_xattn_Wo"].T,
        "rows": np.concatenate([i["L0_xattn_bq"], i["L0_xattn_bk"], i["L0_xattn_bv"], i["L0_xattn_bo"],
                                i["L1_xattn_b_q"], i["L1_xattn_b_kv"], i["L1_xattn_b_o"]])[None],
        "w_q": i["L0_ffn_w_q"], "w_qT": i["L0_ffn_w_q"].reshape(D, 16, P).transpose(2, 1, 0),
        "keysT": i["L0_ffn_keys"].transpose(3, 2, 0, 1).reshape(P, 16, NK),
        "gamma": i["L0_ffn_bn_gamma"].reshape(16, P).T, "beta": i["L0_ffn_bn_beta"].reshape(16, P).T,
        "downT": i["L0_ffn_down_embed"].T, "upl": i["L0_ffn_up_embed"].reshape(EH, P, D).transpose(1, 0, 2),
        "Wq1": i["L1_xattn_W_q"], "Wkv1": i["L1_xattn_W_kv"], "Wo1": i["L1_xattn_W_o"],
        "rw": i["L1_ffn_router_w"].T, "w1T": i["L1_ffn_actor_w1"].T, "b1": i["L1_ffn_actor_b1"][:, None],
        "w2T": np.concatenate([i["L1_ffn_actor_w2"].T, i["L1_ffn_actor_b2"][None]], 0),
        "guT": np.stack([i["L1_ffn_gate_w"], i["L1_ffn_up_w"]], 1).transpose(3, 0, 1, 2),
        "dn": i["L1_ffn_down_w"].reshape(E8, D, IT, IP).transpose(3, 0, 2, 1).reshape(IP, E8 * IT, D),
    }
    lay.update(constants())
    nc = bacc.Bacc("TRN2", target_bir_lowering=False, num_devices=1)
    arrays, aps = {}, {}
    for name, x in lay.items():
        x = np.ascontiguousarray(x)
        arrays["in_" + name] = x
        aps[name] = nc.dram_tensor("in_" + name, x.shape, mybir.dt.from_np(x.dtype), kind="ExternalInput").ap()
    out = nc.dram_tensor("out_0", (B, L, D), F32, kind="ExternalOutput").ap()
    program(nc, aps, out)
    r = run_bass_kernel_spmd(nc, [arrays], core_ids=[0])
    return r.results[0]["out_0"]
```
